# Optimizing a Trainium2 kernel written in Bass

```python
import numpy as np
import jax
import jax.numpy as jnp

def _softmax(x, axis=-1):
    return jax.nn.softmax(x, axis=axis)

def _gelu(x):
    return jax.nn.gelu(x, approximate=True)

def _silu(x):
    return jax.nn.silu(x)

def _sigmoid(x):
    return jax.nn.sigmoid(x)

def _layernorm(x, axis=-1, eps=1e-05):
    m = jnp.mean(x, axis=axis, keepdims=True)
    v = jnp.var(x, axis=axis, keepdims=True)
    return (x - m) / jnp.sqrt(v + eps)

def _scatter_add(tgt, idx, src, axis=0):
    return tgt.at[idx].add(src)

def _segment_sum(src, seg, n):
    return jax.ops.segment_sum(src, seg, n)
kernel_name = 'mk_decoder_preln_d1_seqx_r8_58c05f'

def setup_inputs(seed: int=0):
    np.random.seed(seed)
    _w = jnp.asarray

    def _rec_inputs():
        import jax
        import jax.numpy as jnp
        _rk = jax.random.key(seed)
        x = -0.0003929 + 0.9999 * jax.random.normal(jax.random.fold_in(_rk, 1), (8, 128, 512), jnp.float32)
        _lenS = 128 - jax.random.randint(jax.random.fold_in(_rk, 7), (8,), 0, max(1, 128 // 4) + 1, jnp.int32)
        _lenS2 = 128 - jax.random.randint(jax.random.fold_in(_rk, 8), (8,), 0, max(1, 128 // 4) + 1, jnp.int32)
        _ctx_4096P = jax.random.normal(jax.random.fold_in(_rk, 11), (8, 16, 512), jnp.float32)
        _ctx_4096c = jax.random.dirichlet(jax.random.fold_in(_rk, 511), 0.3 * jnp.ones((16,), jnp.float32), (8, 128))
        _ctx_4096t = jnp.einsum('bsk,bkd->bsd', _ctx_4096c, _ctx_4096P)
        _ctx_4096t = _ctx_4096t * jax.lax.rsqrt(jnp.mean(jnp.square(_ctx_4096t)) + 1e-12) * 0.953939
        ctx_4096 = 2.81802e-05 + 1.00001 * (_ctx_4096t + 0.3 * jax.random.normal(jax.random.fold_in(_rk, 611), (8, 128, 512), jnp.float32))
        pos_BxS2 = jnp.broadcast_to(jnp.arange(128, dtype=jnp.int32), (8, 128))
        _validS = jnp.arange(128)[None, :] < _lenS[:, None]
        _validS2 = jnp.arange(128)[None, :] < _lenS2[:, None]
        _causal = jnp.tril(jnp.ones((128, 128), dtype=bool))
        mask_BxSxS2_ik0 = jnp.where(jnp.broadcast_to(_validS2[:, None, :], (8, 128, 128)), 0, 1).astype(jnp.int32)
        return (x, ctx_4096, pos_BxS2, mask_BxSxS2_ik0)
    x, ctx_4096, pos_BxS2, mask_BxSxS2_ik0 = _rec_inputs()

    def _L0_attn_setup():
        import jax, jax.numpy as jnp
        import numpy as np
        HIDDEN = 512
        NUM_HEADS = 32
        HEAD_DIM = HIDDEN // NUM_HEADS
        B, S = (2, 128)

        def _alibi_slopes(n):
            start = 2.0 ** (-2.0 ** (-(np.log2(n) - 3)))
            return np.array([start ** (i + 1) for i in range(n)], dtype=np.float32)
        key = jax.random.key(seed)
        k1, k2, k3, k4 = jax.random.split(key, 4)
        hidden_states = jax.random.normal(k1, (B, S, HIDDEN), jnp.float32)
        Wq = jax.random.normal(k2, (HIDDEN, HIDDEN), jnp.float32) * 0.02
        Wkv = jax.random.normal(k3, (HIDDEN, 2 * HEAD_DIM), jnp.float32) * 0.02
        Wo = jax.random.normal(k4, (HIDDEN, HIDDEN), jnp.float32) * 0.02
        return {'hidden_states': hidden_states, 'Wq': Wq, 'Wkv': Wkv, 'Wo': Wo}
    _L0_attn_all = _L0_attn_setup()
    _L0_attn_in = {k: v for k, v in _L0_attn_all.items() if k in ('Wq', 'Wkv', 'Wo')}
    del _L0_attn_all

    def _L0_xattn_setup():
        import jax, jax.numpy as jnp
        import numpy as np
        B, S, E = (2, 256, 512)
        H, KVH, D = (32, 8, 128)
        GROUPS = H // KVH
        MAX_POS = 512
        ROPE_THETA = 10000.0

        def _rope_tables(max_pos, dim, theta):
            inv_freq = 1.0 / theta ** (jnp.arange(0, dim, 2, dtype=jnp.float32) / dim)
            t = jnp.arange(max_pos, dtype=jnp.float32)
            freqs = jnp.einsum('i,j->ij', t, inv_freq)
            emb = jnp.concatenate([freqs, freqs], axis=-1)
            return (jnp.cos(emb), jnp.sin(emb))

        def _rotate_half(x):
            x1, x2 = (x[..., :x.shape[-1] // 2], x[..., x.shape[-1] // 2:])
            return jnp.concatenate([-x2, x1], axis=-1)
        key = jax.random.key(seed)
        ks = jax.random.split(key, 8)
        scale_w = 1.0 / np.sqrt(E)
        query = jax.random.normal(ks[0], (B, S, E), dtype=jnp.float32)
        k_in = jax.random.normal(ks[1], (B, S, E), dtype=jnp.float32)
        v_in = jax.random.normal(ks[2], (B, S, E), dtype=jnp.float32)
        position_ids = jnp.broadcast_to(jnp.arange(S, dtype=jnp.int64), (B, S))
        src_mask = jnp.tril(jnp.ones((S, S), dtype=jnp.int32))
        src_mask = jnp.broadcast_to(src_mask, (B, S, S))
        Wq = jax.random.normal(ks[3], (E, H * D), dtype=jnp.float32) * scale_w
        Wk = jax.random.normal(ks[4], (E, KVH * D), dtype=jnp.float32) * scale_w
        Wv = jax.random.normal(ks[5], (E, KVH * D), dtype=jnp.float32) * scale_w
        Wo = jax.random.normal(ks[6], (H * D, E), dtype=jnp.float32) * scale_w
        return {'query': query, 'key': k_in, 'value': v_in, 'position_ids': position_ids, 'src_mask': src_mask, 'Wq': Wq, 'Wk': Wk, 'Wv': Wv, 'Wo': Wo}
    _L0_xattn_all = _L0_xattn_setup()
    _L0_xattn_in = {k: v for k, v in _L0_xattn_all.items() if k in ('Wq', 'Wk', 'Wv', 'Wo')}
    del _L0_xattn_all

    def _L0_ffn_setup():
        import jax, jax.numpy as jnp
        import numpy as np
        D_MODEL = 512
        D_FF = 1376
        key = jax.random.key(seed)
        k1, k2, k3, k4 = jax.random.split(key, 4)
        x = jax.random.normal(k1, (2, 256, D_MODEL), dtype=jnp.float32)
        W_gate = jax.random.normal(k2, (D_FF, D_MODEL), dtype=jnp.float32) * D_MODEL ** (-0.5)
        W_up = jax.random.normal(k3, (D_FF, D_MODEL), dtype=jnp.float32) * D_MODEL ** (-0.5)
        W_down = jax.random.normal(k4, (D_MODEL, D_FF), dtype=jnp.float32) * D_FF ** (-0.5)
        return {'x': x, 'W_gate': W_gate, 'W_up': W_up, 'W_down': W_down}
    _L0_ffn_all = _L0_ffn_setup()
    _L0_ffn_in = {k: v for k, v in _L0_ffn_all.items() if k in ('W_gate', 'W_up', 'W_down')}
    del _L0_ffn_all
    return {'x': x, 'ctx_4096': ctx_4096, 'pos_BxS2': pos_BxS2, 'mask_BxSxS2_ik0': mask_BxSxS2_ik0, 'L0_attn_Wq': _L0_attn_in['Wq'], 'L0_attn_Wkv': _L0_attn_in['Wkv'], 'L0_attn_Wo': _L0_attn_in['Wo'], 'L0_xattn_Wq': _L0_xattn_in['Wq'], 'L0_xattn_Wk': _L0_xattn_in['Wk'], 'L0_xattn_Wv': _L0_xattn_in['Wv'], 'L0_xattn_Wo': _L0_xattn_in['Wo'], 'L0_ffn_W_gate': _L0_ffn_in['W_gate'], 'L0_ffn_W_up': _L0_ffn_in['W_up'], 'L0_ffn_W_down': _L0_ffn_in['W_down']}

def reference(x, ctx_4096, pos_BxS2, mask_BxSxS2_ik0, L0_attn_Wq, L0_attn_Wkv, L0_attn_Wo, L0_xattn_Wq, L0_xattn_Wk, L0_xattn_Wv, L0_xattn_Wo, L0_ffn_W_gate, L0_ffn_W_up, L0_ffn_W_down):
    import jax
    import jax.numpy as jnp

    def _L0_attn_ref(hidden_states, Wq, Wkv, Wo):
        import jax, jax.numpy as jnp
        import numpy as np
        HIDDEN = 512
        NUM_HEADS = 32
        HEAD_DIM = HIDDEN // NUM_HEADS
        B, S = (2, 128)

        def _alibi_slopes(n):
            start = 2.0 ** (-2.0 ** (-(np.log2(n) - 3)))
            return np.array([start ** (i + 1) for i in range(n)], dtype=np.float32)
        b, s, h = hidden_states.shape
        scale = HEAD_DIM ** (-0.5)
        q = (hidden_states @ Wq).reshape(b, s, NUM_HEADS, HEAD_DIM)
        kv = hidden_states @ Wkv
        k, v = (kv[..., :HEAD_DIM], kv[..., HEAD_DIM:])
        scores = jnp.einsum('bqhd,bkd->bhqk', q, k) * scale
        pos = jnp.arange(s)
        slopes = jnp.asarray(_alibi_slopes(NUM_HEADS))
        bias = slopes[:, None, None] * (pos[None, None, :] - pos[None, :, None]).astype(jnp.float32)
        causal = pos[None, :] <= pos[:, None]
        scores = jnp.where(causal[None, None], scores + bias[None], -jnp.inf)
        attn = jax.nn.softmax(scores, axis=-1)
        out = jnp.einsum('bhqk,bkd->bqhd', attn, v).reshape(b, s, h)
        return out @ Wo

    def _L0_xattn_ref(query, key, value, position_ids, src_mask, Wq, Wk, Wv, Wo):
        import jax, jax.numpy as jnp
        import numpy as np
        B, S, E = (2, 256, 512)
        H, KVH, D = (32, 8, 128)
        GROUPS = H // KVH
        MAX_POS = 512
        ROPE_THETA = 10000.0

        def _rope_tables(max_pos, dim, theta):
            inv_freq = 1.0 / theta ** (jnp.arange(0, dim, 2, dtype=jnp.float32) / dim)
            t = jnp.arange(max_pos, dtype=jnp.float32)
            freqs = jnp.einsum('i,j->ij', t, inv_freq)
            emb = jnp.concatenate([freqs, freqs], axis=-1)
            return (jnp.cos(emb), jnp.sin(emb))

        def _rotate_half(x):
            x1, x2 = (x[..., :x.shape[-1] // 2], x[..., x.shape[-1] // 2:])
            return jnp.concatenate([-x2, x1], axis=-1)
        nb, q_len, _ = query.shape
        q = (query @ Wq).reshape(nb, q_len, H, D).transpose(0, 2, 1, 3)
        k = (key @ Wk).reshape(nb, q_len, KVH, D).transpose(0, 2, 1, 3)
        v = (value @ Wv).reshape(nb, q_len, KVH, D).transpose(0, 2, 1, 3)
        cos_t, sin_t = _rope_tables(MAX_POS, D, ROPE_THETA)
        cos = cos_t[position_ids][:, None]
        sin = sin_t[position_ids][:, None]
        q = q * cos + _rotate_half(q) * sin
        k = k * cos + _rotate_half(k) * sin
        k = jnp.repeat(k, GROUPS, axis=1)
        v = jnp.repeat(v, GROUPS, axis=1)
        scores = jnp.einsum('bhqd,bhkd->bhqk', q, k) / jnp.sqrt(jnp.float32(D))
        mask = src_mask[:, None]
        scores = jnp.where(mask == 0, jnp.float32(-1000000000.0), scores)
        attn = jax.nn.softmax(scores, axis=-1)
        x = jnp.einsum('bhqk,bhkd->bhqd', attn, v)
        x = x.transpose(0, 2, 1, 3).reshape(nb, q_len, H * D)
        return x @ Wo

    def _L0_ffn_ref(x, W_gate, W_up, W_down):
        import jax, jax.numpy as jnp
        import numpy as np
        D_MODEL = 512
        D_FF = 1376
        out_shape = x.shape[:-1] + (W_down.shape[0],)
        xf = x.reshape(-1, x.shape[-1])
        up = jnp.einsum('td,fd->tf', xf, W_up)
        gate = jax.nn.silu(jnp.einsum('td,fd->tf', xf, W_gate))
        h = gate * up
        y = jnp.einsum('tf,df->td', h, W_down)
        return y.reshape(out_shape)
    x = x + _L0_attn_ref(_layernorm(x, axis=-1), L0_attn_Wq, L0_attn_Wkv, L0_attn_Wo)
    x = x + _L0_xattn_ref(_layernorm(x, axis=-1), ctx_4096, ctx_4096, pos_BxS2, mask_BxSxS2_ik0, L0_xattn_Wq, L0_xattn_Wk, L0_xattn_Wv, L0_xattn_Wo)
    x = x + _L0_ffn_ref(_layernorm(x, axis=-1), L0_ffn_W_gate, L0_ffn_W_up, L0_ffn_W_down)
    return x

_drawn_inputs = setup_inputs


def setup_inputs(seed=0):
    import zlib

    import numpy as np

    out = dict(_drawn_inputs(seed))
    spreads = {}
    factors = {'L0_attn_Wq': 7.931}
    for name, (base, spread) in spreads.items():
        noise = np.random.default_rng([zlib.crc32(name.encode()), seed]).standard_normal(out[name].shape)
        drawn = base * np.exp(spread * noise) if base else spread * noise
        out[name] = jnp.asarray(drawn.astype(out[name].dtype))
    for name, factor in factors.items():
        out[name] = (out[name] * factor).astype(out[name].dtype)
    return out
```

```python
from contextlib import ExitStack

import concourse.bass as bass
from concourse import mybir

F32 = mybir.dt.float32
F32R = mybir.dt.float32r
I32 = mybir.dt.int32
ALU = mybir.AluOpType
ACT = mybir.ActivationFunctionType
AX = mybir.AxisListType

P = 128
SEQS = 8
DM = 512
KT = DM // P
HEADS = 32
HD1 = DM // HEADS
QUAD = 4
STEPS = HEADS // QUAD
D2 = 128
GROUPS = 8
HALF = SEQS // 2
HT = HALF * P
TOK = SEQS * P
FF = 1376
FT = (FF + P - 1) // P
FLAST = FF - (FT - 1) * P
MAX_POS = 512
EPS = 1e-5
SCALE1 = HD1 ** -0.5
SCALE2 = float(D2) ** -0.5
MASKED = -1.0e9
UNMASKED = 3.0e38


def alibi_slopes():
    start = 2.0 ** (-2.0 ** (-(5 - 3)))
    return [start ** (i + 1) for i in range(HEADS)]


def block_of(t, b, n=P):
    return t[..., bass.ds(b * n, n)]


def self_attention(nc, m, sem, ps, io):
    SC, TB, OB, G = ps[0:2], ps[2:4], ps[4:6], ps[6:8]
    x, hsT, ctxT = m["x"], m["hsT_hl"], m["ctxT_hl"]
    ident = m["ident"]
    with ExitStack() as stack:
        def sb(name, shape, dt=F32):
            return stack.enter_context(nc.sbuf_tensor(name, shape, dt))

        bias = sb("alibi_bias", [P, HEADS, P])
        rel = sb("relative_position", [P, P])
        head_of_row = sb("head_of_row", [P, 8])
        wq = sb("self_wq", [P, KT, DM])
        wo = sb("self_wo", [P, KT, DM])
        wkv = sb("self_wkv", [P, KT, 2 * HD1])
        wk8 = sb("self_wk_8_times", [P, KT, 8, HD1])
        stats = sb("self_stats", [P, 2, 6])
        mv = sb("x1_mean_var", [P, 2])
        rstd = sb("x1_rstd", [P, 2])
        mv0 = sb("x_mean_var", [P, SEQS, 2])
        rstd0 = sb("x_rstd", [P, 2, SEQS])
        exponent = sb("minus_half_and_eps", [P, 2])
        xn = sb("xn", [P, DM])
        xnT = sb("xnT", [P, KT, P])
        q_tok = sb("q_tok", [P, DM])
        qT = sb("self_qT", [P, KT, P])
        kT = sb("self_kT_8_times", [P, P])
        kexp = sb("self_k_by_head", [P, 8, P])
        v = sb("self_v_and_ones", [P, SEQS, HD1 + 1])
        S = sb("self_scores", [P, 2, QUAD, P])
        PR = sb("self_probs", [P, 2, QUAD, P])
        negmax = sb("self_negmax", [P, 2, QUAD])
        PT = sb("self_probsT", [P, 2, QUAD, P])
        rsum = sb("self_rsum", [P, HEADS])
        attn = sb("self_attn", [P, DM])
        attnT = sb("self_attnT", [P, KT, P])
        hs = sb("self_hs", [P, DM])
        ctx_tok = sb("ctx_tok", [P, DM])
        tables = sb("rope_rows", [P, SEQS, 2 * D2])
        pos = sb("positions", [P, SEQS], I32)
        mask = sb("mask", [P, SEQS, P], I32)
        unmasked = sb("unmasked", [P, P])

        slopes = alibi_slopes()
        block = stack.enter_context(nc.Block())

        @block.sync
        def _(sp):
            sp.dma_start(x[:, 0, :], io["x"][0]).then_inc(sem["x_first"], 16)
            sp.dma_start(rel[:], io["constants"][:, 0:P]).then_inc(sem["rel_loaded"], 16)
            sp.dma_start(head_of_row[:], io["constants"][:, P:P + 8]).then_inc(sem["head_of_row_loaded"], 16)
            sp.dma_start(wkv[:], io["wkv1"].rearrange("(t p) n -> p t n", p=P)).then_inc(sem["wkv1_loaded"], 16)
            sp.dma_start(wq[:], io["wq1"].rearrange("(t p) n -> p t n", p=P)).then_inc(sem["wq1_loaded"], 16)
            sp.dma_start(x[:, 1:SEQS, :], io["x"][1:SEQS].rearrange("b p d -> p b d")).then_inc(sem["x_rest"], 16)
            sp.dma_start(pos[:], io["pos"]).then_inc(sem["pos_loaded"], 16)
            sp.dma_start(wo[:], io["wo1"].rearrange("(t p) n -> p t n", p=P)).then_inc(sem["wo1_loaded"], 16)
            sp.dma_start(mask[:], io["mask"].rearrange("b q k -> q b k")).then_inc(sem["mask_loaded"], 16)

            def load_ctx(b):
                sp.dma_start(ctx_tok[:], io["ctx"][bass.ds(b, 1)].rearrange("b p d -> p (b d)")).then_inc(sem["ctx_loaded"], 16)

            load_ctx(0)
            with sp.Fori(1, SEQS) as b:
                sp.wait_ge(sem["ctx_transposed"], b)
                load_ctx(b)
            for j in range(PIECES):
                load_piece(sp, m, sem, j, piece_source(io, j, 0), first=j < 2)

        @block.gpsimd
        def _(pool):
            nc.gpsimd.memset(ident[:], 0.0).then_inc(sem["ident_zero"], 1)
            pool.wait_ge(sem["ident_zero"], 1)
            nc.gpsimd.affine_select(out=ident[:], in_=ident[:], compare_op=ALU.not_equal, fill=1.0, base=0,
                                    pattern=[[-1, P]], channel_multiplier=1).then_inc(sem["ident_ready"], 1)
            nc.gpsimd.memset(exponent[:, 0:1], -0.5).then_inc(sem["exponent_ready"], 1)
            nc.gpsimd.memset(exponent[:, 1:2], EPS).then_inc(sem["exponent_ready"], 1)
            nc.gpsimd.memset(v[:], 1.0).then_inc(sem["ones_ready"], 1)
            nc.gpsimd.memset(m["one"][:], 1.0).then_inc(sem["one_ready"], 1)
            pool.wait_ge(sem["one_ready"], 1)

            def rstd_of_x(first, last):
                n = last - first
                pool.wait_ge(sem["mv0"], last)
                nc.gpsimd.tensor_tensor(rstd0[:, 0, first:last], mv0[:, first:last, 1], exponent[:, 1:2].to_broadcast([P, n]), ALU.add).then_inc(sem["var_eps0"], 1)
                pool.wait_ge(sem["var_eps0"], 1 if first == 0 else 2)
                nc.gpsimd.tensor_tensor(rstd0[:, 1, first:last], rstd0[:, 0, first:last], exponent[:, 0:1].to_broadcast([P, n]), ALU.pow).then_inc(sem["rstd0"], 1)

            def rstd_of_x1(b):
                pool.wait_ge(sem["mv1"], b + 1)
                nc.gpsimd.tensor_tensor(rstd[:, 0:1], mv[:, 1:2], exponent[:, 1:2], ALU.add).then_inc(sem["var_eps1"], 1)
                pool.wait_ge(sem["var_eps1"], b + 1)
                nc.gpsimd.tensor_tensor(rstd[:, 1:2], rstd[:, 0:1], exponent[:, 0:1], ALU.pow).then_inc(sem["rstd1"], 1)

            def keys_by_head(c, first=False):
                pool.wait_ge(sem["kv_copied"], c + 1)
                if not first:
                    pool.wait_ge(sem["scores1"], STEPS * c)
                nc.gpsimd.tensor_tensor(kexp[:], kT[:].unsqueeze(1).to_broadcast([P, 8, P]),
                                        head_of_row[:].unsqueeze(2).to_broadcast([P, 8, P]), ALU.mult).then_inc(sem["kexp"], 1)

            pool.wait_ge(sem["exponent_ready"], 2)
            rstd_of_x(0, 1)
            pool.wait_ge(sem["rel_loaded"], 16)
            for h in range(HEADS):
                nc.gpsimd.tensor_scalar(bias[:, h, :], rel[:], slopes[h], None, ALU.mult).then_inc(sem["bias"], 1)
                if h == QUAD - 1:
                    pool.wait_ge(sem["head_of_row_loaded"], 16)
                    keys_by_head(0, first=True)
                    rstd_of_x(1, SEQS)
            pool.wait_ge(sem["pos_loaded"], 16)
            for b in range(SEQS):
                nc.gpsimd.indirect_dma_start(
                    tables[:, b, :], None, io["rope"], bass.IndirectOffsetOnAxis(ap=pos[:, b:b + 1].bitcast(mybir.dt.uint32), axis=0),
                ).then_inc(sem["tables_loaded"], 16)

            def body(b, front, back):
                if back:
                    rstd_of_x1(b - 1)
                if front:
                    keys_by_head(b + 1)

            body(0, True, False)
            body(1, True, True)
            with pool.Fori(2, SEQS - 1) as b:
                body(b, True, True)
            body(SEQS - 1, False, True)
            body(SEQS, False, True)
            for j in range(PIECES):
                src = split_piece(nc, pool, m, sem, j % 2, j // 2 + 1, m["wqkv_hl"][:, j])
                pool.wait_ge(sem["piece_high"], j + 1)
                nc.gpsimd.tensor_tensor(m["wqkv_hl"][:, j, 1], src, m["wqkv_hl"][:, j, 0].bitcast(F32), ALU.subtract).then_inc(sem["piece_split"], 1)

        @block.vector
        def _(dve):
            def stats_of_x(b):
                if b > 0:
                    dve.wait_ge(sem["mv0"], b)
                nc.vector.bn_stats(stats[:, 0, :], x[:, b, :]).then_inc(sem["stats0"], 1)
                dve.wait_ge(sem["stats0"], b + 1)
                nc.vector.bn_aggr(mv0[:, b, :], stats[:, 0, :]).then_inc(sem["mv0"], 1)

            def xn_of(c, first=False):
                dve.wait_ge(sem["rstd0"], 1 if first else 2)
                if not first:
                    dve.wait_ge(sem["xn_transposed"], c)
                nc.vector.tensor_scalar(xn[:].unsqueeze(1), x[:, bass.ds(c, 1), :], mv0[:, bass.ds(c, 1), 0], rstd0[:, 1, bass.ds(c, 1)],
                                        ALU.subtract, ALU.mult).then_inc(sem["xn"], 1)

            dve.wait_ge(sem["x_first"], 16)
            stats_of_x(0)
            dve.wait_ge(sem["wkv1_loaded"], 16)
            nc.vector.tensor_copy(wk8[:], wkv[:, :, 0:HD1].unsqueeze(2).to_broadcast([P, KT, 8, HD1])).then_inc(sem["wk8"], 1)
            xn_of(0, first=True)
            nc.vector.memset(m["cap"][:], MASKED).then_inc(sem["cap_filled"], 1)
            nc.vector.memset(unmasked[:], UNMASKED).then_inc(sem["cap_filled"], 1)
            dve.wait_ge(sem["x_rest"], 16)
            for b in range(1, SEQS):
                stats_of_x(b)

            def body(b, scores, front, back, first=False):
                for s in range(STEPS if scores or back else 0):
                    n = STEPS * b + s
                    if scores:
                        dve.wait_ge(sem["scores1"], n + 1)
                        if not first or s >= 2:
                            dve.wait_ge(sem["exp1"], n - 1)
                        if first:
                            dve.wait_ge(sem["bias"], QUAD * (s + 1))
                        nc.vector.tensor_tensor(S[:, s % 2], SC[s % 2][:].rearrange("p (h k) -> p h k", h=QUAD),
                                                bias[:, QUAD * s:QUAD * s + QUAD, :], ALU.add).then_inc(sem["biased1"], 1)
                        dve.wait_ge(sem["biased1"], n + 1)
                        nc.vector.tensor_reduce(negmax[:, s % 2, :], S[:, s % 2], AX.X, ALU.max, negate=True).then_inc(sem["max1"], 1)
                    if s == 0 and scores:
                        dve.wait_ge(sem["ctx_high"], b + 1)
                        nc.vector.tensor_tensor(block_of(ctxT[:, 1], b), G[1][:].rearrange("p (t k) -> p t k", t=KT),
                                                block_of(ctxT[:, 0], b).bitcast(F32), ALU.subtract).then_inc(sem["ctx_low"], 1)
                    if s == 1 and front:
                        xn_of(b + 1)
                    if s == 3 and back:
                        dve.wait_ge(sem["pv1"], STEPS * b)
                        if not (isinstance(b, int) and b == 1):
                            dve.wait_ge(sem["attn"], 2 * (b - 1))
                        for i in range(2):
                            o = OB[i][:, 0:16 * (HD1 + 1)].rearrange("p (h d) -> p h d", h=16)
                            nc.vector.reciprocal(rsum[:, 16 * i:16 * i + 16].unsqueeze(2), o[:, :, HD1:HD1 + 1]).then_inc(sem["rsum1"], 1)
                        dve.wait_ge(sem["rsum1"], 2 * b)
                        if not (isinstance(b, int) and b == 1):
                            dve.wait_ge(sem["attn_transposed"], b - 1)
                        for i in range(2):
                            o = OB[i][:, 0:16 * (HD1 + 1)].rearrange("p (h d) -> p h d", h=16)
                            nc.vector.tensor_tensor(attn[:].rearrange("p (i h d) -> p i h d", i=2, h=16)[:, i], o[:, :, 0:HD1],
                                                    rsum[:, 16 * i:16 * i + 16].unsqueeze(2).to_broadcast([P, 16, HD1]),
                                                    ALU.mult).then_inc(sem["attn"], 1)
                    if s == 6 and back:
                        dve.wait_ge(sem["out1"], b)
                        if not (isinstance(b, int) and b == 1):
                            dve.wait_ge(sem["hs"], b - 1)
                        nc.vector.tensor_tensor(x[:, bass.ds(b - 1, 1), :], x[:, bass.ds(b - 1, 1), :], G[0][:].unsqueeze(1),
                                                ALU.add).then_inc(sem["x1"], 1)
                        dve.wait_ge(sem["x_first"], 16)
                        dve.wait_ge(sem["x1"], b)
                        nc.vector.bn_stats(stats[:, 1, :].unsqueeze(1), x[:, bass.ds(b - 1, 1), :]).then_inc(sem["stats1"], 1)
                        dve.wait_ge(sem["x_first"], 16)
                        dve.wait_ge(sem["stats1"], b)
                        nc.vector.bn_aggr(mv[:], stats[:, 1, :]).then_inc(sem["mv1"], 1)
                    if s == 7 and back:
                        dve.wait_ge(sem["rstd1"], b)
                        if not (isinstance(b, int) and b == 1):
                            dve.wait_ge(sem["hs_transposed"], b - 1)
                        nc.vector.tensor_scalar(hs[:].unsqueeze(1), x[:, bass.ds(b - 1, 1), :], mv[:, 0:1], rstd[:, 1:2],
                                                ALU.subtract, ALU.mult).then_inc(sem["hs"], 1)
                        dve.wait_ge(sem["hs_high"], b)
                        nc.vector.tensor_tensor(block_of(hsT[:, 1], b - 1), G[0][:].rearrange("p (t k) -> p t k", t=KT),
                                                block_of(hsT[:, 0], b - 1).bitcast(F32), ALU.subtract).then_inc(sem["hs_low"], 1)

            body(0, True, True, False, first=True)
            dve.wait_ge(sem["mask_loaded"], 16)
            dve.wait_ge(sem["cap_filled"], 2)
            for b in range(SEQS):
                nc.vector.copy_predicated(m["cap"][:, b, :], mask[:, b, :], unmasked[:])
            body(1, True, True, True)
            with dve.Fori(2, SEQS - 1) as b:
                body(b, True, True, True)
            body(SEQS - 1, True, False, True)
            body(SEQS, False, False, True)

        @block.scalar
        def _(act):
            def copy_xnT(c, first=False):
                act.wait_ge(sem["xn_transposed"], c + 1)
                if not first:
                    act.wait_ge(sem["kv1"], c)
                nc.scalar.copy(xnT[:], G[0][:].rearrange("p (t k) -> p t k", t=KT)).then_inc(sem["xnT"], 1)

            def copy_q(c, first=False):
                act.wait_ge(sem["q1"], c + 1)
                if not first:
                    act.wait_ge(sem["q_transposed"], c)
                nc.scalar.copy(q_tok[:], G[1][:]).then_inc(sem["q_copied"], 1)

            def copy_kv(c, first=False):
                act.wait_ge(sem["kv1"], c + 1)
                if first:
                    act.wait_ge(sem["ones_ready"], 1)
                else:
                    act.wait_ge(sem["kexp"], c)
                nc.scalar.copy(v[:, bass.ds(c, 1), 0:HD1], G[0][:, P:P + HD1].unsqueeze(1))
                nc.scalar.copy(kT[:], G[0][:, 0:P]).then_inc(sem["kv_copied"], 1)

            def copy_qT(c, first=False):
                act.wait_ge(sem["q_transposed"], c + 1)
                if not first:
                    act.wait_ge(sem["scores1"], STEPS * c)
                nc.scalar.copy(qT[:], G[1][:].rearrange("p (t k) -> p t k", t=KT)).then_inc(sem["qT"], 1)

            copy_xnT(0, first=True)
            copy_q(0, first=True)
            copy_kv(0, first=True)
            copy_qT(0, first=True)

            def body(b, scores, front, back, first=False):
                for s in range(STEPS):
                    n = STEPS * b + s
                    if (not first or s >= 2) and (scores or s < 2):
                        act.wait_ge(sem["probs_transposed1"], n - 1)
                        if not first or s >= 4:
                            act.wait_ge(sem["pv1"], n - 3)
                        nc.scalar.copy(PT[:, s % 2], TB[s % 2][:].rearrange("p (h k) -> p h k", h=QUAD)).then_inc(sem["probsT1"], 1)
                    if scores:
                        act.wait_ge(sem["max1"], n + 1)
                        if not first or s >= 2:
                            act.wait_ge(sem["probs_transposed1"], n - 1)
                        for j in range(QUAD):
                            e = nc.scalar.activation(PR[:, s % 2, j, :], S[:, s % 2, j, :], ACT.Exp, bias=negmax[:, s % 2, j:j + 1])
                        e.then_inc(sem["exp1"], 1)
                    if s == 0 and scores:
                        act.wait_ge(sem["ctx_transposed"], b + 1)
                        nc.scalar.copy(block_of(ctxT[:, 0], b), G[1][:].rearrange("p (t k) -> p t k", t=KT)).then_inc(sem["ctx_high"], 1)
                    if s == 2 and front:
                        copy_xnT(b + 1)
                    if s == 3 and front:
                        copy_q(b + 1)
                    if s == 4 and front:
                        copy_kv(b + 1)
                    if s == 4 and back:
                        act.wait_ge(sem["attn_transposed"], b)
                        if not (isinstance(b, int) and b == 1):
                            act.wait_ge(sem["out1"], b - 1)
                        nc.scalar.copy(attnT[:], G[1][:].rearrange("p (t k) -> p t k", t=KT)).then_inc(sem["attnT"], 1)
                    if s == 7 and front:
                        copy_qT(b + 1)
                    if s == 7 and back:
                        act.wait_ge(sem["hs_transposed"], b)
                        nc.scalar.copy(block_of(hsT[:, 0], b - 1), G[0][:].rearrange("p (t k) -> p t k", t=KT)).then_inc(sem["hs_high"], 1)

            body(0, True, True, False, first=True)
            body(1, True, True, True)
            with act.Fori(2, SEQS - 1) as b:
                body(b, True, True, True)
            body(SEQS - 1, True, False, True)
            body(SEQS, False, False, True)
            for i in range(HALF):
                act.wait_ge(sem["tables_transposed"], i + 1)
                t = ps[i][:].rearrange("p (b w k) -> p w b k", b=2, w=2)
                nc.scalar.copy(m["cosT"][:, 2 * i * P:2 * (i + 1) * P].rearrange("p (b k) -> p b k", b=2), t[:, 0])
                nc.scalar.copy(m["sinT"][:, 2 * i * P:2 * (i + 1) * P].rearrange("p (b k) -> p b k", b=2), t[:, 1])

        @block.tensor
        def _(pe):
            def transpose4(bank, src, done):
                for t in range(KT):
                    i = nc.tensor.transpose(bank[:, t * P:(t + 1) * P], src[:, t * P:(t + 1) * P], ident[:])
                i.then_inc(sem[done], 1)

            def xn_transposes(c):
                pe.wait_ge(sem["xn"], c + 1)
                transpose4(G[0], xn, "xn_transposed")

            def q_product(c):
                pe.wait_ge(sem["xnT"], c + 1)
                for t in range(KT):
                    i = nc.tensor.matmul(G[1][:], xnT[:, t, :], wq[:, t, :], start=(t == 0), stop=(t == KT - 1))
                i.then_inc(sem["q1"], 1)

            def kv_product(c):
                for t in range(KT):
                    nc.tensor.matmul(G[0][:, 0:P], wk8[:, t].rearrange("p r d -> p (r d)"), xnT[:, t, :], start=(t == 0), stop=(t == KT - 1))
                for t in range(KT):
                    i = nc.tensor.matmul(G[0][:, P:P + HD1], xnT[:, t, :], wkv[:, t, HD1:2 * HD1], start=(t == 0), stop=(t == KT - 1))
                i.then_inc(sem["kv1"], 1)

            def q_transposes(c):
                pe.wait_ge(sem["q_copied"], c + 1)
                transpose4(G[1], q_tok, "q_transposed")

            pe.wait_ge(sem["ident_ready"], 1)
            xn_transposes(0)
            pe.wait_ge(sem["wq1_loaded"], 16)
            q_product(0)
            pe.wait_ge(sem["wk8"], 1)
            kv_product(0)
            q_transposes(0)
            pe.wait_ge(sem["wo1_loaded"], 16)

            def body(b, scores, front, back, first=False):
                for s in range(STEPS):
                    n = STEPS * b + s
                    if scores:
                        if s == 0:
                            pe.wait_ge(sem["qT"], b + 1)
                            pe.wait_ge(sem["kexp"], b + 1)
                        if not first or s >= 2:
                            pe.wait_ge(sem["biased1"], n - 1)
                        nc.tensor.matmul(SC[s % 2][:], qT[:, s // 2, :], kexp[:, QUAD * (s % 2):QUAD * (s % 2) + QUAD, :].rearrange("p h k -> p (h k)"),
                                         start=True, stop=True).then_inc(sem["scores1"], 1)
                    if (not first or s >= 2) and (scores or s < 2):
                        pe.wait_ge(sem["exp1"], n - 1)
                        if not first or s >= 4:
                            pe.wait_ge(sem["probsT1"], n - 3)
                        for j in range(QUAD):
                            i = nc.tensor.transpose(TB[s % 2][:, j * P:(j + 1) * P], PR[:, s % 2, j, :], ident[:])
                        i.then_inc(sem["probs_transposed1"], 1)
                    if (not first or s >= 3) and (scores or s < 3):
                        r = (s - 3) % STEPS
                        owner = b if s >= 3 else b - 1
                        pe.wait_ge(sem["probsT1"], n - 2)
                        if r % HALF == 0 and not (isinstance(owner, int) and owner == 0):
                            pe.wait_ge(sem["attn"], 2 * owner)
                        for j in range(QUAD):
                            c = (QUAD * (r % HALF) + j) * (HD1 + 1)
                            i = nc.tensor.matmul(OB[r // HALF][:, c:c + HD1 + 1], PT[:, r % 2, j, :], v[:, bass.ds(owner, 1), :].rearrange("p b d -> p (b d)"),
                                                 start=True, stop=True)
                        i.then_inc(sem["pv1"], 1)
                    if s == 0 and scores:
                        pe.wait_ge(sem["ctx_loaded"], 16 * b + 16)
                        transpose4(G[1], ctx_tok, "ctx_transposed")
                    if s == 2 and front:
                        pe.wait_ge(sem["kv_copied"], b + 1)
                        if not (isinstance(b, int) and b < 2):
                            pe.wait_ge(sem["hs_low"], b - 1)
                        xn_transposes(b + 1)
                    if s == 3 and front:
                        pe.wait_ge(sem["ctx_low"], b + 1)
                        q_product(b + 1)
                    if s == 4 and front:
                        kv_product(b + 1)
                    if s == 4 and back:
                        if front:
                            pe.wait_ge(sem["q_copied"], b + 2)
                        elif scores:
                            pe.wait_ge(sem["ctx_low"], b + 1)
                        pe.wait_ge(sem["attn"], 2 * b)
                        transpose4(G[1], attn, "attn_transposed")
                    if s == 5 and back:
                        if front:
                            pe.wait_ge(sem["kv_copied"], b + 2)
                        else:
                            pe.wait_ge(sem["hs_low"], b - 1)
                        pe.wait_ge(sem["attnT"], b)
                        for t in range(KT):
                            i = nc.tensor.matmul(G[0][:], attnT[:, t, :], wo[:, t, :], start=(t == 0), stop=(t == KT - 1))
                        i.then_inc(sem["out1"], 1)
                    if s == 7 and front:
                        if first:
                            pe.wait_ge(sem["q_copied"], b + 2)
                        else:
                            pe.wait_ge(sem["attnT"], b)
                        q_transposes(b + 1)
                    if s == 7 and back:
                        pe.wait_ge(sem["hs"], b)
                        transpose4(G[0], hs, "hs_transposed")

            body(0, True, True, False, first=True)
            body(1, True, True, True)
            with pe.Fori(2, SEQS - 1) as b:
                body(b, True, True, True)
            body(SEQS - 1, True, False, True)
            body(SEQS, False, False, True)
            pe.wait_ge(sem["tables_loaded"], 16 * SEQS)
            pe.wait_ge(sem["biased1"], STEPS * SEQS)
            pe.wait_ge(sem["probsT1"], STEPS * SEQS)
            for i in range(HALF):
                for b in range(2):
                    for w in range(2):
                        t = nc.tensor.transpose(ps[i][:, (2 * b + w) * P:(2 * b + w + 1) * P], tables[:, 2 * i + b, w * P:(w + 1) * P], ident[:])
                t.then_inc(sem["tables_transposed"], 1)


PIECES = 6
PIECE_TURN = [0, 1, 2, 3, 8, 9]
WO_TURN = 4
TURNS = 10


def piece_source(io, j, g):
    name, at = ("wk2", g) if j == 0 else ("wv2", g) if j == PIECES - 1 else ("wq2", g * QUAD + (j - 1))
    return io[name].rearrange("(t p) n -> p t n", p=P)[:, :, bass.ds(at * P, P)]


def load_piece(sp, m, sem, turn, source, first=False):
    slot = (turn if isinstance(turn, int) else turn[1]) % 2
    turn = turn if isinstance(turn, int) else turn[0]
    if not first:
        sp.wait_ge(sem["piece_split"], turn - 1)
    dst = m["stage"][:, slot, :]
    if len(source.shape) == 3:
        dst = dst.rearrange("p (t n) -> p t n", t=KT)
    sp.dma_start(dst, source).then_inc(sem[f"piece_loaded{slot}"], 16)


def split_piece(nc, pool, m, sem, slot, loads, dst):
    pool.wait_ge(sem[f"piece_loaded{slot}"], 16 * loads)
    src = m["stage"][:, slot, :]
    if len(dst.shape) == 4:
        src = src.rearrange("p (t n) -> p t n", t=KT)
    one = m["one"][:].to_broadcast([P, DM])
    if len(dst.shape) == 4:
        one = one.rearrange("p (t n) -> p t n", t=KT)
    nc.gpsimd.tensor_tensor(dst[:, 0], src, one, ALU.mult).then_inc(sem["piece_high"], 1)
    return src


def products(nc, out, stationary, moving, first, last):
    for k, (a, b) in enumerate(((0, 0), (0, 1), (1, 0))):
        i = nc.tensor.matmul(out, stationary[:, a], moving[:, b], start=(first and k == 0), stop=(last and k == 2))
    return i


def half_of(t, half):
    return t[..., half * HT:(half + 1) * HT]


def cross_attention(nc, m, sem, ps, io):
    PB, SC, TB, OB, YB = ps[0:2], ps[2:4], ps[4:6], ps[6], ps[7]
    x, hsT, ctxT, cap, ident, w = m["x"], m["hsT_hl"], m["ctxT_hl"], m["cap"], m["ident"], m["wqkv_hl"]
    with ExitStack() as stack:
        def sb(name, shape, dt=F32):
            return stack.enter_context(nc.sbuf_tensor(name, shape, dt))

        wo = sb("cross_wo_hl", [P, 2, QUAD, DM], F32R)
        qT = sb("cross_qT_hl", [P, 2, QUAD, TOK], F32R)
        kT = sb("cross_kT_hl", [P, 2, TOK], F32R)
        v = sb("cross_v_hl", [P, 2, SEQS, D2], F32R)
        rot = sb("rotated", [P, 2, HT])
        cross = sb("rotated_other_half", [P, HT])
        S = sb("cross_scores", [P, 2, QUAD, P])
        negmax = sb("cross_negmax", [P, 2, QUAD])
        rowsum = sb("cross_rowsum", [P, 2, QUAD])
        rinv = sb("cross_rinv", [P, 2, QUAD])
        PT = sb("cross_probsT_hl", [P, 2, QUAD * P], F32R)
        oT = sb("cross_outT_hl", [P, 2, QUAD * P], F32R)
        block = stack.enter_context(nc.Block())

        def blocks_in(b):
            pairs = {0: (0, 1), 1: (2, 3), 2: (4, 5)}
            return [(j, 1, 0) for j in pairs.get(b, ())] + [(j, 0, 1) for j in pairs.get(b - 4, ())]

        def turns_in(b):
            return {1: [(0, 0, 1), (1, 1, 1)],
                    2: [(2, 2, 1), (3, 3, 1)] + [(WO_TURN + h, PIECES + h, 0) for h in range(QUAD)],
                    3: [(8, 4, 1), (9, 5, 1)]}.get(b, [])

        def turn_of(g, t, last):
            return PIECES + TURNS * g + (t - WO_TURN if last else t)

        @block.sync
        def _(sp):
            def body(g, last):
                for b in range(SEQS):
                    for t, which, ahead in turns_in(b):
                        if ahead and last:
                            continue
                        if which < PIECES:
                            source = piece_source(io, which, g + 1)
                        else:
                            source = io["wo2"][bass.ds((g * QUAD + which - PIECES) * P, P), :]
                        load_piece(sp, m, sem, (turn_of(g, t, last), t), source)

            with sp.Fori(0, GROUPS - 1) as g:
                body(g, False)
            body(GROUPS - 1, True)

        @block.gpsimd
        def _(pool):
            def rope_sum(rr, j, half):
                pool.wait_ge(sem["rope_read"], rr + 1)
                nc.gpsimd.tensor_tensor(rot[:, (half + j) % 2, :], rot[:, (half + j) % 2, :], cross[:], ALU.add).then_inc(sem["rope_sum"], 1)
                pool.wait_ge(sem["rope_high"], rr + 1)
                dst = kT if j == 0 else qT[:, :, j - 1]
                nc.gpsimd.tensor_tensor(half_of(dst[:, 1], half), rot[:, (half + j) % 2, :], half_of(dst[:, 0], half).bitcast(F32),
                                        ALU.subtract).then_inc(sem["rope_low"], 1)

            for j in range(PIECES - 1):
                rope_sum(j, j, 0)

            def body(g, first, last):
                for b in range(SEQS):
                    n = SEQS * g + b
                    for j, half, ahead in blocks_in(b):
                        if j < PIECES - 1 and not (ahead and last):
                            rope_sum(10 * (g + ahead) + 5 * half + j, j, half)
                    pool.wait_ge(sem["rinv2"], n + 1)
                    nc.gpsimd.tensor_tensor(S[:, b % 2], S[:, b % 2], rinv[:, b % 2, :].unsqueeze(2).to_broadcast([P, QUAD, P]), ALU.mult).then_inc(sem["probs2"], 1)
                    for t, which, ahead in turns_in(b):
                        if ahead and last:
                            continue
                        turn = turn_of(g, t, last)
                        loads = (PIECES // 2 + TURNS // 2 * g) + (t - WO_TURN if last else t) // 2 + 1
                        if which < PIECES:
                            pool.wait_ge(sem["projected"], 12 * g + 6 + which + 1)
                            dst = w[:, which]
                        else:
                            if not first:
                                pool.wait_ge(sem["out2"], SEQS * g)
                            dst = wo[:, :, which - PIECES]
                        src = split_piece(nc, pool, m, sem, t % 2, loads, dst)
                        pool.wait_ge(sem["piece_high"], turn + 1)
                        nc.gpsimd.tensor_tensor(dst[:, 1], src, dst[:, 0].bitcast(F32), ALU.subtract).then_inc(sem["piece_split"], 1)

            body(0, True, False)
            with pool.Fori(1, GROUPS - 1) as g:
                body(g, False, False)
            body(GROUPS - 1, False, True)

        @block.vector
        def _(dve):
            def rope(g, half, j, first=False):
                rr = 10 * g + 5 * half + j
                pb = PB[j % 2]
                dve.wait_ge(sem["projected"], 12 * g + 6 * half + j + 1)
                if not first or j >= 2:
                    dve.wait_ge(sem["rope_low"], rr - 1)
                if not first or j >= 1:
                    dve.wait_ge(sem["rope_sum"], rr)
                nc.vector.tensor_tensor(rot[:, (half + j) % 2, :], pb[:], half_of(m["cosT"][:], half), ALU.mult)
                nc.vector.tensor_tensor(cross[0:64, :], pb[64:128, :], half_of(m["sinT"][0:64, :], half), ALU.mult)
                nc.vector.tensor_tensor(cross[64:128, :], pb[0:64, :], half_of(m["sinT"][64:128, :], half), ALU.mult).then_inc(sem["rope_read"], 1)

            def v_low(g, half):
                dve.wait_ge(sem["v_high"], 2 * g + half + 1)
                nc.vector.tensor_tensor(v[:, 1, half * HALF:(half + 1) * HALF, :], PB[1][:].rearrange("p (b d) -> p b d", b=HALF),
                                        v[:, 0, half * HALF:(half + 1) * HALF, :].bitcast(F32), ALU.subtract).then_inc(sem["v_low"], 1)

            for j in range(PIECES - 1):
                rope(0, 0, j, first=True)
            v_low(0, 0)

            def body(g, first, last, tail=False):
                for b in range(3 if tail else SEQS):
                    n = SEQS * g + b
                    blocks = [x for x in blocks_in(b) if not (x[2] and last)] if not tail else []
                    if not tail:
                        dve.wait_ge(sem["scores2"], n + 1)
                        if not first or b >= 2:
                            dve.wait_ge(sem["probs_transposed2"], n - 1)
                        nc.vector.scalar_tensor_tensor(out=S[:, b % 2], in0=SC[b % 2][:].rearrange("p (h k) -> p h k", h=QUAD), scalar=SCALE2,
                                                       in1=cap[:, b, :].unsqueeze(1).to_broadcast([P, QUAD, P]), op0=ALU.mult, op1=ALU.min).then_inc(sem["masked2"], 1)
                        dve.wait_ge(sem["masked2"], n + 1)
                        nc.vector.tensor_reduce(negmax[:, b % 2, :], S[:, b % 2], AX.X, ALU.max, negate=True).then_inc(sem["max2"], 1)
                    for j, half, ahead in blocks[:1]:
                        rope(g + ahead, half, j)
                    if not first or b >= 3:
                        y = (b - 3) % SEQS
                        dve.wait_ge(sem["out2"], n - 2)
                        if not first or b >= 4:
                            dve.wait_ge(sem["x2"], n - 3)
                        nc.vector.tensor_tensor(x[:, y, :], x[:, y, :], YB[:], ALU.add).then_inc(sem["x2"], 1)
                    for j, half, ahead in blocks[1:]:
                        if j < PIECES - 1:
                            rope(g + ahead, half, j)
                        else:
                            v_low(g + ahead, half)
                    if not tail:
                        dve.wait_ge(sem["exp2"], n + 1)
                        nc.vector.reciprocal(rinv[:, b % 2, :], rowsum[:, b % 2, :]).then_inc(sem["rinv2"], 1)
                    if (not first or b >= 2) and (not tail or b < 2):
                        dve.wait_ge(sem["outT_high"], n - 1)
                        nc.vector.tensor_tensor(oT[:, 1], OB[:], oT[:, 0].bitcast(F32), ALU.subtract).then_inc(sem["outT_low"], 1)
                    if (not first or b >= 1) and (not tail or b < 1):
                        dve.wait_ge(sem["probsT_high"], n)
                        nc.vector.tensor_tensor(PT[:, 1], TB[(b - 1) % 2][:], PT[:, 0].bitcast(F32), ALU.subtract).then_inc(sem["probsT_low"], 1)

            body(0, True, False)
            with dve.Fori(1, GROUPS - 1) as g:
                body(g, False, False)
            body(GROUPS - 1, False, True)
            body(GROUPS, False, True, tail=True)

        @block.scalar
        def _(act):
            def rope_high(g, half, j, first=False):
                act.wait_ge(sem["rope_sum"], 10 * g + 5 * half + j + 1)
                if not first:
                    act.wait_ge(sem["scores2"], SEQS * g if half else SEQS * g - HALF)
                dst = kT if j == 0 else qT[:, :, j - 1]
                nc.scalar.copy(half_of(dst[:, 0], half), rot[:, (half + j) % 2, :]).then_inc(sem["rope_high"], 1)

            def v_high(g, half, first=False):
                act.wait_ge(sem["projected"], 12 * g + 6 * half + 6)
                if not first:
                    act.wait_ge(sem["pv2"], SEQS * g if half else SEQS * g - HALF)
                nc.scalar.copy(v[:, 0, half * HALF:(half + 1) * HALF, :], PB[1][:].rearrange("p (b d) -> p b d", b=HALF)).then_inc(sem["v_high"], 1)

            for j in range(PIECES - 1):
                rope_high(0, 0, j, first=True)
            v_high(0, 0, first=True)

            def body(g, first, last, tail=False):
                for b in range(2 if tail else SEQS):
                    n = SEQS * g + b
                    if not tail:
                        act.wait_ge(sem["max2"], n + 1)
                        for h in range(QUAD):
                            e = nc.scalar.activation(S[:, b % 2, h, :], S[:, b % 2, h, :], ACT.Exp, bias=negmax[:, b % 2, h:h + 1],
                                                     accum_out=rowsum[:, b % 2, h:h + 1])
                        e.then_inc(sem["exp2"], 1)
                        for j, half, ahead in blocks_in(b):
                            if ahead and last:
                                continue
                            if j < PIECES - 1:
                                rope_high(g + ahead, half, j, first=first and not ahead)
                            else:
                                v_high(g + ahead, half, first=first and not ahead)
                    if (not first or b >= 2) and (not tail or b < 2):
                        act.wait_ge(sem["pv2"], n - 1)
                        if not first or b >= 3:
                            act.wait_ge(sem["out2"], n - 2)
                        nc.scalar.copy(oT[:, 0], OB[:]).then_inc(sem["outT_high"], 1)
                    if (not first or b >= 1) and (not tail or b < 1):
                        act.wait_ge(sem["probs_transposed2"], n)
                        if not first or b >= 2:
                            act.wait_ge(sem["pv2"], n - 1)
                        nc.scalar.copy(PT[:, 0], TB[(b - 1) % 2][:]).then_inc(sem["probsT_high"], 1)

            body(0, True, False)
            with act.Fori(1, GROUPS - 1) as g:
                body(g, False, False)
            body(GROUPS - 1, False, True)
            body(GROUPS, False, True, tail=True)

        @block.tensor
        def _(pe):
            def project(g, half, j, first=False):
                rr = 10 * g + 5 * half + j
                if j == 0 and not first:
                    pe.wait_ge(sem["rope_read"], rr)
                elif j == 1 and not first:
                    pe.wait_ge(sem["v_low"], 2 * g + half)
                elif 2 <= j < PIECES - 1:
                    pe.wait_ge(sem["rope_read"], rr - 1)
                elif j == PIECES - 1:
                    pe.wait_ge(sem["rope_read"], rr - 1)
                if half == 0:
                    turn = j if isinstance(g, int) and g == 0 else PIECES + TURNS * (g - 1) + PIECE_TURN[j]
                    pe.wait_ge(sem["piece_split"], turn + 1)
                if j < PIECES - 1:
                    src = ctxT if j == 0 else hsT
                    for t in range(KT):
                        i = products(nc, PB[j % 2][:], w[:, j, :, t], half_of(src[:, :, t], half), t == 0, t == KT - 1)
                else:
                    for b in range(HALF):
                        for t in range(KT):
                            i = products(nc, PB[1][:, b * P:(b + 1) * P], ctxT[:, :, t, (half * HALF + b) * P:(half * HALF + b + 1) * P], w[:, j, :, t],
                                         t == 0, t == KT - 1)
                i.then_inc(sem["projected"], 1)

            for j in range(PIECES):
                project(0, 0, j, first=True)

            def body(g, first, last, tail=False):
                for b in range(3 if tail else SEQS):
                    n = SEQS * g + b
                    blocks = [x for x in blocks_in(b) if not (x[2] and last)] if not tail else []
                    if not tail:
                        if b % HALF == 0:
                            pe.wait_ge(sem["rope_low"], 10 * g + (10 if b else 5))
                        if not first or b >= 2:
                            pe.wait_ge(sem["masked2"], n - 1)
                        for h in range(QUAD):
                            i = products(nc, SC[b % 2][:, h * P:(h + 1) * P], qT[:, :, h, b * P:(b + 1) * P], kT[:, :, b * P:(b + 1) * P], True, True)
                        i.then_inc(sem["scores2"], 1)
                    for j, half, ahead in blocks[:1]:
                        project(g + ahead, half, j)
                    if not first or b >= 3:
                        if b == 3:
                            pe.wait_ge(sem["piece_split"], turn_of(g, WO_TURN + QUAD, last))
                        pe.wait_ge(sem["outT_low"], n - 2)
                        if not first or b >= 4:
                            pe.wait_ge(sem["x2"], n - 3)
                        for h in range(QUAD):
                            i = products(nc, YB[:], oT[:, :, h * P:(h + 1) * P], wo[:, :, h], h == 0, h == QUAD - 1)
                        i.then_inc(sem["out2"], 1)
                    for j, half, ahead in blocks[1:]:
                        project(g + ahead, half, j)
                    if (not first or b >= 2) and (not tail or b < 2):
                        if b == 2:
                            pe.wait_ge(sem["v_low"], 2 * g + 1)
                        if b == 6:
                            pe.wait_ge(sem["v_low"], 2 * g + 2)
                        pe.wait_ge(sem["probsT_low"], n - 1)
                        if not first or b >= 3:
                            pe.wait_ge(sem["outT_low"], n - 2)
                        products(nc, OB[:], v[:, :, (b - 2) % SEQS, :], PT[:], True, True).then_inc(sem["pv2"], 1)
                    if (not first or b >= 1) and (not tail or b < 1):
                        pe.wait_ge(sem["probs2"], n)
                        if not first or b >= 3:
                            pe.wait_ge(sem["probsT_low"], n - 2)
                        for h in range(QUAD):
                            i = nc.tensor.transpose(TB[(b - 1) % 2][:, h * P:(h + 1) * P], S[:, (b - 1) % 2, h, :], ident[:])
                        i.then_inc(sem["probs_transposed2"], 1)

            body(0, True, False)
            with pe.Fori(1, GROUPS - 1) as g:
                body(g, False, False)
            body(GROUPS - 1, False, True)
            body(GROUPS, False, True, tail=True)


def feed_forward(nc, m, sem, ps, io):
    GATE, UP, TW, TD, YB = ps[0:2], ps[2:4], ps[4:6], ps[6], [ps[7], ps[6]]
    x, hsT, ident = m["x"], m["hsT_hl"], m["ident"]
    with ExitStack() as stack:
        def sb(name, shape, dt=F32):
            return stack.enter_context(nc.sbuf_tensor(name, shape, dt))

        hT = sb("ff_hT_hl", [P, 2, FT, TOK], F32R)
        wdT = sb("ff_downT_hl", [P, 2, FT, DM], F32R)
        wT = sb("ff_gate_upT_hl", [P, 2, 2, KT, P], F32R)
        raw = sb("ff_gate_up_rows", [P, 2, DM])
        rawd = sb("ff_down_rows", [P, KT, P])
        tmp = sb("ff_work", [P, 4, DM])
        stats = sb("x2_stats", [P, 6])
        mv = sb("x2_mean_var", [P, SEQS, 2])
        rstd = sb("x2_rstd", [P, 2, SEQS])
        exponent = sb("minus_half_and_eps_again", [P, 2])
        block = stack.enter_context(nc.Block())

        def width(i):
            return FLAST if isinstance(i, int) and i == FT - 1 else P

        @block.sync
        def _(sp):
            def load(i, first=False):
                n = width(i)
                at = i * P if isinstance(i, int) else sp.snap(i * P)
                for k, name in enumerate(("wg", "wu")):
                    if not first:
                        sp.wait_ge(sem["w_transposed"], 2 * i + k - 1)
                    if not first and k == 1:
                        sp.wait_ge(sem["wd_transposed"], i)
                    sp.dma_start(raw[0:n, k, :], io[name][bass.ds(at, n), :]).then_inc(sem[f"{name}_loaded"], 16)
                sp.dma_start(rawd[:, :, 0:n], io["wd"].rearrange("(t p) f -> p t f", p=P)[:, :, bass.ds(at, n)]).then_inc(sem["wd_loaded"], 16)

            load(0, first=True)
            with sp.Fori(1, FT - 1) as i:
                load(i)
            load(FT - 1)
            for b in range(SEQS):
                sp.wait_ge(sem["x3"], b + 1)
                sp.dma_start(io["out"][b], x[:, b, :]).then_inc(sem["out_stored"], 16)
            sp.wait_ge(sem["out_stored"], 16 * SEQS)

        @block.gpsimd
        def _(pool):
            nc.gpsimd.memset(exponent[:, 0:1], -0.5).then_inc(sem["exponent3_ready"], 1)
            nc.gpsimd.memset(exponent[:, 1:2], EPS).then_inc(sem["exponent3_ready"], 1)
            pool.wait_ge(sem["exponent3_ready"], 2)
            pool.wait_ge(sem["mv2"], SEQS)
            nc.gpsimd.tensor_tensor(rstd[:, 0, :], mv[:, :, 1], exponent[:, 1:2].to_broadcast([P, SEQS]), ALU.add).then_inc(sem["var_eps2"], 1)
            pool.wait_ge(sem["var_eps2"], 1)
            nc.gpsimd.tensor_tensor(rstd[:, 1, :], rstd[:, 0, :], exponent[:, 0:1].to_broadcast([P, SEQS]), ALU.pow).then_inc(sem["rstd2"], 1)

            def h_low(i):
                n = width(i)
                for half in range(2):
                    pool.wait_ge(sem["h_high"], 2 * i + half + 1)
                    nc.gpsimd.tensor_tensor(half_of(hT[0:n, 1, bass.ds(i, 1), :], half), tmp[0:n, 2 + half:3 + half, :],
                                            half_of(hT[0:n, 0, bass.ds(i, 1), :], half).bitcast(F32), ALU.subtract).then_inc(sem["h_low"], 1)

            h_low(0)
            with pool.Fori(1, FT - 1) as i:
                h_low(i)
            h_low(FT - 1)

        @block.vector
        def _(dve):
            for b in range(SEQS):
                if b > 0:
                    dve.wait_ge(sem["mv2"], b)
                nc.vector.bn_stats(stats[:], x[:, b, :]).then_inc(sem["stats2"], 1)
                dve.wait_ge(sem["stats2"], b + 1)
                nc.vector.bn_aggr(mv[:, b, :], stats[:]).then_inc(sem["mv2"], 1)
            dve.wait_ge(sem["rstd2"], 1)
            for b in range(SEQS + 1):
                if b < SEQS:
                    if b >= 2:
                        dve.wait_ge(sem["hs2_transposed"], b - 1)
                    nc.vector.tensor_scalar(tmp[:, b % 2, :], x[:, b, :], mv[:, b, 0:1], rstd[:, 1, b:b + 1], ALU.subtract, ALU.mult).then_inc(sem["hs2"], 1)
                if b > 0:
                    dve.wait_ge(sem["hs2_high"], b)
                    nc.vector.tensor_tensor(block_of(hsT[:, 1], b - 1), TW[(b - 1) % 2][:].rearrange("p (t k) -> p t k", t=KT),
                                            block_of(hsT[:, 0], b - 1).bitcast(F32), ALU.subtract).then_inc(sem["hs2_low"], 1)

            def w_low(i, k):
                n = width(i)
                dve.wait_ge(sem["w_high"], 2 * i + k + 1)
                nc.vector.tensor_tensor(wT[:, k, 1, :, 0:n], TW[k][:].rearrange("p (t f) -> p t f", t=KT)[:, :, 0:n],
                                        wT[:, k, 0, :, 0:n].bitcast(F32), ALU.subtract).then_inc(sem["w_low"], 1)

            def body(i, first=False):
                n = width(i)
                w_low(i, 1)
                dve.wait_ge(sem["wd_high"], i + 1)
                nc.vector.tensor_tensor(wdT[0:n, 1, bass.ds(i, 1), :], TD[0:n, :].unsqueeze(1), wdT[0:n, 0, bass.ds(i, 1), :].bitcast(F32),
                                        ALU.subtract).then_inc(sem["wd_low"], 1)
                if not (isinstance(i, int) and i == FT - 1):
                    w_low(i + 1, 0)
                for half in range(2):
                    dve.wait_ge(sem["silu"], 2 * i + half + 1)
                    dve.wait_ge(sem["ff_product"], 4 * i + half + 3)
                    if not first:
                        dve.wait_ge(sem["h_low"], 2 * i + half - 1)
                    nc.vector.tensor_tensor(tmp[0:n, 2 + half, :], tmp[0:n, half, :], UP[half][0:n, :], ALU.mult).then_inc(sem["h_product"], 1)

            w_low(0, 0)
            body(0, first=True)
            with dve.Fori(1, FT - 2) as i:
                body(i)
            body(FT - 2)
            body(FT - 1)
            for b in range(SEQS):
                dve.wait_ge(sem["y3"], b + 1)
                nc.vector.tensor_tensor(x[:, b, :], x[:, b, :], YB[b % 2][:], ALU.add).then_inc(sem["x3"], 1)

        @block.scalar
        def _(act):
            for b in range(SEQS):
                act.wait_ge(sem["hs2_transposed"], b + 1)
                nc.scalar.copy(block_of(hsT[:, 0], b), TW[b % 2][:].rearrange("p (t k) -> p t k", t=KT)).then_inc(sem["hs2_high"], 1)

            def w_high(i, k, first=False):
                n = width(i)
                act.wait_ge(sem["w_transposed"], 2 * i + k + 1)
                if not first:
                    act.wait_ge(sem["ff_product"], 4 * i + 2 * k - 2)
                nc.scalar.copy(wT[:, k, 0, :, 0:n], TW[k][:].rearrange("p (t f) -> p t f", t=KT)[:, :, 0:n]).then_inc(sem["w_high"], 1)

            def body(i, first=False):
                n = width(i)
                w_high(i, 1, first)
                act.wait_ge(sem["wd_transposed"], i + 1)
                nc.scalar.copy(wdT[0:n, 0, bass.ds(i, 1), :], TD[0:n, :].unsqueeze(1)).then_inc(sem["wd_high"], 1)
                for half in range(2):
                    act.wait_ge(sem["ff_product"], 4 * i + half + 1)
                    if not first:
                        act.wait_ge(sem["h_product"], 2 * i + half - 1)
                    nc.scalar.activation(tmp[0:n, half, :], GATE[half][0:n, :], ACT.Silu).then_inc(sem["silu"], 1)
                if not (isinstance(i, int) and i == FT - 1):
                    w_high(i + 1, 0)
                for half in range(2):
                    act.wait_ge(sem["h_product"], 2 * i + half + 1)
                    nc.scalar.copy(half_of(hT[0:n, 0, bass.ds(i, 1), :], half), tmp[0:n, 2 + half:3 + half, :]).then_inc(sem["h_high"], 1)

            w_high(0, 0, first=True)
            body(0, first=True)
            with act.Fori(1, FT - 2) as i:
                body(i)
            body(FT - 2)
            body(FT - 1)

        @block.tensor
        def _(pe):
            for b in range(SEQS):
                pe.wait_ge(sem["hs2"], b + 1)
                if b >= 2:
                    pe.wait_ge(sem["hs2_low"], b - 1)
                for t in range(KT):
                    i = nc.tensor.transpose(TW[b % 2][:, t * P:(t + 1) * P], tmp[:, b % 2, t * P:(t + 1) * P], ident[:])
                i.then_inc(sem["hs2_transposed"], 1)

            def w_transposes(i, k, first=False):
                n = width(i)
                pe.wait_ge(sem["wg_loaded" if k == 0 else "wu_loaded"], 16 * i + 16)
                if first:
                    pe.wait_ge(sem["hs2_low"], SEQS)
                else:
                    pe.wait_ge(sem["w_low"], 2 * i + k - 1)
                for t in range(KT):
                    e = nc.tensor.transpose(TW[k][:, t * P:t * P + n], raw[0:n, k, t * P:(t + 1) * P], ident[0:n, 0:n])
                e.then_inc(sem["w_transposed"], 1)

            def product(i, k, first=False):
                n = width(i)
                pe.wait_ge(sem["w_low"], 2 * i + k + 1)
                for half in range(2):
                    if not first:
                        pe.wait_ge(sem["h_product" if k else "silu"], 2 * i + half - 1)
                    out = (UP if k else GATE)[half][0:n, :]
                    for t in range(KT):
                        e = products(nc, out, wT[:, k, :, t, 0:n], half_of(hsT[:, :, t], half), t == 0, t == KT - 1)
                    e.then_inc(sem["ff_product"], 1)

            def body(i, first=False):
                n = width(i)
                w_transposes(i, 1, first)
                pe.wait_ge(sem["wd_loaded"], 16 * i + 16)
                if not first:
                    pe.wait_ge(sem["wd_low"], i)
                for t in range(KT):
                    e = nc.tensor.transpose(TD[0:n, t * P:(t + 1) * P], rawd[:, t, 0:n], ident[:])
                e.then_inc(sem["wd_transposed"], 1)
                product(i, 0, first)
                if not (isinstance(i, int) and i == FT - 1):
                    w_transposes(i + 1, 0)
                product(i, 1, first)

            w_transposes(0, 0, first=True)
            body(0, first=True)
            with pe.Fori(1, FT - 2) as i:
                body(i)
            body(FT - 2)
            body(FT - 1)
            pe.wait_ge(sem["wd_low"], FT)
            pe.wait_ge(sem["h_low"], 2 * FT)
            for b in range(SEQS):
                if b >= 2:
                    pe.wait_ge(sem["x3"], b - 1)
                for i in range(FT):
                    n = width(i)
                    e = products(nc, YB[b % 2][:], block_of(hT[0:n, :, i], b), wdT[0:n, :, i], i == 0, i == FT - 1)
                e.then_inc(sem["y3"], 1)


SEMAPHORES = """x_first rel_loaded head_of_row_loaded wkv1_loaded wq1_loaded x_rest pos_loaded wo1_loaded mask_loaded
ctx_loaded ctx_transposed ident_zero ident_ready exponent_ready ones_ready mv0 mv1 var_eps0 var_eps1 rstd0 rstd1
kv_copied scores1 kexp bias tables_loaded stats0 stats1 xn_transposed xn wk8 cap_filled exp1 biased1 max1 ctx_high
ctx_low pv1 rsum1 attn_transposed attn out1 x1 hs_transposed hs hs_high hs_low kv1 xnT q1 q_transposed q_copied qT
probs_transposed1 probsT1 attnT tables_transposed out_stored one_ready
piece_split piece_high piece_loaded0 piece_loaded1 rope_read rope_sum rope_high rope_low rinv2 probs2 projected out2
scores2 masked2 max2 exp2 v_high v_low x2 outT_high outT_low probsT_high probsT_low probs_transposed2 pv2
exponent3_ready mv2 stats2 var_eps2 rstd2 hs2 hs2_transposed hs2_high hs2_low wg_loaded wu_loaded wd_loaded
w_transposed w_high w_low wd_transposed wd_high wd_low ff_product silu h_product h_high h_low y3 x3""".split()


def program(nc, io):
    with ExitStack() as stack:
        def sb(name, shape, dt=F32):
            return stack.enter_context(nc.sbuf_tensor(name, shape, dt))

        sem = {name: stack.enter_context(nc.semaphore(name)) for name in SEMAPHORES}
        ps = [stack.enter_context(nc.psum_tensor(f"bank{i}", [P, 512], F32)) for i in range(8)]
        m = {
            "x": sb("x", [P, SEQS, DM]),
            "ident": sb("ident", [P, P]),
            "hsT_hl": sb("hsT_hl", [P, 2, KT, TOK], F32R),
        }
        with ExitStack() as attention:
            def asb(name, shape, dt=F32):
                return attention.enter_context(nc.sbuf_tensor(name, shape, dt))

            m["ctxT_hl"] = asb("ctxT_hl", [P, 2, KT, TOK], F32R)
            m["cosT"] = asb("cosT", [P, TOK])
            m["sinT"] = asb("sinT", [P, TOK])
            m["cap"] = asb("cap", [P, SEQS, P])
            m["one"] = asb("one", [P, 1])
            m["wqkv_hl"] = asb("cross_wqkv_hl", [P, PIECES, 2, KT, P], F32R)
            m["stage"] = asb("weights_staged", [P, 2, DM])
            self_attention(nc, m, sem, ps, io)
            cross_attention(nc, m, sem, ps, io)
        feed_forward(nc, m, sem, ps, io)


def constant_tables():
    import numpy as np

    i = np.arange(P)
    rel = (i[None, :] - i[:, None]).astype(np.float32)
    rel[i[None, :] > i[:, None]] = -1.0e30
    own = (i[:, None] // HD1 == np.arange(8)[None, :]).astype(np.float32) * np.float32(SCALE1)
    inv = (1.0 / np.float32(10000.0) ** (np.arange(0, D2, 2, dtype=np.float32) / np.float32(D2))).astype(np.float32)
    angle = np.arange(MAX_POS, dtype=np.float32)[:, None] * inv[None, :]
    cos, sin = np.cos(angle), np.sin(angle)
    rope = np.concatenate([cos, cos, -sin, sin], axis=1).astype(np.float32)
    return np.ascontiguousarray(np.concatenate([rel, own], axis=1)), rope


_INPUTS = {
    "x": "x", "ctx": "ctx_4096", "pos": "pos_BxS2", "mask": "mask_BxSxS2_ik0",
    "wq1": "L0_attn_Wq", "wkv1": "L0_attn_Wkv", "wo1": "L0_attn_Wo",
    "wq2": "L0_xattn_Wq", "wk2": "L0_xattn_Wk", "wv2": "L0_xattn_Wv", "wo2": "L0_xattn_Wo",
    "wg": "L0_ffn_W_gate", "wu": "L0_ffn_W_up", "wd": "L0_ffn_W_down",
}


def kernel(**inputs):
    import numpy as _np
    import concourse.bacc as _bacc
    from concourse import mybir as _mybir
    from concourse.bass_utils import run_bass_kernel_spmd as _run

    nc = _bacc.Bacc("TRN2", target_bir_lowering=False, num_devices=1)
    arrays, io = {}, {}
    constants, rope = constant_tables()
    given = {name: _np.ascontiguousarray(inputs[source]) for name, source in _INPUTS.items()}
    given["pos"] = _np.ascontiguousarray(given["pos"].T)
    for name, a in {**given, "constants": constants, "rope": rope}.items():
        arrays[f"in_{name}"] = a
        io[name] = nc.dram_tensor(f"in_{name}", a.shape, _mybir.dt.from_np(a.dtype), kind="ExternalInput").ap()
    io["out"] = nc.dram_tensor("out", (SEQS, P, DM), _mybir.dt.float32, kind="ExternalOutput").ap()
    program(nc, io)
    r = _run(nc, [arrays], core_ids=[0])
    return r.results[0]["out"]
```

```python
from contextlib import ExitStack

import concourse.bass as bass
from concourse import mybir

F32 = mybir.dt.float32
F32R = mybir.dt.float32r
I32 = mybir.dt.int32
ALU = mybir.AluOpType
ACT = mybir.ActivationFunctionType
AX = mybir.AxisListType

P = 128
SEQS = 8
DM = 512
KT = DM // P
HEADS = 32
HD1 = DM // HEADS
QUAD = 4
STEPS = HEADS // QUAD
D2 = 128
GROUPS = 8
HALF = SEQS // 2
HT = HALF * P
TOK = SEQS * P
FF = 1376
FT = (FF + P - 1) // P
FLAST = FF - (FT - 1) * P
MAX_POS = 512
EPS = 1e-5
SCALE1 = HD1 ** -0.5
SCALE2 = float(D2) ** -0.5
MASKED = -1.0e9
UNMASKED = 3.0e38


def alibi_slopes():
    start = 2.0 ** (-2.0 ** (-(5 - 3)))
    return [start ** (i + 1) for i in range(HEADS)]


def block_of(t, b, n=P):
    return t[..., bass.ds(b * n, n)]


def self_attention(nc, m, sem, ps, io):
    SC, TB, OB, G = ps[0:2], ps[2:4], ps[4:6], ps[6:8]
    x, hsT, ctxT = m["x"], m["hsT_hl"], m["ctxT_hl"]
    ident = m["ident"]
    with ExitStack() as stack:
        def sb(name, shape, dt=F32):
            return stack.enter_context(nc.sbuf_tensor(name, shape, dt))

        bias = sb("alibi_bias", [P, HEADS, P])
        rel = sb("relative_position", [P, P])
        head_of_row = sb("head_of_row", [P, 8])
        wq = sb("self_wq", [P, KT, DM])
        wo = sb("self_wo", [P, KT, DM])
        wkv = sb("self_wkv", [P, KT, 2 * HD1])
        wk8 = sb("self_wk_8_times", [P, KT, 8, HD1])
        stats = sb("self_stats", [P, 2, 6])
        mv = sb("x1_mean_var", [P, 2])
        rstd = sb("x1_rstd", [P, 2])
        mv0 = sb("x_mean_var", [P, SEQS, 2])
        rstd0 = sb("x_rstd", [P, 2, SEQS])
        exponent = sb("minus_half_and_eps", [P, 2])
        xn = sb("xn", [P, DM])
        xnT = sb("xnT", [P, KT, P])
        q_tok = sb("q_tok", [P, DM])
        qT = sb("self_qT", [P, KT, P])
        kT = sb("self_kT_8_times", [P, P])
        kexp = sb("self_k_by_head", [P, 2, 8, P])
        v = sb("self_v_and_ones", [P, SEQS, HD1 + 1])
        S = sb("self_scores", [P, 2, QUAD, P])
        PR = sb("self_probs", [P, 2, QUAD, P])
        negmax = sb("self_negmax", [P, 2, QUAD])
        PT = sb("self_probsT", [P, 2, QUAD, P])
        rsum = sb("self_rsum", [P, HEADS])
        attn = sb("self_attn", [P, DM])
        attnT = sb("self_attnT", [P, KT, P])
        hs = sb("self_hs", [P, DM])
        ctx_tok = sb("ctx_tok", [P, DM])
        tables = sb("rope_rows", [P, SEQS, 2 * D2])
        pos = sb("positions", [P, SEQS], I32)
        mask = sb("mask", [P, SEQS, P], I32)
        unmasked = sb("unmasked", [P, P])

        slopes = alibi_slopes()
        block = stack.enter_context(nc.Block())

        @block.sync
        def _(sp):
            sp.dma_start(x[:, 0, :], io["x"][0]).then_inc(sem["x_first"], 16)
            sp.dma_start(rel[:], io["constants"][:, 0:P]).then_inc(sem["rel_loaded"], 16)
            sp.dma_start(head_of_row[:], io["constants"][:, P:P + 8]).then_inc(sem["head_of_row_loaded"], 16)
            sp.dma_start(wkv[:], io["wkv1"].rearrange("(t p) n -> p t n", p=P)).then_inc(sem["wkv1_loaded"], 16)
            sp.dma_start(wq[:], io["wq1"].rearrange("(t p) n -> p t n", p=P)).then_inc(sem["wq1_loaded"], 16)
            sp.dma_start(x[:, 1:SEQS, :], io["x"][1:SEQS].rearrange("b p d -> p b d")).then_inc(sem["x_rest"], 16)
            sp.dma_start(pos[:], io["pos"]).then_inc(sem["pos_loaded"], 16)
            sp.dma_start(wo[:], io["wo1"].rearrange("(t p) n -> p t n", p=P)).then_inc(sem["wo1_loaded"], 16)
            sp.dma_start(mask[:], io["mask"].rearrange("b q k -> q b k")).then_inc(sem["mask_loaded"], 16)

            def load_ctx(b):
                sp.dma_start(ctx_tok[:], io["ctx"][bass.ds(b, 1)].rearrange("b p d -> p (b d)")).then_inc(sem["ctx_loaded"], 16)

            load_ctx(0)
            with sp.Fori(1, SEQS) as b:
                sp.wait_ge(sem["ctx_transposed"], b)
                load_ctx(b)
            for j in range(PIECES):
                load_piece(sp, m, sem, j, j % 2, piece_source(io, j, 0), first=j < 2)

        @block.gpsimd
        def _(pool):
            nc.gpsimd.memset(ident[:], 0.0).then_inc(sem["ident_zero"], 1)
            pool.wait_ge(sem["ident_zero"], 1)
            nc.gpsimd.affine_select(out=ident[:], in_=ident[:], compare_op=ALU.not_equal, fill=1.0, base=0,
                                    pattern=[[-1, P]], channel_multiplier=1).then_inc(sem["ident_ready"], 1)
            nc.gpsimd.memset(exponent[:, 0:1], -0.5).then_inc(sem["exponent_ready"], 1)
            nc.gpsimd.memset(exponent[:, 1:2], EPS).then_inc(sem["exponent_ready"], 1)
            nc.gpsimd.memset(v[:], 1.0).then_inc(sem["ones_ready"], 1)

            def rstd_of_x(first, last):
                n = last - first
                pool.wait_ge(sem["mv0"], last)
                nc.gpsimd.tensor_tensor(rstd0[:, 0, first:last], mv0[:, first:last, 1], exponent[:, 1:2].to_broadcast([P, n]), ALU.add).then_inc(sem["var_eps0"], 1)
                pool.wait_ge(sem["var_eps0"], 1 if first == 0 else 2)
                nc.gpsimd.tensor_tensor(rstd0[:, 1, first:last], rstd0[:, 0, first:last], exponent[:, 0:1].to_broadcast([P, n]), ALU.pow).then_inc(sem["rstd0"], 1)

            def rstd_of_x1(b):
                pool.wait_ge(sem["mv1"], b + 1)
                nc.gpsimd.tensor_tensor(rstd[:, 0:1], mv[:, 1:2], exponent[:, 1:2], ALU.add).then_inc(sem["var_eps1"], 1)
                pool.wait_ge(sem["var_eps1"], b + 1)
                nc.gpsimd.tensor_tensor(rstd[:, 1:2], rstd[:, 0:1], exponent[:, 0:1], ALU.pow).then_inc(sem["rstd1"], 1)

            def keys_by_head(c):
                pool.wait_ge(sem["kv_copied"], c + 1)
                if not (isinstance(c, int) and c < 2):
                    pool.wait_ge(sem["scores1"], STEPS * (c - 1))
                nc.gpsimd.tensor_tensor(kexp[:, bass.ds(c % 2, 1)].rearrange("p s h k -> p (s h) k"), kT[:].unsqueeze(1).to_broadcast([P, 8, P]),
                                        head_of_row[:].unsqueeze(2).to_broadcast([P, 8, P]), ALU.mult).then_inc(sem["kexp"], 1)

            pool.wait_ge(sem["exponent_ready"], 2)
            rstd_of_x(0, 1)
            pool.wait_ge(sem["rel_loaded"], 16)
            for h in range(HEADS):
                nc.gpsimd.tensor_scalar(bias[:, h, :], rel[:], slopes[h], None, ALU.mult).then_inc(sem["bias"], 1)
                if h == QUAD - 1:
                    pool.wait_ge(sem["head_of_row_loaded"], 16)
                    keys_by_head(0)
                    rstd_of_x(1, SEQS)
            pool.wait_ge(sem["pos_loaded"], 16)
            for b in range(SEQS):
                nc.gpsimd.indirect_dma_start(
                    tables[:, b, :], None, io["rope"], bass.IndirectOffsetOnAxis(ap=pos[:, b:b + 1].bitcast(mybir.dt.uint32), axis=0),
                ).then_inc(sem["tables_loaded"], 16)

            def body(b, front, back):
                if back:
                    rstd_of_x1(b - 1)
                if front:
                    keys_by_head(b + 1)

            body(0, True, False)
            body(1, True, True)
            with pool.Fori(2, SEQS - 1) as b:
                body(b, True, True)
            body(SEQS - 1, False, True)
            body(SEQS, False, True)
            for j in range(PIECES):
                piece_low(nc, pool, m, sem, j % 2, j, m["wqkv_hl"][:, j])

        @block.vector
        def _(dve):
            def stats_of_x(b):
                if b > 0:
                    dve.wait_ge(sem["mv0"], b)
                nc.vector.bn_stats(stats[:, 0, :], x[:, b, :]).then_inc(sem["stats0"], 1)
                dve.wait_ge(sem["stats0"], b + 1)
                nc.vector.bn_aggr(mv0[:, b, :], stats[:, 0, :]).then_inc(sem["mv0"], 1)

            def xn_of(c, first=False):
                dve.wait_ge(sem["rstd0"], 1 if first else 2)
                if not first:
                    dve.wait_ge(sem["xn_transposed"], c)
                nc.vector.tensor_scalar(xn[:].unsqueeze(1), x[:, bass.ds(c, 1), :], mv0[:, bass.ds(c, 1), 0], rstd0[:, 1, bass.ds(c, 1)],
                                        ALU.subtract, ALU.mult).then_inc(sem["xn"], 1)

            dve.wait_ge(sem["x_first"], 16)
            stats_of_x(0)
            dve.wait_ge(sem["wkv1_loaded"], 16)
            nc.vector.tensor_copy(wk8[:], wkv[:, :, 0:HD1].unsqueeze(2).to_broadcast([P, KT, 8, HD1])).then_inc(sem["wk8"], 1)
            xn_of(0, first=True)
            nc.vector.memset(m["cap"][:], MASKED).then_inc(sem["cap_filled"], 1)
            nc.vector.memset(unmasked[:], UNMASKED).then_inc(sem["cap_filled"], 1)
            dve.wait_ge(sem["x_rest"], 16)
            for b in range(1, SEQS):
                stats_of_x(b)

            def normalise(b, i):
                o = OB[i][:, 0:16 * (HD1 + 1)].rearrange("p (h d) -> p h d", h=16)
                earlier = not (isinstance(b, int) and b == 0)
                dve.wait_ge(sem["pv1"], STEPS * b + HALF * (i + 1))
                if earlier:
                    dve.wait_ge(sem["attn"], 2 * b - 1 + i)
                nc.vector.reciprocal(rsum[:, 16 * i:16 * i + 16].unsqueeze(2), o[:, :, HD1:HD1 + 1]).then_inc(sem["rsum1"], 1)
                dve.wait_ge(sem["rsum1"], 2 * b + i + 1)
                if earlier:
                    dve.wait_ge(sem["attn_transposed"], b)
                nc.vector.tensor_tensor(attn[:].rearrange("p (i h d) -> p i h d", i=2, h=16)[:, i], o[:, :, 0:HD1],
                                        rsum[:, 16 * i:16 * i + 16].unsqueeze(2).to_broadcast([P, 16, HD1]),
                                        ALU.mult).then_inc(sem["attn"], 1)

            def hs_low(p):
                dve.wait_ge(sem["hs_high"], p + 1)
                nc.vector.tensor_tensor(block_of(hsT[:, 1], p), G[0][:].rearrange("p (t k) -> p t k", t=KT),
                                        block_of(hsT[:, 0], p).bitcast(F32), ALU.subtract).then_inc(sem["hs_low"], 1)

            def body(b, scores, front, back, first=False):
                for s in range(STEPS if scores or back else 0):
                    n = STEPS * b + s
                    if s == 3 and back:
                        normalise(b - 1, 1)
                    if scores:
                        dve.wait_ge(sem["scores1"], n + 1)
                        if not first or s >= 2:
                            dve.wait_ge(sem["exp1"], n - 1)
                        if first:
                            dve.wait_ge(sem["bias"], QUAD * (s + 1))
                        nc.vector.tensor_tensor(S[:, s % 2], SC[s % 2][:].rearrange("p (h k) -> p h k", h=QUAD),
                                                bias[:, QUAD * s:QUAD * s + QUAD, :], ALU.add).then_inc(sem["biased1"], 1)
                        dve.wait_ge(sem["biased1"], n + 1)
                        nc.vector.tensor_reduce(negmax[:, s % 2, :], S[:, s % 2], AX.X, ALU.max, negate=True).then_inc(sem["max1"], 1)
                    if s == 0 and scores:
                        dve.wait_ge(sem["ctx_high"], b + 1)
                        nc.vector.tensor_tensor(block_of(ctxT[:, 1], b), G[1][:].rearrange("p (t k) -> p t k", t=KT),
                                                block_of(ctxT[:, 0], b).bitcast(F32), ALU.subtract).then_inc(sem["ctx_low"], 1)
                    if s == 1 and front:
                        xn_of(b + 1)
                    if s == 7 and scores:
                        normalise(b, 0)
                    if s == 1 and not (isinstance(b, int) and b < 2):
                        hs_low(b - 2)
                    if s == 6 and back:
                        dve.wait_ge(sem["out1"], b)
                        if not (isinstance(b, int) and b == 1):
                            dve.wait_ge(sem["hs"], b - 1)
                        nc.vector.tensor_tensor(x[:, bass.ds(b - 1, 1), :], x[:, bass.ds(b - 1, 1), :], G[0][:].unsqueeze(1),
                                                ALU.add).then_inc(sem["x1"], 1)
                        dve.wait_ge(sem["x_first"], 16)
                        dve.wait_ge(sem["x1"], b)
                        nc.vector.bn_stats(stats[:, 1, :].unsqueeze(1), x[:, bass.ds(b - 1, 1), :]).then_inc(sem["stats1"], 1)
                        dve.wait_ge(sem["x_first"], 16)
                        dve.wait_ge(sem["stats1"], b)
                        nc.vector.bn_aggr(mv[:], stats[:, 1, :]).then_inc(sem["mv1"], 1)
                    if s == 7 and back:
                        dve.wait_ge(sem["rstd1"], b)
                        if not (isinstance(b, int) and b == 1):
                            dve.wait_ge(sem["hs_transposed"], b - 1)
                        nc.vector.tensor_scalar(hs[:].unsqueeze(1), x[:, bass.ds(b - 1, 1), :], mv[:, 0:1], rstd[:, 1:2],
                                                ALU.subtract, ALU.mult).then_inc(sem["hs"], 1)

            body(0, True, True, False, first=True)
            dve.wait_ge(sem["mask_loaded"], 16)
            dve.wait_ge(sem["cap_filled"], 2)
            for b in range(SEQS):
                nc.vector.copy_predicated(m["cap"][:, b, :], mask[:, b, :], unmasked[:])
            body(1, True, True, True)
            with dve.Fori(2, SEQS - 1) as b:
                body(b, True, True, True)
            body(SEQS - 1, True, False, True)
            body(SEQS, False, False, True)
            hs_low(SEQS - 1)

        @block.scalar
        def _(act):
            def copy_xnT(c, first=False):
                act.wait_ge(sem["xn_transposed"], c + 1)
                if not first:
                    act.wait_ge(sem["kv1"], c)
                nc.scalar.copy(xnT[:], G[0][:].rearrange("p (t k) -> p t k", t=KT)).then_inc(sem["xnT"], 1)

            def copy_q(c, first=False):
                act.wait_ge(sem["q1"], c + 1)
                if not first:
                    act.wait_ge(sem["q_transposed"], c)
                nc.scalar.copy(q_tok[:], G[1][:]).then_inc(sem["q_copied"], 1)

            def copy_kv(c, first=False):
                act.wait_ge(sem["kv1"], c + 1)
                if first:
                    act.wait_ge(sem["ones_ready"], 1)
                else:
                    act.wait_ge(sem["kexp"], c)
                nc.scalar.copy(v[:, bass.ds(c, 1), 0:HD1], G[0][:, P:P + HD1].unsqueeze(1))
                nc.scalar.copy(kT[:], G[0][:, 0:P]).then_inc(sem["kv_copied"], 1)

            def copy_qT(c, first=False):
                act.wait_ge(sem["q_transposed"], c + 1)
                if not first:
                    act.wait_ge(sem["scores1"], STEPS * c)
                nc.scalar.copy(qT[:], G[1][:].rearrange("p (t k) -> p t k", t=KT)).then_inc(sem["qT"], 1)

            copy_xnT(0, first=True)
            copy_q(0, first=True)
            copy_kv(0, first=True)
            copy_qT(0, first=True)

            def hs_high(p):
                act.wait_ge(sem["hs_transposed"], p + 1)
                nc.scalar.copy(block_of(hsT[:, 0], p), G[0][:].rearrange("p (t k) -> p t k", t=KT)).then_inc(sem["hs_high"], 1)

            def body(b, scores, front, back, first=False):
                for s in range(STEPS):
                    n = STEPS * b + s
                    if s == 7 and front:
                        copy_qT(b + 1)
                    if (not first or s >= 2) and (scores or s < 2):
                        act.wait_ge(sem["probs_transposed1"], n - 1)
                        if not first or s >= 4:
                            act.wait_ge(sem["pv1"], n - 3)
                        nc.scalar.copy(PT[:, s % 2], TB[s % 2][:].rearrange("p (h k) -> p h k", h=QUAD)).then_inc(sem["probsT1"], 1)
                    if scores:
                        act.wait_ge(sem["max1"], n + 1)
                        if not first or s >= 2:
                            act.wait_ge(sem["probs_transposed1"], n - 1)
                        for j in range(QUAD):
                            e = nc.scalar.activation(PR[:, s % 2, j, :], S[:, s % 2, j, :], ACT.Exp, bias=negmax[:, s % 2, j:j + 1])
                        e.then_inc(sem["exp1"], 1)
                    if s == 0 and scores:
                        act.wait_ge(sem["ctx_transposed"], b + 1)
                        nc.scalar.copy(block_of(ctxT[:, 0], b), G[1][:].rearrange("p (t k) -> p t k", t=KT)).then_inc(sem["ctx_high"], 1)
                    if s == 2 and front:
                        copy_xnT(b + 1)
                    if s == 3 and front:
                        copy_q(b + 1)
                    if s == 4 and front:
                        copy_kv(b + 1)
                    if s == 4 and back:
                        act.wait_ge(sem["attn_transposed"], b)
                        if not (isinstance(b, int) and b == 1):
                            act.wait_ge(sem["out1"], b - 1)
                        nc.scalar.copy(attnT[:], G[1][:].rearrange("p (t k) -> p t k", t=KT)).then_inc(sem["attnT"], 1)
                    if s == 1 and not (isinstance(b, int) and b < 2):
                        hs_high(b - 2)
                    if s == 3 and not scores:
                        for i in range(HALF):
                            act.wait_ge(sem["tables_transposed"], i + 1)
                            t = ps[i][:].rearrange("p (b w k) -> p w b k", b=2, w=2)
                            nc.scalar.copy(m["cosT"][:, 2 * i * P:2 * (i + 1) * P].rearrange("p (b k) -> p b k", b=2), t[:, 0])
                            nc.scalar.copy(m["sinT"][:, 2 * i * P:2 * (i + 1) * P].rearrange("p (b k) -> p b k", b=2), t[:, 1])

            body(0, True, True, False, first=True)
            body(1, True, True, True)
            with act.Fori(2, SEQS - 1) as b:
                body(b, True, True, True)
            body(SEQS - 1, True, False, True)
            body(SEQS, False, False, True)
            for j in range(PIECES):
                piece_high(nc, act, m, sem, j % 2, j // 2 + 1, m["wqkv_hl"][:, j])
            hs_high(SEQS - 1)

        @block.tensor
        def _(pe):
            def transpose4(bank, src, done):
                for t in range(KT):
                    i = nc.tensor.transpose(bank[:, t * P:(t + 1) * P], src[:, t * P:(t + 1) * P], ident[:])
                i.then_inc(sem[done], 1)

            def xn_transposes(c):
                pe.wait_ge(sem["xn"], c + 1)
                transpose4(G[0], xn, "xn_transposed")

            def q_product(c):
                pe.wait_ge(sem["xnT"], c + 1)
                for t in range(KT):
                    i = nc.tensor.matmul(G[1][:], xnT[:, t, :], wq[:, t, :], start=(t == 0), stop=(t == KT - 1))
                i.then_inc(sem["q1"], 1)

            def kv_product(c):
                for t in range(KT):
                    nc.tensor.matmul(G[0][:, 0:P], wk8[:, t].rearrange("p r d -> p (r d)"), xnT[:, t, :], start=(t == 0), stop=(t == KT - 1))
                for t in range(KT):
                    i = nc.tensor.matmul(G[0][:, P:P + HD1], xnT[:, t, :], wkv[:, t, HD1:2 * HD1], start=(t == 0), stop=(t == KT - 1))
                i.then_inc(sem["kv1"], 1)

            def q_transposes(c):
                pe.wait_ge(sem["q_copied"], c + 1)
                transpose4(G[1], q_tok, "q_transposed")

            def hs_transposes(p):
                pe.wait_ge(sem["hs"], p + 1)
                transpose4(G[0], hs, "hs_transposed")

            pe.wait_ge(sem["ident_ready"], 1)
            xn_transposes(0)
            pe.wait_ge(sem["wq1_loaded"], 16)
            q_product(0)
            pe.wait_ge(sem["wk8"], 1)
            kv_product(0)
            q_transposes(0)
            pe.wait_ge(sem["wo1_loaded"], 16)

            def body(b, scores, front, back, first=False):
                for s in range(STEPS):
                    n = STEPS * b + s
                    if scores:
                        if s == 0:
                            pe.wait_ge(sem["qT"], b + 1)
                            pe.wait_ge(sem["kexp"], b + 1)
                        if not first or s >= 2:
                            pe.wait_ge(sem["biased1"], n - 1)
                        keys = kexp[:, bass.ds(b % 2, 1), QUAD * (s % 2):QUAD * (s % 2) + QUAD, :].rearrange("p s h k -> p (s h k)")
                        nc.tensor.matmul(SC[s % 2][:], qT[:, s // 2, :], keys, start=True, stop=True).then_inc(sem["scores1"], 1)
                    if s == 7 and front:
                        if first:
                            pe.wait_ge(sem["q_copied"], b + 2)
                        else:
                            pe.wait_ge(sem["attnT"], b)
                        q_transposes(b + 1)
                    if (not first or s >= 2) and (scores or s < 2):
                        pe.wait_ge(sem["exp1"], n - 1)
                        if not first or s >= 4:
                            pe.wait_ge(sem["probsT1"], n - 3)
                        for j in range(QUAD):
                            i = nc.tensor.transpose(TB[s % 2][:, j * P:(j + 1) * P], PR[:, s % 2, j, :], ident[:])
                        i.then_inc(sem["probs_transposed1"], 1)
                    if (not first or s >= 3) and (scores or s < 3):
                        r = (s - 3) % STEPS
                        owner = b if s >= 3 else b - 1
                        pe.wait_ge(sem["probsT1"], n - 2)
                        if r % HALF == 0 and not (isinstance(owner, int) and owner == 0):
                            pe.wait_ge(sem["attn"], 2 * owner - 1 + r // HALF)
                        for j in range(QUAD):
                            c = (QUAD * (r % HALF) + j) * (HD1 + 1)
                            i = nc.tensor.matmul(OB[r // HALF][:, c:c + HD1 + 1], PT[:, r % 2, j, :], v[:, bass.ds(owner, 1), :].rearrange("p b d -> p (b d)"),
                                                 start=True, stop=True)
                        i.then_inc(sem["pv1"], 1)
                    if s == 0 and scores:
                        pe.wait_ge(sem["ctx_loaded"], 16 * b + 16)
                        transpose4(G[1], ctx_tok, "ctx_transposed")
                    if s == 2 and front:
                        pe.wait_ge(sem["kv_copied"], b + 1)
                        if not (isinstance(b, int) and b < 2):
                            pe.wait_ge(sem["hs_low"], b - 1)
                        xn_transposes(b + 1)
                    if s == 3 and front:
                        pe.wait_ge(sem["ctx_low"], b + 1)
                        q_product(b + 1)
                    if s == 4 and front:
                        kv_product(b + 1)
                    if s == 4 and back:
                        if front:
                            pe.wait_ge(sem["q_copied"], b + 2)
                        elif scores:
                            pe.wait_ge(sem["ctx_low"], b + 1)
                        pe.wait_ge(sem["attn"], 2 * b)
                        transpose4(G[1], attn, "attn_transposed")
                    if s == 5 and back:
                        if front:
                            pe.wait_ge(sem["kv_copied"], b + 2)
                        else:
                            pe.wait_ge(sem["hs_low"], b - 1)
                        pe.wait_ge(sem["attnT"], b)
                        for t in range(KT):
                            i = nc.tensor.matmul(G[0][:], attnT[:, t, :], wo[:, t, :], start=(t == 0), stop=(t == KT - 1))
                        i.then_inc(sem["out1"], 1)
                    if s == 1 and not (isinstance(b, int) and b < 2):
                        hs_transposes(b - 2)
                    if s == 3 and not scores:
                        pe.wait_ge(sem["tables_loaded"], 16 * SEQS)
                        pe.wait_ge(sem["biased1"], STEPS * SEQS)
                        pe.wait_ge(sem["probsT1"], STEPS * SEQS)
                        for i in range(HALF):
                            for k in range(2):
                                for w in range(2):
                                    t = nc.tensor.transpose(ps[i][:, (2 * k + w) * P:(2 * k + w + 1) * P], tables[:, 2 * i + k, w * P:(w + 1) * P], ident[:])
                            t.then_inc(sem["tables_transposed"], 1)

            body(0, True, True, False, first=True)
            body(1, True, True, True)
            with pe.Fori(2, SEQS - 1) as b:
                body(b, True, True, True)
            body(SEQS - 1, True, False, True)
            body(SEQS, False, False, True)
            hs_transposes(SEQS - 1)


PIECES = 6
PIECE_TURN = [0, 1, 2, 7, 8, 9]
WO_TURN = 3
TURNS = 10


def piece_source(io, j, g):
    name, at = ("wk2", g) if j == 0 else ("wv2", g) if j == PIECES - 1 else ("wq2", g * QUAD + (j - 1))
    return io[name].rearrange("(t p) n -> p t n", p=P)[:, :, bass.ds(at * P, P)]


def load_piece(sp, m, sem, turn, slot, source, first=False):
    if not first:
        sp.wait_ge(sem["piece_split"], turn - 1)
    dst = m["stage"][:, slot, :]
    if len(source.shape) == 3:
        dst = dst.rearrange("p (t n) -> p t n", t=KT)
    sp.dma_start(dst, source).then_inc(sem[f"piece_loaded{slot}"], 16)


def piece_high(nc, act, m, sem, slot, loads, dst):
    src = m["stage"][:, slot, :]
    if len(dst.shape) == 4:
        src = src.rearrange("p (t n) -> p t n", t=KT)
    act.wait_ge(sem[f"piece_loaded{slot}"], 16 * loads)
    nc.scalar.copy(dst[:, 0], src).then_inc(sem["piece_high"], 1)


def piece_low(nc, pool, m, sem, slot, turn, dst):
    src = m["stage"][:, slot, :]
    if len(dst.shape) == 4:
        src = src.rearrange("p (t n) -> p t n", t=KT)
    pool.wait_ge(sem["piece_high"], turn + 1)
    nc.gpsimd.tensor_tensor(dst[:, 1], src, dst[:, 0].bitcast(F32), ALU.subtract).then_inc(sem["piece_split"], 1)


def products(nc, out, stationary, moving, first, last):
    for k, (a, b) in enumerate(((0, 0), (0, 1), (1, 0))):
        i = nc.tensor.matmul(out, stationary[:, a], moving[:, b], start=(first and k == 0), stop=(last and k == 2))
    return i


def half_of(t, half):
    return t[..., half * HT:(half + 1) * HT]


def cross_attention(nc, m, sem, ps, io):
    PB, SC, TB, OB, YB = ps[0:2], ps[2:4], ps[4:6], ps[6], ps[7]
    x, hsT, ctxT, cap, ident, w = m["x"], m["hsT_hl"], m["ctxT_hl"], m["cap"], m["ident"], m["wqkv_hl"]
    with ExitStack() as stack:
        def sb(name, shape, dt=F32):
            return stack.enter_context(nc.sbuf_tensor(name, shape, dt))

        wo = sb("cross_wo_hl", [P, 2, QUAD, DM], F32R)
        qT = sb("cross_qT_hl", [P, 2, QUAD, TOK], F32R)
        kT = sb("cross_kT_hl", [P, 2, TOK], F32R)
        v = sb("cross_v_hl", [P, 2, SEQS, D2], F32R)
        rot = sb("rotated", [P, 2, HT])
        cross = sb("rotated_other_half", [P, HT])
        S = sb("cross_scores", [P, 2, QUAD, P])
        negmax = sb("cross_negmax", [P, 2, QUAD])
        rowsum = sb("cross_rowsum", [P, 2, QUAD])
        rinv = sb("cross_rinv", [P, 2, QUAD])
        PT = sb("cross_probsT_hl", [P, 2, QUAD * P], F32R)
        oT = sb("cross_outT_hl", [P, 2, 2, QUAD * P], F32R)
        block = stack.enter_context(nc.Block())

        def blocks_in(b):
            pairs = {0: (0, 1), 1: (2, 3), 2: (4, 5)}
            return [(j, 1, 0) for j in pairs.get(b, ())] + [(j, 0, 1) for j in pairs.get(b - 4, ())]

        def turns_in(b, last):
            own = {1: [(0, 1, 0), (1, 1, 1), (2, 1, 2)],
                   2: [(PIECES, 0, WO_TURN), (PIECES + 1, 0, WO_TURN + 1)],
                   3: [(PIECES + 2, 0, WO_TURN + 2), (PIECES + 3, 0, WO_TURN + 3)],
                   4: [(3, 1, 7), (4, 1, 8)],
                   5: [(5, 1, 9)]}.get(b, [])
            return [(which, 0, t - WO_TURN) for which, ahead, t in own if not ahead] if last else own

        def outputs_in(b, first, tail):
            before, after = {0: ([-3], []), 1: ([-2], []), 2: ([-1], []), 3: ([], []), 4: ([0], []),
                             5: ([1], [2]), 6: ([3], []), 7: ([4], [])}[b]
            return [[y for y in ys if not (first and y < 0)] for ys in (before, after)]

        @block.sync
        def _(sp):
            def body(g, last):
                for b in range(SEQS):
                    for which, ahead, t in turns_in(b, last):
                        if which < PIECES:
                            source = piece_source(io, which, g + 1)
                        else:
                            source = io["wo2"][bass.ds((g * QUAD + which - PIECES) * P, P), :]
                        load_piece(sp, m, sem, PIECES + TURNS * g + t, t % 2, source)

            with sp.Fori(0, GROUPS - 1) as g:
                body(g, False)
            body(GROUPS - 1, True)

        @block.gpsimd
        def _(pool):
            def rope_sum(rr, j, half):
                pool.wait_ge(sem["rope_read"], rr + 1)
                nc.gpsimd.tensor_tensor(rot[:, (half + j) % 2, :], rot[:, (half + j) % 2, :], cross[:], ALU.add).then_inc(sem["rope_sum"], 1)
                pool.wait_ge(sem["rope_high"], rr + 1)
                dst = kT if j == 0 else qT[:, :, j - 1]
                nc.gpsimd.tensor_tensor(half_of(dst[:, 1], half), rot[:, (half + j) % 2, :], half_of(dst[:, 0], half).bitcast(F32),
                                        ALU.subtract).then_inc(sem["rope_low"], 1)

            for j in range(PIECES - 1):
                rope_sum(j, j, 0)

            def body(g, first, last):
                for b in range(SEQS):
                    n = SEQS * g + b
                    for j, half, ahead in blocks_in(b):
                        if j < PIECES - 1 and not (ahead and last):
                            rope_sum(10 * (g + ahead) + 5 * half + j, j, half)
                    pool.wait_ge(sem["rinv2"], n + 1)
                    nc.gpsimd.tensor_tensor(S[:, b % 2], S[:, b % 2], rinv[:, b % 2, :].unsqueeze(2).to_broadcast([P, QUAD, P]), ALU.mult).then_inc(sem["probs2"], 1)
                    for which, ahead, t in turns_in(b, last):
                        dst = w[:, which] if which < PIECES else wo[:, :, which - PIECES]
                        piece_low(nc, pool, m, sem, t % 2, PIECES + TURNS * g + t, dst)

            body(0, True, False)
            with pool.Fori(1, GROUPS - 1) as g:
                body(g, False, False)
            body(GROUPS - 1, False, True)

        @block.vector
        def _(dve):
            def rope(g, half, j, first=False):
                rr = 10 * g + 5 * half + j
                pb = PB[j % 2]
                dve.wait_ge(sem["projected"], 12 * g + 6 * half + j + 1)
                if not first or j >= 2:
                    dve.wait_ge(sem["rope_low"], rr - 1)
                if not first and j == 0:
                    dve.wait_ge(sem["v_transposed"], 2 * g + half)
                if not first or j >= 1:
                    dve.wait_ge(sem["rope_sum"], rr)
                nc.vector.tensor_tensor(rot[:, (half + j) % 2, :], pb[:], half_of(m["cosT"][:], half), ALU.mult)
                nc.vector.tensor_tensor(cross[0:64, :], pb[64:128, :], half_of(m["sinT"][0:64, :], half), ALU.mult)
                nc.vector.tensor_tensor(cross[64:128, :], pb[0:64, :], half_of(m["sinT"][64:128, :], half), ALU.mult).then_inc(sem["rope_read"], 1)

            def v_low(g, half):
                dve.wait_ge(sem["v_high"], 2 * g + half + 1)
                nc.vector.tensor_tensor(v[:, 1, half * HALF:(half + 1) * HALF, :], PB[1][:].rearrange("p (b d) -> p b d", b=HALF),
                                        v[:, 0, half * HALF:(half + 1) * HALF, :].bitcast(F32), ALU.subtract).then_inc(sem["v_low"], 1)

            def add_output(g, y, first):
                dve.wait_ge(sem["out2"], SEQS * g + y + 1)
                if not (first and y == 0):
                    dve.wait_ge(sem["x2"], SEQS * g + y)
                nc.vector.tensor_tensor(x[:, y % SEQS, :], x[:, y % SEQS, :], YB[:], ALU.add).then_inc(sem["x2"], 1)

            for j in range(PIECES - 1):
                rope(0, 0, j, first=True)
            v_low(0, 0)

            def body(g, first, last, tail=False):
                for b in range(3 if tail else SEQS):
                    n = SEQS * g + b
                    blocks = [x for x in blocks_in(b) if not (x[2] and last)] if not tail else []
                    if not tail:
                        dve.wait_ge(sem["scores2"], n + 1)
                        if not first or b >= 2:
                            dve.wait_ge(sem["probs_transposed2"], n - 1)
                        nc.vector.scalar_tensor_tensor(out=S[:, b % 2], in0=SC[b % 2][:].rearrange("p (h k) -> p h k", h=QUAD), scalar=SCALE2,
                                                       in1=cap[:, b, :].unsqueeze(1).to_broadcast([P, QUAD, P]), op0=ALU.mult, op1=ALU.min).then_inc(sem["masked2"], 1)
                        dve.wait_ge(sem["masked2"], n + 1)
                        nc.vector.tensor_reduce(negmax[:, b % 2, :], S[:, b % 2], AX.X, ALU.max, negate=True).then_inc(sem["max2"], 1)
                    for j, half, ahead in blocks[:1]:
                        rope(g + ahead, half, j)
                    before, after = outputs_in(b, first, tail)
                    for y in before:
                        add_output(g, y, first)
                    for j, half, ahead in blocks[1:]:
                        if j < PIECES - 1:
                            rope(g + ahead, half, j)
                    for y in after:
                        add_output(g, y, first)
                    if not tail:
                        dve.wait_ge(sem["exp2"], n + 1)
                        nc.vector.reciprocal(rinv[:, b % 2, :], rowsum[:, b % 2, :]).then_inc(sem["rinv2"], 1)
                    if (not first or b >= 2) and (not tail or b < 2):
                        dve.wait_ge(sem["outT_high"], n - 1)
                        nc.vector.tensor_tensor(oT[:, b % 2, 1], OB[:], oT[:, b % 2, 0].bitcast(F32), ALU.subtract).then_inc(sem["outT_low"], 1)
                    if (not first or b >= 1) and (not tail or b < 1):
                        dve.wait_ge(sem["probsT_high"], n)
                        nc.vector.tensor_tensor(PT[:, 1], TB[(b - 1) % 2][:], PT[:, 0].bitcast(F32), ALU.subtract).then_inc(sem["probsT_low"], 1)
                    for j, half, ahead in blocks[1:]:
                        if j == PIECES - 1:
                            v_low(g + ahead, half)

            body(0, True, False)
            with dve.Fori(1, GROUPS - 1) as g:
                body(g, False, False)
            body(GROUPS - 1, False, True)
            body(GROUPS, False, True, tail=True)

        @block.scalar
        def _(act):
            def rope_high(g, half, j, first=False):
                act.wait_ge(sem["rope_sum"], 10 * g + 5 * half + j + 1)
                if not first:
                    act.wait_ge(sem["scores2"], SEQS * g if half else SEQS * g - HALF)
                dst = kT if j == 0 else qT[:, :, j - 1]
                nc.scalar.copy(half_of(dst[:, 0], half), rot[:, (half + j) % 2, :]).then_inc(sem["rope_high"], 1)

            def v_copy(g, half):
                act.wait_ge(sem["projected"], 12 * g + 6 * half + 6)
                act.wait_ge(sem["rope_low"], 10 * g + 5 * half + 4)
                nc.scalar.copy(rot[:, (half + 1) % 2, :], PB[1][:]).then_inc(sem["vT"], 1)

            def v_high(g, half, first=False):
                act.wait_ge(sem["v_transposed"], 2 * g + half + 1)
                if not first:
                    act.wait_ge(sem["pv2"], SEQS * g if half else SEQS * g - HALF)
                nc.scalar.copy(v[:, 0, half * HALF:(half + 1) * HALF, :], PB[1][:].rearrange("p (b d) -> p b d", b=HALF)).then_inc(sem["v_high"], 1)

            for j in range(PIECES - 1):
                rope_high(0, 0, j, first=True)
            v_copy(0, 0)
            v_high(0, 0, first=True)

            def body(g, first, last, tail=False):
                for b in range(2 if tail else SEQS):
                    n = SEQS * g + b
                    if not tail:
                        act.wait_ge(sem["max2"], n + 1)
                        for h in range(QUAD):
                            e = nc.scalar.activation(S[:, b % 2, h, :], S[:, b % 2, h, :], ACT.Exp, bias=negmax[:, b % 2, h:h + 1],
                                                     accum_out=rowsum[:, b % 2, h:h + 1])
                        e.then_inc(sem["exp2"], 1)
                        for j, half, ahead in blocks_in(b):
                            if ahead and last:
                                continue
                            if j < PIECES - 1:
                                rope_high(g + ahead, half, j, first=first and not ahead)
                            else:
                                v_copy(g + ahead, half)
                    if (not first or b >= 2) and (not tail or b < 2):
                        act.wait_ge(sem["pv2"], n - 1)
                        if not first or b >= 4:
                            act.wait_ge(sem["out2"], n - 3)
                        nc.scalar.copy(oT[:, b % 2, 0], OB[:]).then_inc(sem["outT_high"], 1)
                    if (not first or b >= 1) and (not tail or b < 1):
                        act.wait_ge(sem["probs_transposed2"], n)
                        if not first or b >= 2:
                            act.wait_ge(sem["pv2"], n - 1)
                        nc.scalar.copy(PT[:, 0], TB[(b - 1) % 2][:]).then_inc(sem["probsT_high"], 1)
                    if not tail:
                        for j, half, ahead in blocks_in(b):
                            if j == PIECES - 1 and not (ahead and last):
                                v_high(g + ahead, half, first=first and not ahead)
                    for which, ahead, t in turns_in(b, last) if not tail else ():
                        if which < PIECES:
                            act.wait_ge(sem["projected"], 12 * g + 6 + which + 1)
                            dst = w[:, which]
                        else:
                            if not first:
                                act.wait_ge(sem["out2"], SEQS * g)
                            dst = wo[:, :, which - PIECES]
                        piece_high(nc, act, m, sem, t % 2, PIECES // 2 + TURNS // 2 * g + t // 2 + 1, dst)

            body(0, True, False)
            with act.Fori(1, GROUPS - 1) as g:
                body(g, False, False)
            body(GROUPS - 1, False, True)
            body(GROUPS, False, True, tail=True)

        @block.tensor
        def _(pe):
            def project(g, half, j, first=False):
                rr = 10 * g + 5 * half + j
                if j == 0 and not first:
                    pe.wait_ge(sem["rope_read"], rr)
                elif j == 1 and not first:
                    pe.wait_ge(sem["v_low"], 2 * g + half)
                elif 2 <= j < PIECES - 1:
                    pe.wait_ge(sem["rope_read"], rr - 1)
                elif j == PIECES - 1:
                    pe.wait_ge(sem["rope_read"], rr - 1)
                if half == 0:
                    turn = j if isinstance(g, int) and g == 0 else PIECES + TURNS * (g - 1) + PIECE_TURN[j]
                    pe.wait_ge(sem["piece_split"], turn + 1)
                src = hsT if 0 < j < PIECES - 1 else ctxT
                for t in range(KT):
                    i = products(nc, PB[j % 2][:], w[:, j, :, t], half_of(src[:, :, t], half), t == 0, t == KT - 1)
                i.then_inc(sem["projected"], 1)

            def transpose_v(g, half):
                pe.wait_ge(sem["vT"], 2 * g + half + 1)
                for b in range(HALF):
                    i = nc.tensor.transpose(PB[1][:, b * P:(b + 1) * P], rot[:, (half + 1) % 2, b * P:(b + 1) * P], ident[:])
                i.then_inc(sem["v_transposed"], 1)

            def output(g, y, first, last):
                pe.wait_ge(sem["outT_low"], SEQS * g + y + 1)
                if not (first and y == 0):
                    pe.wait_ge(sem["x2"], SEQS * g + y)
                for h in range(QUAD):
                    if y == 0:
                        pe.wait_ge(sem["piece_split"], PIECES + TURNS * g + (0 if last else WO_TURN) + h + 1)
                    i = products(nc, YB[:], oT[:, y % 2, :, h * P:(h + 1) * P], wo[:, :, h], h == 0, h == QUAD - 1)
                i.then_inc(sem["out2"], 1)

            for j in range(PIECES):
                project(0, 0, j, first=True)
            transpose_v(0, 0)

            def body(g, first, last, tail=False):
                for b in range(3 if tail else SEQS):
                    n = SEQS * g + b
                    blocks = [x for x in blocks_in(b) if not (x[2] and last)] if not tail else []
                    if not tail:
                        if b % HALF == 0:
                            pe.wait_ge(sem["rope_low"], 10 * g + (10 if b else 5))
                        if not first or b >= 2:
                            pe.wait_ge(sem["masked2"], n - 1)
                        for h in range(QUAD):
                            i = products(nc, SC[b % 2][:, h * P:(h + 1) * P], qT[:, :, h, b * P:(b + 1) * P], kT[:, :, b * P:(b + 1) * P], True, True)
                        i.then_inc(sem["scores2"], 1)
                    for j, half, ahead in blocks[:1]:
                        project(g + ahead, half, j)
                    before, after = outputs_in(b, first, tail)
                    for y in before:
                        output(g, y, first, last)
                    for j, half, ahead in blocks[1:]:
                        project(g + ahead, half, j)
                    for y in after:
                        output(g, y, first, last)
                    if (not first or b >= 2) and (not tail or b < 2):
                        if b == 2:
                            pe.wait_ge(sem["v_low"], 2 * g + 1)
                        if b == 6:
                            pe.wait_ge(sem["v_low"], 2 * g + 2)
                        pe.wait_ge(sem["probsT_low"], n - 1)
                        if not first or b >= 3:
                            pe.wait_ge(sem["outT_low"], n - 2)
                        products(nc, OB[:], v[:, :, (b - 2) % SEQS, :], PT[:], True, True).then_inc(sem["pv2"], 1)
                    if (not first or b >= 1) and (not tail or b < 1):
                        pe.wait_ge(sem["probs2"], n)
                        if not first or b >= 3:
                            pe.wait_ge(sem["probsT_low"], n - 2)
                        for h in range(QUAD):
                            i = nc.tensor.transpose(TB[(b - 1) % 2][:, h * P:(h + 1) * P], S[:, (b - 1) % 2, h, :], ident[:])
                        i.then_inc(sem["probs_transposed2"], 1)
                    for j, half, ahead in blocks[1:]:
                        if j == PIECES - 1:
                            transpose_v(g + ahead, half)

            body(0, True, False)
            with pe.Fori(1, GROUPS - 1) as g:
                body(g, False, False)
            body(GROUPS - 1, False, True)
            body(GROUPS, False, True, tail=True)


def feed_forward(nc, m, sem, ps, io):
    GATE, UP, TW, TD, YB = ps[0:2], ps[2:4], ps[4:6], ps[6], [ps[7], ps[6]]
    x, hsT, ident = m["x"], m["hsT_hl"], m["ident"]
    with ExitStack() as stack:
        def sb(name, shape, dt=F32):
            return stack.enter_context(nc.sbuf_tensor(name, shape, dt))

        hT = sb("ff_hT_hl", [P, 2, FT, TOK], F32R)
        wdT = sb("ff_downT_hl", [P, 2, FT, DM], F32R)
        wT = sb("ff_gate_upT_hl", [P, 2, 2, KT, P], F32R)
        raw = sb("ff_gate_up_rows", [P, 2, DM])
        rawd = sb("ff_down_rows", [P, KT, P])
        tmp = sb("ff_work", [P, 4, DM])
        stats = sb("x2_stats", [P, 6])
        mv = sb("x2_mean_var", [P, SEQS, 2])
        rstd = sb("x2_rstd", [P, 2, SEQS])
        exponent = sb("minus_half_and_eps_again", [P, 2])
        block = stack.enter_context(nc.Block())

        def width(i):
            return FLAST if isinstance(i, int) and i == FT - 1 else P

        @block.sync
        def _(sp):
            def load(i, first=False):
                n = width(i)
                at = i * P if isinstance(i, int) else sp.snap(i * P)
                for k, name in enumerate(("wg", "wu")):
                    if not first:
                        sp.wait_ge(sem["w_transposed"], 2 * i + k - 1)
                    if not first and k == 1:
                        sp.wait_ge(sem["wd_transposed"], i)
                    sp.dma_start(raw[0:n, k, :], io[name][bass.ds(at, n), :]).then_inc(sem[f"{name}_loaded"], 16)
                sp.dma_start(rawd[:, :, 0:n], io["wd"].rearrange("(t p) f -> p t f", p=P)[:, :, bass.ds(at, n)]).then_inc(sem["wd_loaded"], 16)

            load(0, first=True)
            with sp.Fori(1, FT - 1) as i:
                load(i)
            load(FT - 1)
            for b in range(SEQS):
                sp.wait_ge(sem["x3"], b + 1)
                sp.dma_start(io["out"][b], x[:, b, :]).then_inc(sem["out_stored"], 16)
            sp.wait_ge(sem["out_stored"], 16 * SEQS)

        @block.gpsimd
        def _(pool):
            nc.gpsimd.memset(exponent[:, 0:1], -0.5).then_inc(sem["exponent3_ready"], 1)
            nc.gpsimd.memset(exponent[:, 1:2], EPS).then_inc(sem["exponent3_ready"], 1)
            pool.wait_ge(sem["exponent3_ready"], 2)
            pool.wait_ge(sem["mv2"], SEQS)
            nc.gpsimd.tensor_tensor(rstd[:, 0, :], mv[:, :, 1], exponent[:, 1:2].to_broadcast([P, SEQS]), ALU.add).then_inc(sem["var_eps2"], 1)
            pool.wait_ge(sem["var_eps2"], 1)
            nc.gpsimd.tensor_tensor(rstd[:, 1, :], rstd[:, 0, :], exponent[:, 0:1].to_broadcast([P, SEQS]), ALU.pow).then_inc(sem["rstd2"], 1)

            def h_low(i):
                n = width(i)
                for half in range(2):
                    pool.wait_ge(sem["h_high"], 2 * i + half + 1)
                    nc.gpsimd.tensor_tensor(half_of(hT[0:n, 1, bass.ds(i, 1), :], half), tmp[0:n, 2 + half:3 + half, :],
                                            half_of(hT[0:n, 0, bass.ds(i, 1), :], half).bitcast(F32), ALU.subtract).then_inc(sem["h_low"], 1)

            h_low(0)
            with pool.Fori(1, FT - 1) as i:
                h_low(i)
            h_low(FT - 1)

        @block.vector
        def _(dve):
            for b in range(SEQS):
                if b > 0:
                    dve.wait_ge(sem["mv2"], b)
                nc.vector.bn_stats(stats[:], x[:, b, :]).then_inc(sem["stats2"], 1)
                dve.wait_ge(sem["stats2"], b + 1)
                nc.vector.bn_aggr(mv[:, b, :], stats[:]).then_inc(sem["mv2"], 1)
            dve.wait_ge(sem["rstd2"], 1)
            for b in range(SEQS + 1):
                if b < SEQS:
                    if b >= 2:
                        dve.wait_ge(sem["hs2_transposed"], b - 1)
                    nc.vector.tensor_scalar(tmp[:, b % 2, :], x[:, b, :], mv[:, b, 0:1], rstd[:, 1, b:b + 1], ALU.subtract, ALU.mult).then_inc(sem["hs2"], 1)
                if b > 0:
                    dve.wait_ge(sem["hs2_high"], b)
                    nc.vector.tensor_tensor(block_of(hsT[:, 1], b - 1), TW[(b - 1) % 2][:].rearrange("p (t k) -> p t k", t=KT),
                                            block_of(hsT[:, 0], b - 1).bitcast(F32), ALU.subtract).then_inc(sem["hs2_low"], 1)

            def w_low(i, k):
                n = width(i)
                dve.wait_ge(sem["w_high"], 2 * i + k + 1)
                nc.vector.tensor_tensor(wT[:, k, 1, :, 0:n], TW[k][:].rearrange("p (t f) -> p t f", t=KT)[:, :, 0:n],
                                        wT[:, k, 0, :, 0:n].bitcast(F32), ALU.subtract).then_inc(sem["w_low"], 1)

            def body(i, first=False):
                n = width(i)
                w_low(i, 1)
                dve.wait_ge(sem["wd_high"], i + 1)
                nc.vector.tensor_tensor(wdT[0:n, 1, bass.ds(i, 1), :], TD[0:n, :].unsqueeze(1), wdT[0:n, 0, bass.ds(i, 1), :].bitcast(F32),
                                        ALU.subtract).then_inc(sem["wd_low"], 1)
                if not (isinstance(i, int) and i == FT - 1):
                    w_low(i + 1, 0)
                for half in range(2):
                    dve.wait_ge(sem["silu"], 2 * i + half + 1)
                    dve.wait_ge(sem["ff_product"], 4 * i + half + 3)
                    if not first:
                        dve.wait_ge(sem["h_low"], 2 * i + half - 1)
                    nc.vector.tensor_tensor(tmp[0:n, 2 + half, :], tmp[0:n, half, :], UP[half][0:n, :], ALU.mult).then_inc(sem["h_product"], 1)

            w_low(0, 0)
            body(0, first=True)
            with dve.Fori(1, FT - 2) as i:
                body(i)
            body(FT - 2)
            body(FT - 1)
            for b in range(SEQS):
                dve.wait_ge(sem["y3"], b + 1)
                nc.vector.tensor_tensor(x[:, b, :], x[:, b, :], YB[b % 2][:], ALU.add).then_inc(sem["x3"], 1)

        @block.scalar
        def _(act):
            for b in range(SEQS):
                act.wait_ge(sem["hs2_transposed"], b + 1)
                nc.scalar.copy(block_of(hsT[:, 0], b), TW[b % 2][:].rearrange("p (t k) -> p t k", t=KT)).then_inc(sem["hs2_high"], 1)

            def w_high(i, k, first=False):
                n = width(i)
                act.wait_ge(sem["w_transposed"], 2 * i + k + 1)
                if not first:
                    act.wait_ge(sem["ff_product"], 4 * i + 2 * k - 2)
                nc.scalar.copy(wT[:, k, 0, :, 0:n], TW[k][:].rearrange("p (t f) -> p t f", t=KT)[:, :, 0:n]).then_inc(sem["w_high"], 1)

            def body(i, first=False):
                n = width(i)
                w_high(i, 1, first)
                act.wait_ge(sem["wd_transposed"], i + 1)
                nc.scalar.copy(wdT[0:n, 0, bass.ds(i, 1), :], TD[0:n, :].unsqueeze(1)).then_inc(sem["wd_high"], 1)
                for half in range(2):
                    act.wait_ge(sem["ff_product"], 4 * i + half + 1)
                    if not first:
                        act.wait_ge(sem["h_product"], 2 * i + half - 1)
                    nc.scalar.activation(tmp[0:n, half, :], GATE[half][0:n, :], ACT.Silu).then_inc(sem["silu"], 1)
                if not (isinstance(i, int) and i == FT - 1):
                    w_high(i + 1, 0)
                for half in range(2):
                    act.wait_ge(sem["h_product"], 2 * i + half + 1)
                    nc.scalar.copy(half_of(hT[0:n, 0, bass.ds(i, 1), :], half), tmp[0:n, 2 + half:3 + half, :]).then_inc(sem["h_high"], 1)

            w_high(0, 0, first=True)
            body(0, first=True)
            with act.Fori(1, FT - 2) as i:
                body(i)
            body(FT - 2)
            body(FT - 1)

        @block.tensor
        def _(pe):
            for b in range(SEQS):
                pe.wait_ge(sem["hs2"], b + 1)
                if b >= 2:
                    pe.wait_ge(sem["hs2_low"], b - 1)
                for t in range(KT):
                    i = nc.tensor.transpose(TW[b % 2][:, t * P:(t + 1) * P], tmp[:, b % 2, t * P:(t + 1) * P], ident[:])
                i.then_inc(sem["hs2_transposed"], 1)

            def w_transposes(i, k, first=False):
                n = width(i)
                pe.wait_ge(sem["wg_loaded" if k == 0 else "wu_loaded"], 16 * i + 16)
                if first:
                    pe.wait_ge(sem["hs2_low"], SEQS)
                else:
                    pe.wait_ge(sem["w_low"], 2 * i + k - 1)
                for t in range(KT):
                    e = nc.tensor.transpose(TW[k][:, t * P:t * P + n], raw[0:n, k, t * P:(t + 1) * P], ident[0:n, 0:n])
                e.then_inc(sem["w_transposed"], 1)

            def product(i, k, first=False):
                n = width(i)
                pe.wait_ge(sem["w_low"], 2 * i + k + 1)
                for half in range(2):
                    if not first:
                        pe.wait_ge(sem["h_product" if k else "silu"], 2 * i + half - 1)
                    out = (UP if k else GATE)[half][0:n, :]
                    for t in range(KT):
                        e = products(nc, out, wT[:, k, :, t, 0:n], half_of(hsT[:, :, t], half), t == 0, t == KT - 1)
                    e.then_inc(sem["ff_product"], 1)

            def body(i, first=False):
                n = width(i)
                w_transposes(i, 1, first)
                pe.wait_ge(sem["wd_loaded"], 16 * i + 16)
                if not first:
                    pe.wait_ge(sem["wd_low"], i)
                for t in range(KT):
                    e = nc.tensor.transpose(TD[0:n, t * P:(t + 1) * P], rawd[:, t, 0:n], ident[:])
                e.then_inc(sem["wd_transposed"], 1)
                product(i, 0, first)
                if not (isinstance(i, int) and i == FT - 1):
                    w_transposes(i + 1, 0)
                product(i, 1, first)

            w_transposes(0, 0, first=True)
            body(0, first=True)
            with pe.Fori(1, FT - 2) as i:
                body(i)
            body(FT - 2)
            body(FT - 1)
            pe.wait_ge(sem["wd_low"], FT)
            pe.wait_ge(sem["h_low"], 2 * FT)
            for b in range(SEQS):
                if b >= 2:
                    pe.wait_ge(sem["x3"], b - 1)
                for i in range(FT):
                    n = width(i)
                    e = products(nc, YB[b % 2][:], block_of(hT[0:n, :, i], b), wdT[0:n, :, i], i == 0, i == FT - 1)
                e.then_inc(sem["y3"], 1)


SEMAPHORES = """x_first rel_loaded head_of_row_loaded wkv1_loaded wq1_loaded x_rest pos_loaded wo1_loaded mask_loaded
ctx_loaded ctx_transposed ident_zero ident_ready exponent_ready ones_ready mv0 mv1 var_eps0 var_eps1 rstd0 rstd1
kv_copied scores1 kexp bias tables_loaded stats0 stats1 xn_transposed xn wk8 cap_filled exp1 biased1 max1 ctx_high
ctx_low pv1 rsum1 attn_transposed attn out1 x1 hs_transposed hs hs_high hs_low kv1 xnT q1 q_transposed q_copied qT
probs_transposed1 probsT1 attnT tables_transposed out_stored
piece_split piece_high piece_loaded0 piece_loaded1 rope_read rope_sum rope_high rope_low rinv2 probs2 projected out2
scores2 masked2 max2 exp2 v_high v_low vT v_transposed x2 outT_high outT_low probsT_high probsT_low probs_transposed2 pv2
exponent3_ready mv2 stats2 var_eps2 rstd2 hs2 hs2_transposed hs2_high hs2_low wg_loaded wu_loaded wd_loaded
w_transposed w_high w_low wd_transposed wd_high wd_low ff_product silu h_product h_high h_low y3 x3""".split()


def program(nc, io):
    with ExitStack() as stack:
        def sb(name, shape, dt=F32):
            return stack.enter_context(nc.sbuf_tensor(name, shape, dt))

        sem = {name: stack.enter_context(nc.semaphore(name)) for name in SEMAPHORES}
        ps = [stack.enter_context(nc.psum_tensor(f"bank{i}", [P, 512], F32)) for i in range(8)]
        m = {
            "x": sb("x", [P, SEQS, DM]),
            "ident": sb("ident", [P, P]),
            "hsT_hl": sb("hsT_hl", [P, 2, KT, TOK], F32R),
        }
        with ExitStack() as attention:
            def asb(name, shape, dt=F32):
                return attention.enter_context(nc.sbuf_tensor(name, shape, dt))

            m["ctxT_hl"] = asb("ctxT_hl", [P, 2, KT, TOK], F32R)
            m["cosT"] = asb("cosT", [P, TOK])
            m["sinT"] = asb("sinT", [P, TOK])
            m["cap"] = asb("cap", [P, SEQS, P])
            m["wqkv_hl"] = asb("cross_wqkv_hl", [P, PIECES, 2, KT, P], F32R)
            m["stage"] = asb("weights_staged", [P, 2, DM])
            self_attention(nc, m, sem, ps, io)
            cross_attention(nc, m, sem, ps, io)
        feed_forward(nc, m, sem, ps, io)


def constant_tables():
    import numpy as np

    i = np.arange(P)
    rel = (i[None, :] - i[:, None]).astype(np.float32)
    rel[i[None, :] > i[:, None]] = -1.0e30
    own = (i[:, None] // HD1 == np.arange(8)[None, :]).astype(np.float32) * np.float32(SCALE1)
    inv = (1.0 / np.float32(10000.0) ** (np.arange(0, D2, 2, dtype=np.float32) / np.float32(D2))).astype(np.float32)
    angle = np.arange(MAX_POS, dtype=np.float32)[:, None] * inv[None, :]
    cos, sin = np.cos(angle), np.sin(angle)
    rope = np.concatenate([cos, cos, -sin, sin], axis=1).astype(np.float32)
    return np.ascontiguousarray(np.concatenate([rel, own], axis=1)), rope


_INPUTS = {
    "x": "x", "ctx": "ctx_4096", "pos": "pos_BxS2", "mask": "mask_BxSxS2_ik0",
    "wq1": "L0_attn_Wq", "wkv1": "L0_attn_Wkv", "wo1": "L0_attn_Wo",
    "wq2": "L0_xattn_Wq", "wk2": "L0_xattn_Wk", "wv2": "L0_xattn_Wv", "wo2": "L0_xattn_Wo",
    "wg": "L0_ffn_W_gate", "wu": "L0_ffn_W_up", "wd": "L0_ffn_W_down",
}


def kernel(**inputs):
    import numpy as _np
    import concourse.bacc as _bacc
    from concourse import mybir as _mybir
    from concourse.bass_utils import run_bass_kernel_spmd as _run

    nc = _bacc.Bacc("TRN2", target_bir_lowering=False, num_devices=1)
    arrays, io = {}, {}
    constants, rope = constant_tables()
    given = {name: _np.ascontiguousarray(inputs[source]) for name, source in _INPUTS.items()}
    given["pos"] = _np.ascontiguousarray(given["pos"].T)
    for name, a in {**given, "constants": constants, "rope": rope}.items():
        arrays[f"in_{name}"] = a
        io[name] = nc.dram_tensor(f"in_{name}", a.shape, _mybir.dt.from_np(a.dtype), kind="ExternalInput").ap()
    io["out"] = nc.dram_tensor("out", (SEQS, P, DM), _mybir.dt.float32, kind="ExternalOutput").ap()
    program(nc, io)
    r = _run(nc, [arrays], core_ids=[0])
    return r.results[0]["out"]
```

```python
from contextlib import ExitStack

import concourse.bass as bass
from concourse import mybir

F32 = mybir.dt.float32
F32R = mybir.dt.float32r
I32 = mybir.dt.int32
ALU = mybir.AluOpType
ACT = mybir.ActivationFunctionType
AX = mybir.AxisListType

P = 128
SEQS = 8
DM = 512
KT = DM // P
HEADS = 32
HD1 = DM // HEADS
QUAD = 4
STEPS = HEADS // QUAD
D2 = 128
GROUPS = 8
HALF = SEQS // 2
HT = HALF * P
TOK = SEQS * P
SLOTS = 5
FF = 1376
FT = (FF + P - 1) // P
FLAST = FF - (FT - 1) * P
MAX_POS = 512
EPS = 1e-5
SCALE1 = HD1 ** -0.5
SCALE2 = float(D2) ** -0.5
MASKED = -1.0e9
UNMASKED = 3.0e38


def alibi_slopes():
    start = 2.0 ** (-2.0 ** (-(5 - 3)))
    return [start ** (i + 1) for i in range(HEADS)]


def since(b, k):
    return b >= k if isinstance(b, int) else k <= 3


def block_of(t, b, n=P):
    return t[..., bass.ds(b * n, n)]


def self_attention(nc, m, sem, ps, io):
    SC, TB, OB, G = ps[0:2], ps[2:4], ps[4:6], ps[6:8]
    x, hsT, ctxT = m["x"], m["hsT_hl"], m["ctxT_hl"]
    ident, exponent = m["ident"], m["exponent"]
    with ExitStack() as stack:
        def sb(name, shape, dt=F32):
            return stack.enter_context(nc.sbuf_tensor(name, shape, dt))

        bias = sb("alibi_bias", [P, HEADS, P])
        rel = sb("relative_position", [P, P])
        head_of_row = sb("head_of_row", [P, QUAD])
        wq = sb("self_wq", [P, KT, DM])
        wo = sb("self_wo", [P, KT, DM])
        wkv = sb("self_wkv", [P, KT, 2 * HD1])
        wk8 = sb("self_wk_8_times", [P, KT, 8, HD1])
        stats = sb("self_stats", [P, 2, 6])
        mv = sb("x1_mean_var", [P, 2])
        rstd = sb("x1_rstd", [P, 2])
        mv0 = sb("x_mean_var", [P, SEQS, 2])
        rstd0 = sb("x_rstd", [P, 2, SEQS])
        xn = sb("xn", [P, DM])
        xnT = sb("xnT", [P, KT, P])
        q_hl = sb("self_q_hl", [P, STEPS, 2, QUAD * HD1], F32R)
        qT = sb("self_qT_high_above_low", [P, STEPS, P], F32R)
        kT = sb("self_kT_8_times_hl", [P, 2, P], F32R)
        kexp = sb("self_k_by_head_hl", [P, 2, 2, QUAD, P], F32R)
        v = sb("self_v_and_ones", [P, SEQS, HD1 + 1])
        S = sb("self_scores", [P, 2, QUAD, P])
        PR = sb("self_probs", [P, 2, QUAD, P])
        negmax = sb("self_negmax", [P, 2, QUAD])
        PT = sb("self_probsT", [P, 2, QUAD, P])
        rsum = sb("self_rsum", [P, HEADS])
        attn = sb("self_attn", [P, DM])
        attnT = sb("self_attnT", [P, KT, P])
        hs = sb("self_hs", [P, DM])
        ctx_tok = sb("ctx_tok", [P, DM])
        pos = sb("positions", [P, SEQS], I32)

        tables = wq[:].rearrange("p t (h w) -> p (t h) w", h=2)
        slopes = alibi_slopes()
        block = stack.enter_context(nc.Block())

        @block.sync
        def _(sp):
            sp.dma_start(x[:, 0, :], io["x"][0]).then_inc(sem["x_first"], 16)
            sp.dma_start(rel[:], io["constants"][:, 0:P]).then_inc(sem["rel_loaded"], 16)
            sp.dma_start(head_of_row[:], io["constants"][:, P:P + QUAD]).then_inc(sem["head_of_row_loaded"], 16)
            sp.dma_start(wkv[:], io["wkv1"].rearrange("(t p) n -> p t n", p=P)).then_inc(sem["wkv1_loaded"], 16)
            sp.dma_start(wq[:], io["wq1"].rearrange("(t p) n -> p t n", p=P)).then_inc(sem["wq1_loaded"], 16)
            sp.dma_start(x[:, 1:SEQS, :], io["x"][1:SEQS].rearrange("b p d -> p b d")).then_inc(sem["x_rest"], 16)
            sp.dma_start(pos[:], io["pos"]).then_inc(sem["pos_loaded"], 16)
            sp.dma_start(wo[:], io["wo1"].rearrange("(t p) n -> p t n", p=P)).then_inc(sem["wo1_loaded"], 16)
            sp.dma_start(m["cap"][:].bitcast(I32), io["mask"].rearrange("b q k -> q b k")).then_inc(sem["mask_loaded"], 16)

            def load_ctx(b):
                sp.dma_start(ctx_tok[:], io["ctx"][bass.ds(b, 1)].rearrange("b p d -> p (b d)")).then_inc(sem["ctx_loaded"], 16)

            load_ctx(0)
            with sp.Fori(1, SEQS) as b:
                sp.wait_ge(sem["ctx_transposed"], b)
                load_ctx(b)
            for j in range(PIECES):
                load_piece(sp, m, sem, j, j % SLOTS, piece_source(io, j, 0), first=j < SLOTS)

        @block.gpsimd
        def _(pool):
            nc.gpsimd.memset(ident[:], 0.0).then_inc(sem["ident_zero"], 1)
            pool.wait_ge(sem["ident_zero"], 1)
            nc.gpsimd.affine_select(out=ident[:], in_=ident[:], compare_op=ALU.not_equal, fill=1.0, base=0,
                                    pattern=[[-1, P]], channel_multiplier=1).then_inc(sem["ident_ready"], 1)
            nc.gpsimd.memset(exponent[:, 0:1], -0.5).then_inc(sem["exponent_ready"], 1)
            nc.gpsimd.memset(exponent[:, 1:2], EPS).then_inc(sem["exponent_ready"], 1)
            nc.gpsimd.memset(v[:], 1.0).then_inc(sem["ones_ready"], 1)

            def rstd_of_x(first, last):
                n = last - first
                pool.wait_ge(sem["mv0"], last)
                nc.gpsimd.tensor_tensor(rstd0[:, 0, first:last], mv0[:, first:last, 1], exponent[:, 1:2].to_broadcast([P, n]), ALU.add).then_inc(sem["var_eps0"], 1)
                pool.wait_ge(sem["var_eps0"], min(first, 2) + 1)
                nc.gpsimd.tensor_tensor(rstd0[:, 1, first:last], rstd0[:, 0, first:last], exponent[:, 0:1].to_broadcast([P, n]), ALU.pow).then_inc(sem["rstd0"], 1)

            def xn_of(c):
                pool.wait_ge(sem["rstd0"], 2 if isinstance(c, int) and c == 1 else 3)
                pool.wait_ge(sem["xn_transposed"], c)
                nc.gpsimd.tensor_tensor(xn[:].unsqueeze(1), x[:, bass.ds(c, 1), :], mv0[:, bass.ds(c, 1), 0:1].to_broadcast([P, 1, DM]),
                                        ALU.subtract).then_inc(sem["xn_centred"], 1)
                pool.wait_ge(sem["xn_centred"], c)
                nc.gpsimd.tensor_tensor(xn[:], xn[:], rstd0[:, 1, bass.ds(c, 1)].to_broadcast([P, DM]), ALU.mult).then_inc(sem["xn"], 1)

            def hs_of(b):
                pool.wait_ge(sem["mv1"], b + 1)
                nc.gpsimd.tensor_tensor(rstd[:, 0:1], mv[:, 1:2], exponent[:, 1:2], ALU.add).then_inc(sem["var_eps1"], 1)
                pool.wait_ge(sem["var_eps1"], b + 1)
                nc.gpsimd.tensor_tensor(rstd[:, 1:2], rstd[:, 0:1], exponent[:, 0:1], ALU.pow).then_inc(sem["rstd1"], 1)
                if not (isinstance(b, int) and b == 0):
                    pool.wait_ge(sem["hs_transposed"], b)
                nc.gpsimd.tensor_tensor(hs[:].unsqueeze(1), x[:, bass.ds(b, 1), :], mv[:, 0:1].unsqueeze(1).to_broadcast([P, 1, DM]),
                                        ALU.subtract).then_inc(sem["hs_centred"], 1)
                pool.wait_ge(sem["rstd1"], b + 1)
                pool.wait_ge(sem["hs_centred"], b + 1)
                nc.gpsimd.tensor_tensor(hs[:], hs[:], rstd[:, 1:2].to_broadcast([P, DM]), ALU.mult).then_inc(sem["hs"], 1)

            def keys_by_head(c):
                pool.wait_ge(sem["kv_copied"], c + 1)
                if since(c, 2):
                    pool.wait_ge(sem["scores1"], STEPS * (c - 1))
                for part in range(2):
                    i = nc.gpsimd.tensor_tensor(kexp[:, bass.ds(c % 2, 1), part].rearrange("p s h k -> p (s h) k"),
                                                kT[:, part:part + 1, :].bitcast(F32).to_broadcast([P, QUAD, P]),
                                                head_of_row[:].unsqueeze(2).to_broadcast([P, QUAD, P]), ALU.mult)
                i.then_inc(sem["kexp"], 1)

            pool.wait_ge(sem["exponent_ready"], 2)
            rstd_of_x(0, 1)
            pool.wait_ge(sem["rel_loaded"], 16)
            for h in range(HEADS):
                nc.gpsimd.tensor_scalar(bias[:, h, :], rel[:], slopes[h], None, ALU.mult).then_inc(sem["bias"], 1)
                if h == 15:
                    pool.wait_ge(sem["head_of_row_loaded"], 16)
                    keys_by_head(0)
                    rstd_of_x(1, 2)
                    xn_of(1)

            def body(b):
                if not since(b, SEQS - 1) and since(b, 1):
                    xn_of(b + 1)
                if since(b, 2) and not since(b, SEQS):
                    hs_of(b - 2)
                if not since(b, SEQS - 1):
                    keys_by_head(b + 1)

            body(0)
            rstd_of_x(2, SEQS)
            body(1)
            body(2)
            with pool.Fori(3, SEQS - 1) as b:
                body(b)
            body(SEQS - 1)
            pool.wait_ge(sem["pos_loaded"], 16)
            pool.wait_ge(sem["q1"], SEQS)
            for b in range(SEQS):
                nc.gpsimd.indirect_dma_start(
                    tables[:, b, :], None, io["rope"], bass.IndirectOffsetOnAxis(ap=pos[:, b:b + 1].bitcast(mybir.dt.uint32), axis=0),
                ).then_inc(sem["tables_loaded"], 16)
            for j in range(PIECES):
                piece_low(nc, pool, m, sem, j % SLOTS, j, m["wqkv_hl"][:, j])
            body(SEQS)

        @block.vector
        def _(dve):
            def stats_of_x(b):
                if b > 0:
                    dve.wait_ge(sem["mv0"], b)
                nc.vector.bn_stats(stats[:, 0, :], x[:, b, :]).then_inc(sem["stats0"], 1)
                dve.wait_ge(sem["stats0"], b + 1)
                nc.vector.bn_aggr(mv0[:, b, :], stats[:, 0, :]).then_inc(sem["mv0"], 1)

            dve.wait_ge(sem["x_first"], 16)
            stats_of_x(0)
            dve.wait_ge(sem["wkv1_loaded"], 16)
            nc.vector.tensor_copy(wk8[:], wkv[:, :, 0:HD1].unsqueeze(2).to_broadcast([P, KT, 8, HD1])).then_inc(sem["wk8"], 1)
            dve.wait_ge(sem["rstd0"], 1)
            nc.vector.tensor_scalar(xn[:], x[:, 0, :], mv0[:, 0, 0:1], rstd0[:, 1, 0:1], ALU.subtract, ALU.mult).then_inc(sem["xn"], 1)

            def q_low(c):
                dve.wait_ge(sem["q_high"], c + 1)
                nc.vector.tensor_tensor(q_hl[:, :, 1, :], G[1][:].rearrange("p (s d) -> p s d", s=STEPS), q_hl[:, :, 0, :].bitcast(F32),
                                        ALU.subtract).then_inc(sem["q_copied"], 1)

            def k_low(c):
                dve.wait_ge(sem["kv_high"], c + 1)
                nc.vector.tensor_tensor(kT[:, 1, :], G[0][:, 0:P], kT[:, 0, :].bitcast(F32), ALU.subtract).then_inc(sem["kv_copied"], 1)

            q_low(0)
            k_low(0)
            dve.wait_ge(sem["x_rest"], 16)
            stats_of_x(1)

            def normalise(b, i):
                o = OB[i][:, 0:16 * (HD1 + 1)].rearrange("p (h d) -> p h d", h=16)
                earlier = not (isinstance(b, int) and b == 0)
                dve.wait_ge(sem["pv1"], STEPS * b + HALF * (i + 1))
                if earlier:
                    dve.wait_ge(sem["attn"], 2 * b - 1 + i)
                nc.vector.reciprocal(rsum[:, 16 * i:16 * i + 16].unsqueeze(2), o[:, :, HD1:HD1 + 1]).then_inc(sem["rsum1"], 1)
                dve.wait_ge(sem["rsum1"], 2 * b + i + 1)
                if earlier:
                    dve.wait_ge(sem["attn_transposed"], b)
                nc.vector.tensor_tensor(attn[:].rearrange("p (i h d) -> p i h d", i=2, h=16)[:, i], o[:, :, 0:HD1],
                                        rsum[:, 16 * i:16 * i + 16].unsqueeze(2).to_broadcast([P, 16, HD1]),
                                        ALU.mult).then_inc(sem["attn"], 1)

            def hs_low(p):
                dve.wait_ge(sem["hs_high"], p + 1)
                nc.vector.tensor_tensor(block_of(hsT[:, 1], p), G[0][:].rearrange("p (t k) -> p t k", t=KT),
                                        block_of(hsT[:, 0], p).bitcast(F32), ALU.subtract).then_inc(sem["hs_low"], 1)

            def add_output(b):
                dve.wait_ge(sem["out1"], b + 1)
                nc.vector.tensor_tensor(x[:, bass.ds(b, 1), :], x[:, bass.ds(b, 1), :], G[0][:].unsqueeze(1), ALU.add).then_inc(sem["x1"], 1)

            def body(b):
                scores, front = not since(b, SEQS), not since(b, SEQS - 1)
                for s in range(STEPS):
                    n = STEPS * b + s
                    if s == 3 and since(b, 1):
                        normalise(b - 1, 1)
                    if scores:
                        dve.wait_ge(sem["scores1"], n + 1)
                        if since(b, 1) or s >= 2:
                            dve.wait_ge(sem["exp1"], n - 1)
                        if not since(b, 1):
                            dve.wait_ge(sem["bias"], QUAD * (s + 1))
                        nc.vector.tensor_tensor(S[:, s % 2], SC[s % 2][:].rearrange("p (h k) -> p h k", h=QUAD),
                                                bias[:, QUAD * s:QUAD * s + QUAD, :], ALU.add).then_inc(sem["biased1"], 1)
                        dve.wait_ge(sem["biased1"], n + 1)
                        nc.vector.tensor_reduce(negmax[:, s % 2, :], S[:, s % 2], AX.X, ALU.max, negate=True).then_inc(sem["max1"], 1)
                    if s < SEQS - 2 and not since(b, 1):
                        stats_of_x(s + 2)
                    if s == 0 and since(b, 2):
                        add_output(b - 2)
                    if s == 1 and since(b, 2) and not since(b, SEQS):
                        dve.wait_ge(sem["x_first"], 16)
                        dve.wait_ge(sem["x1"], b - 1)
                        nc.vector.bn_stats(stats[:, 1, :].unsqueeze(1), x[:, bass.ds(b - 2, 1), :]).then_inc(sem["stats1"], 1)
                        dve.wait_ge(sem["x_first"], 16)
                        dve.wait_ge(sem["stats1"], b - 1)
                        if since(b, 3):
                            dve.wait_ge(sem["hs"], b - 2)
                        nc.vector.bn_aggr(mv[:], stats[:, 1, :]).then_inc(sem["mv1"], 1)
                    if s == 3 and since(b, 2) and not since(b, SEQS):
                        hs_low(b - 2)
                    if s == 4 and front:
                        q_low(b + 1)
                        k_low(b + 1)
                    if s == 6 and scores:
                        dve.wait_ge(sem["ctx_high"], b + 1)
                        nc.vector.tensor_tensor(block_of(ctxT[:, 1], b), G[1][:].rearrange("p (t k) -> p t k", t=KT),
                                                block_of(ctxT[:, 0], b).bitcast(F32), ALU.subtract).then_inc(sem["ctx_low"], 1)
                    if s == 7 and scores:
                        normalise(b, 0)

            body(0)
            dve.wait_ge(sem["mask_loaded"], 16)
            nc.vector.tensor_scalar(m["cap"][:], m["cap"][:].bitcast(I32), 0, UNMASKED, ALU.not_equal, ALU.mult).then_inc(sem["mask_is_set"], 1)
            dve.wait_ge(sem["mask_is_set"], 1)
            nc.vector.tensor_scalar(m["cap"][:], m["cap"][:], MASKED, None, ALU.add)
            body(1)
            body(2)
            with dve.Fori(3, SEQS - 1) as b:
                body(b)
            for b in range(SEQS - 1, SEQS + 1):
                body(b)
            add_output(SEQS - 1)

        @block.scalar
        def _(act):
            def copy_xnT(c, first=False):
                act.wait_ge(sem["xn_transposed"], c + 1)
                if not first:
                    act.wait_ge(sem["kv1"], c)
                nc.scalar.copy(xnT[:], G[0][:].rearrange("p (t k) -> p t k", t=KT)).then_inc(sem["xnT"], 1)

            def copy_q(c, first=False):
                act.wait_ge(sem["q1"], c + 1)
                if not first:
                    act.wait_ge(sem["q_transposed"], 2 * c)
                nc.scalar.copy(q_hl[:, :, 0, :], G[1][:].rearrange("p (s d) -> p s d", s=STEPS)).then_inc(sem["q_high"], 1)

            def copy_kv(c, first=False):
                act.wait_ge(sem["kv1"], c + 1)
                if first:
                    act.wait_ge(sem["ones_ready"], 1)
                else:
                    act.wait_ge(sem["kexp"], c)
                nc.scalar.copy(v[:, bass.ds(c, 1), 0:HD1], G[0][:, P:P + HD1].unsqueeze(1))
                nc.scalar.copy(kT[:, 0, :], G[0][:, 0:P]).then_inc(sem["kv_high"], 1)

            def copy_qT(c, half, first=False):
                act.wait_ge(sem["q_transposed"], 2 * c + half + 1)
                if not first:
                    act.wait_ge(sem["scores1"], STEPS * c - STEPS + HALF * (half + 1))
                nc.scalar.copy(qT[:, HALF * half:HALF * (half + 1), :], G[1][:].rearrange("p (s k) -> p s k", s=HALF)).then_inc(sem["qT"], 1)

            copy_xnT(0, first=True)
            copy_q(0, first=True)
            copy_kv(0, first=True)
            copy_qT(0, 0, first=True)
            copy_qT(0, 1, first=True)

            def hs_high(p):
                act.wait_ge(sem["hs_transposed"], p + 1)
                nc.scalar.copy(block_of(hsT[:, 0], p), G[0][:].rearrange("p (t k) -> p t k", t=KT)).then_inc(sem["hs_high"], 1)

            def body(b):
                scores, front = not since(b, SEQS), not since(b, SEQS - 1)
                back = since(b, 1)
                for s in range(STEPS):
                    n = STEPS * b + s
                    if s == 1 and scores and since(b, 1):
                        copy_qT(b, 1)
                    if (since(b, 1) or s >= 2) and (scores or s < 2):
                        act.wait_ge(sem["probs_transposed1"], n - 1)
                        if since(b, 1) or s >= 4:
                            act.wait_ge(sem["pv1"], n - 3)
                        nc.scalar.copy(PT[:, s % 2], TB[s % 2][:].rearrange("p (h k) -> p h k", h=QUAD)).then_inc(sem["probsT1"], 1)
                    if s == 7 and not since(b, 1):
                        copy_qT(b + 1, 0)
                    if s == 5 and back:
                        act.wait_ge(sem["attn_transposed"], b)
                        if since(b, 2):
                            act.wait_ge(sem["out1"], b - 1)
                        nc.scalar.copy(attnT[:], G[0][:].rearrange("p (t k) -> p t k", t=KT)).then_inc(sem["attnT"], 1)
                    if s == 1 and front:
                        copy_xnT(b + 1)
                    if scores:
                        act.wait_ge(sem["max1"], n + 1)
                        if since(b, 1) or s >= 2:
                            act.wait_ge(sem["probs_transposed1"], n - 1)
                        for j in range(QUAD):
                            e = nc.scalar.activation(PR[:, s % 2, j, :], S[:, s % 2, j, :], ACT.Exp, bias=negmax[:, s % 2, j:j + 1])
                        e.then_inc(sem["exp1"], 1)
                    if s == 7 and front and since(b, 1):
                        copy_qT(b + 1, 0)
                    if s == 3 and front:
                        copy_q(b + 1)
                    if s == 3 and since(b, 2) and not since(b, SEQS):
                        hs_high(b - 2)
                    if 1 <= s <= PIECES and scores and not front:
                        piece_high(nc, act, m, sem, (s - 1) % SLOTS, (s - 1) // SLOTS + 1, m["wqkv_hl"][:, s - 1])
                    if s == 4 and front:
                        copy_kv(b + 1)
                    if s == 5 and scores:
                        act.wait_ge(sem["ctx_transposed"], b + 1)
                        nc.scalar.copy(block_of(ctxT[:, 0], b), G[1][:].rearrange("p (t k) -> p t k", t=KT)).then_inc(sem["ctx_high"], 1)
                    if s == 5 and back and not scores:
                        for i in range(HALF):
                            act.wait_ge(sem["tables_transposed"], i + 1)
                            t = ps[i][:].rearrange("p (b w k) -> p w b k", b=2, w=2)
                            nc.scalar.copy(m["cosT"][:, 2 * i * P:2 * (i + 1) * P].rearrange("p (b k) -> p b k", b=2), t[:, 0])
                            nc.scalar.copy(m["sinT"][:, 2 * i * P:2 * (i + 1) * P].rearrange("p (b k) -> p b k", b=2), t[:, 1])

            for b in range(3):
                body(b)
            with act.Fori(3, SEQS - 1) as b:
                body(b)
            for b in range(SEQS - 1, SEQS + 1):
                body(b)

        @block.tensor
        def _(pe):
            def transpose4(bank, src, done):
                for t in range(KT):
                    i = nc.tensor.transpose(bank[:, t * P:(t + 1) * P], src[:, t * P:(t + 1) * P], ident[:])
                i.then_inc(sem[done], 1)

            def xn_transposes(c):
                pe.wait_ge(sem["xn"], c + 1)
                transpose4(G[0], xn, "xn_transposed")

            def q_product(c, tiles):
                for t in tiles:
                    i = nc.tensor.matmul(G[1][:], xnT[:, t, :], wq[:, t, :], start=(t == 0), stop=(t == KT - 1))
                if t == KT - 1:
                    i.then_inc(sem["q1"], 1)

            def kv_product(c):
                for t in range(KT):
                    nc.tensor.matmul(G[0][:, 0:P], wk8[:, t].rearrange("p r d -> p (r d)"), xnT[:, t, :], start=(t == 0), stop=(t == KT - 1))
                for t in range(KT):
                    i = nc.tensor.matmul(G[0][:, P:P + HD1], xnT[:, t, :], wkv[:, t, HD1:2 * HD1], start=(t == 0), stop=(t == KT - 1))
                i.then_inc(sem["kv1"], 1)

            def q_transposes(c, half):
                pe.wait_ge(sem["q_copied"], c + 1)
                if half == 1:
                    pe.wait_ge(sem["qT"], 2 * c + 1)
                for s in range(HALF):
                    i = nc.tensor.transpose(G[1][:, s * P:(s + 1) * P], q_hl[:, HALF * half + s].rearrange("p a d -> p (a d)").bitcast(F32), ident[:])
                i.then_inc(sem["q_transposed"], 1)

            def out_product(tiles):
                for t in tiles:
                    i = nc.tensor.matmul(G[0][:], attnT[:, t, :], wo[:, t, :], start=(t == 0), stop=(t == KT - 1))
                if t == KT - 1:
                    i.then_inc(sem["out1"], 1)

            def hs_transposes(p):
                pe.wait_ge(sem["hs"], p + 1)
                transpose4(G[0], hs, "hs_transposed")

            pe.wait_ge(sem["ident_ready"], 1)
            xn_transposes(0)
            pe.wait_ge(sem["xnT"], 1)
            pe.wait_ge(sem["wq1_loaded"], 16)
            q_product(0, range(KT))
            pe.wait_ge(sem["wk8"], 1)
            kv_product(0)
            q_transposes(0, 0)
            q_transposes(0, 1)

            def body(b):
                scores, front = not since(b, SEQS), not since(b, SEQS - 1)
                back = since(b, 1)
                for s in range(STEPS):
                    n = STEPS * b + s
                    if scores:
                        if s == 0:
                            pe.wait_ge(sem["qT"], 2 * b + 1)
                            pe.wait_ge(sem["kexp"], b + 1)
                        if s == 4:
                            pe.wait_ge(sem["qT"], 2 * b + 2)
                        if since(b, 1) or s >= 2:
                            pe.wait_ge(sem["biased1"], n - 1)
                        for part in range(2):
                            keys = kexp[:, bass.ds(b % 2, 1), part].rearrange("p s h k -> p (s h k)")
                            i = nc.tensor.matmul(SC[s % 2][:], qT[:, s, :], keys, start=(part == 0), stop=(part == 1))
                        i.then_inc(sem["scores1"], 1)
                    if s == 7 and not since(b, 1):
                        pe.wait_ge(sem["ctx_low"], b + 1)
                        q_transposes(b + 1, 0)
                    if (since(b, 1) or s >= 2) and (scores or s < 2):
                        pe.wait_ge(sem["exp1"], n - 1)
                        if since(b, 1) or s >= 4:
                            pe.wait_ge(sem["probsT1"], n - 3)
                        for j in range(QUAD):
                            i = nc.tensor.transpose(TB[s % 2][:, j * P:(j + 1) * P], PR[:, s % 2, j, :], ident[:])
                        i.then_inc(sem["probs_transposed1"], 1)
                    if (since(b, 1) or s >= 3) and (scores or s < 3):
                        r = (s - 3) % STEPS
                        owner = b if s >= 3 else b - 1
                        pe.wait_ge(sem["probsT1"], n - 2)
                        if r % HALF == 0 and (since(b, 2) or owner >= 1):
                            pe.wait_ge(sem["attn"], 2 * owner - 1 + r // HALF)
                        for j in range(QUAD):
                            c = (QUAD * (r % HALF) + j) * (HD1 + 1)
                            i = nc.tensor.matmul(OB[r // HALF][:, c:c + HD1 + 1], PT[:, r % 2, j, :], v[:, bass.ds(owner, 1), :].rearrange("p b d -> p (b d)"),
                                                 start=True, stop=True)
                        i.then_inc(sem["pv1"], 1)
                    if s == 0 and scores and since(b, 1):
                        q_transposes(b, 1)
                    if s == 1 and front:
                        pe.wait_ge(sem["kv_copied"], b + 1)
                        if since(b, 2):
                            pe.wait_ge(sem["x1"], b - 1)
                        xn_transposes(b + 1)
                    if s == 2 and front:
                        pe.wait_ge(sem["xnT"], b + 2)
                        pe.wait_ge(sem["qT"], 2 * b + 2)
                        q_product(b + 1, (0, 1))
                    if s == 3 and front:
                        q_product(b + 1, (2, 3))
                    if s == 3 and since(b, 2) and not since(b, SEQS):
                        hs_transposes(b - 2)
                    if s == 4 and front:
                        if since(b, 2):
                            pe.wait_ge(sem["hs_low"], b - 1)
                        kv_product(b + 1)
                    if s == 5 and back:
                        if front:
                            pe.wait_ge(sem["kv_copied"], b + 2)
                        elif scores:
                            pe.wait_ge(sem["hs_low"], b - 1)
                        else:
                            pe.wait_ge(sem["x1"], b - 1)
                        pe.wait_ge(sem["attn"], 2 * b)
                        transpose4(G[0], attn, "attn_transposed")
                    if s == 5 and scores:
                        pe.wait_ge(sem["ctx_loaded"], 16 * b + 16)
                        if front:
                            pe.wait_ge(sem["q_copied"], b + 2)
                        transpose4(G[1], ctx_tok, "ctx_transposed")
                    if s == 5 and back and not scores:
                        pe.wait_ge(sem["tables_loaded"], 16 * SEQS)
                        pe.wait_ge(sem["biased1"], STEPS * SEQS)
                        pe.wait_ge(sem["probsT1"], STEPS * SEQS)
                        for i in range(HALF):
                            for k in range(2):
                                for w in range(2):
                                    t = nc.tensor.transpose(ps[i][:, (2 * k + w) * P:(2 * k + w + 1) * P], tables[:, 2 * i + k, w * P:(w + 1) * P], ident[:])
                            t.then_inc(sem["tables_transposed"], 1)
                    if s == 6 and back:
                        pe.wait_ge(sem["attnT"], b)
                        if not since(b, 2):
                            pe.wait_ge(sem["wo1_loaded"], 16)
                        out_product((0, 1))
                    if s == 7 and front and since(b, 1):
                        pe.wait_ge(sem["ctx_low"], b + 1)
                        q_transposes(b + 1, 0)
                    if s == 7 and back:
                        out_product((2, 3))

            for b in range(3):
                body(b)
            with pe.Fori(3, SEQS - 1) as b:
                body(b)
            for b in range(SEQS - 1, SEQS + 1):
                body(b)


PIECES = 6
PIECE_TURN = [0, 1, 2, 7, 8, 9]
WO_TURN = 3
TURNS = 10


def piece_source(io, j, g):
    name, at = ("wk2", g) if j == 0 else ("wv2", g) if j == PIECES - 1 else ("wq2", g * QUAD + (j - 1))
    return io[name].rearrange("(t p) n -> p t n", p=P)[:, :, bass.ds(at * P, P)]


def load_piece(sp, m, sem, turn, slot, source, first=False):
    if not first:
        sp.wait_ge(sem["piece_split"], turn - SLOTS + 1)
    dst = m["stage"][:, slot, :]
    if len(source.shape) == 3:
        dst = dst.rearrange("p (t n) -> p t n", t=KT)
    sp.dma_start(dst, source).then_inc(sem[f"piece_loaded{slot}"], 16)


def piece_high(nc, act, m, sem, slot, loads, dst):
    src = m["stage"][:, slot, :]
    if len(dst.shape) == 4:
        src = src.rearrange("p (t n) -> p t n", t=KT)
    act.wait_ge(sem[f"piece_loaded{slot}"], 16 * loads)
    nc.scalar.copy(dst[:, 0], src).then_inc(sem["piece_high"], 1)


def piece_low(nc, pool, m, sem, slot, turn, dst):
    src = m["stage"][:, slot, :]
    if len(dst.shape) == 4:
        src = src.rearrange("p (t n) -> p t n", t=KT)
    pool.wait_ge(sem["piece_high"], turn + 1)
    nc.gpsimd.tensor_tensor(dst[:, 1], src, dst[:, 0].bitcast(F32), ALU.subtract).then_inc(sem["piece_split"], 1)


def products(nc, out, stationary, moving, first, last):
    for k, (a, b) in enumerate(((0, 0), (0, 1), (1, 0))):
        i = nc.tensor.matmul(out, stationary[:, a], moving[:, b], start=(first and k == 0), stop=(last and k == 2))
    return i


EARLY = 2
NORM_SEQ = [SEQS - 2, SEQS - 1] + list(range(SEQS))


def norm_stats(nc, dve, m, sem, k):
    if k >= EARLY:
        dve.wait_ge(sem["x2"], SEQS * (GROUPS - 1) + NORM_SEQ[k] + 1)
    if k > 0:
        dve.wait_ge(sem["norm_mv"], k)
    nc.vector.bn_stats(m["norm_stats"][:], m["x"][:, NORM_SEQ[k], :]).then_inc(sem["norm_stats"], 1)
    dve.wait_ge(sem["norm_stats"], k + 1)
    nc.vector.bn_aggr(m["norm_mv"][:, k, :], m["norm_stats"][:]).then_inc(sem["norm_mv"], 1)


def norm_rstd(nc, pool, m, sem, k):
    r, e = m["norm_rstd"], m["exponent"]
    pool.wait_ge(sem["norm_mv"], k + 1)
    nc.gpsimd.tensor_tensor(r[:, k, 0:1], m["norm_mv"][:, k, 1:2], e[:, 1:2], ALU.add).then_inc(sem["norm_var_eps"], 1)
    pool.wait_ge(sem["norm_var_eps"], k + 1)
    nc.gpsimd.tensor_tensor(r[:, k, 1:2], r[:, k, 0:1], e[:, 0:1], ALU.pow).then_inc(sem["norm_rstd"], 1)


def norm_rows(nc, dve, m, sem, k, rows):
    dve.wait_ge(sem["norm_rstd"], k + 1)
    if EARLY <= k < EARLY + 2:
        dve.wait_ge(sem["piece_split"], PIECES + TURNS * (GROUPS - 1) + QUAD)
    elif k >= EARLY + 2:
        dve.wait_ge(sem["norm_transposed"], k - 1)
    nc.vector.tensor_scalar(rows, m["x"][:, NORM_SEQ[k], :], m["norm_mv"][:, k, 0:1], m["norm_rstd"][:, k, 1:2],
                            ALU.subtract, ALU.mult).then_inc(sem["norm_rows"], 1)


def norm_transposes(nc, pe, m, sem, k, rows, bank):
    pe.wait_ge(sem["norm_rows"], k + 1)
    for t in range(KT):
        i = nc.tensor.transpose(bank[:, t * P:(t + 1) * P], rows[:, t * P:(t + 1) * P], m["ident"][:])
    i.then_inc(sem["norm_transposed"], 1)


def norm_high(nc, act, m, sem, k, bank):
    act.wait_ge(sem["norm_transposed"], k + 1)
    nc.scalar.copy(block_of(m["hsT_hl"][:, 0], NORM_SEQ[k]), bank[:].rearrange("p (t k) -> p t k", t=KT)).then_inc(sem["norm_high"], 1)


def norm_low(nc, dve, m, sem, k, bank):
    dve.wait_ge(sem["norm_high"], k + 1)
    nc.vector.tensor_tensor(block_of(m["hsT_hl"][:, 1], NORM_SEQ[k]), bank[:].rearrange("p (t k) -> p t k", t=KT),
                            block_of(m["hsT_hl"][:, 0], NORM_SEQ[k]).bitcast(F32), ALU.subtract).then_inc(sem["norm_low"], 1)


def width_of(i):
    return FLAST if isinstance(i, int) and i == FT - 1 else P


def load_ff_rows(sp, m, sem, io, i):
    n = width_of(i)
    at = i * P if isinstance(i, int) else sp.snap(i * P)
    for k, name in enumerate(("wg", "wu")):
        if not (isinstance(i, int) and i == 0):
            sp.wait_ge(sem["w_transposed"], 2 * i + k - 1)
            if k == 1:
                sp.wait_ge(sem["wd_transposed"], i)
        sp.dma_start(m["gate_up_rows"][0:n, k, :], io[name][bass.ds(at, n), :]).then_inc(sem[f"{name}_loaded"], 16)
    sp.dma_start(m["down_rows"][:, :, 0:n], io["wd"].rearrange("(t p) f -> p t f", p=P)[:, :, bass.ds(at, n)]).then_inc(sem["wd_loaded"], 16)


def half_of(t, half):
    return t[..., half * HT:(half + 1) * HT]


def cross_attention(nc, m, sem, ps, io):
    PB, SC, TB, OB, YB = ps[0:2], ps[2:4], ps[4:6], ps[6], ps[7]
    x, hsT, ctxT, cap, ident, w = m["x"], m["hsT_hl"], m["ctxT_hl"], m["cap"], m["ident"], m["wqkv_hl"]
    with ExitStack() as stack:
        def sb(name, shape, dt=F32):
            return stack.enter_context(nc.sbuf_tensor(name, shape, dt))

        wo = sb("cross_wo_hl", [P, 2, QUAD, DM], F32R)
        qT = sb("cross_qT", [P, QUAD, TOK])
        kT = sb("cross_kT", [P, TOK])
        v = sb("cross_v_hl", [P, 2, SEQS, D2], F32R)
        rot = sb("rotated", [P, 2, HT])
        cross = sb("rotated_other_half", [P, 2, HT])
        S = sb("cross_scores", [P, 2, QUAD, P])
        negmax = sb("cross_negmax", [P, 2, QUAD])
        rowsum = sb("cross_rowsum", [P, 2, QUAD])
        rinv = sb("cross_rinv", [P, 2, QUAD])
        PT = sb("cross_probsT_hl", [P, 2, QUAD * P], F32R)
        oT = sb("cross_outT_hl", [P, 2, 2, QUAD * P], F32R)
        last_hs = sb("last_hs_rows", [P, EARLY, DM])
        block = stack.enter_context(nc.Block())

        def norm_bank(k):
            return PB[k % 2] if k >= EARLY else (SC[1], YB)[k]

        def rows_of(k):
            return m["norm_rows"][:, k % 2, :] if k >= EARLY else last_hs[:, k, :]

        NORM_STATS = {5: [2], 6: [3, 4], 7: [5], 8: [6]}
        NORM_ROWS = {6: [2], 7: [3, 4], 8: [5], 9: [6]}
        NORM_LOWS = {7: [2], 8: [3, 4], 9: [5], 10: [6]}

        def norms_in(table, b, last, tail):
            return table.get(SEQS + b if tail else b, []) if last else []

        def blocks_in(b):
            pairs = {0: (0, 1), 1: (2, 3), 2: (4, 5)}
            return [(j, 1, 0) for j in pairs.get(b, ())] + [(j, 0, 1) for j in pairs.get(b - 4, ())]

        def turns_in(b, last):
            if last:
                return [(PIECES + h, 0, h) for h in range(QUAD)] if b == 2 else []
            return {1: [(0, 1, 0), (1, 1, 1), (2, 1, 2)],
                    2: [(PIECES + h, 0, WO_TURN + h) for h in range(QUAD - 1)],
                    3: [(PIECES + QUAD - 1, 0, WO_TURN + QUAD - 1)],
                    4: [(3, 1, 7), (4, 1, 8)],
                    5: [(5, 1, 9)]}.get(b, [])

        def outputs_in(b, first, last, tail):
            before, after = {0: ([-3], []), 1: ([-2], []), 2: ([-1], []), 3: ([], []), 4: ([0], []),
                             5: ([1], [2]), 6: ([3], []), 7: ([4], [])}[b]
            late = []
            if last and b == 5:
                after, late = [], after
            if tail or (last and b >= 6):
                before, late = [], before
            return [[y for y in ys if not (first and y < 0)] for ys in (before, after, late)]

        @block.sync
        def _(sp):
            def body(g, last):
                for b in range(SEQS):
                    for which, ahead, t in turns_in(b, last):
                        if which < PIECES:
                            source = piece_source(io, which, g + 1)
                        else:
                            source = io["wo2"][bass.ds((g * QUAD + which - PIECES) * P, P), :]
                        load_piece(sp, m, sem, PIECES + TURNS * g + t, (PIECES + t) % SLOTS, source)

            with sp.Fori(0, GROUPS - 1) as g:
                body(g, False)
            body(GROUPS - 1, True)
            sp.wait_ge(sem["piece_split"], PIECES + TURNS * (GROUPS - 1) + QUAD)
            load_ff_rows(sp, m, sem, io, 0)

        @block.gpsimd
        def _(pool):
            def rope_sum(g, half, j, first=False):
                pool.wait_ge(sem["rope_read"], 10 * g + 5 * half + j + 1)
                if not first:
                    pool.wait_ge(sem["scores2"], SEQS * g if half else SEQS * g - HALF)
                dst = kT[:] if j == 0 else qT[:, j - 1, :]
                nc.gpsimd.tensor_tensor(half_of(dst, half), rot[:, (half + j) % 2, :], cross[:, (half + j) % 2, :], ALU.add).then_inc(sem["roped"], 1)

            for k in range(EARLY):
                norm_rstd(nc, pool, m, sem, k)
            for j in range(PIECES - 1):
                rope_sum(0, 0, j, first=True)

            def body(g, first, last):
                for b in range(SEQS):
                    n = SEQS * g + b
                    for j, half, ahead in blocks_in(b):
                        if j < PIECES - 1 and not (ahead and last):
                            rope_sum(g + ahead, half, j, first=first and not ahead)
                    pool.wait_ge(sem["rinv2"], n + 1)
                    nc.gpsimd.tensor_tensor(S[:, b % 2], S[:, b % 2], rinv[:, b % 2, :].unsqueeze(2).to_broadcast([P, QUAD, P]), ALU.mult).then_inc(sem["probs2"], 1)
                    for which, ahead, t in turns_in(b, last):
                        dst = w[:, which] if which < PIECES else wo[:, :, which - PIECES]
                        piece_low(nc, pool, m, sem, (PIECES + t) % SLOTS, PIECES + TURNS * g + t, dst)
                    for k in norms_in(NORM_STATS, b, last, False):
                        norm_rstd(nc, pool, m, sem, k)

            body(0, True, False)
            with pool.Fori(1, GROUPS - 1) as g:
                body(g, False, False)
            body(GROUPS - 1, False, True)
            for k in NORM_STATS[SEQS]:
                norm_rstd(nc, pool, m, sem, k)

        @block.vector
        def _(dve):
            def rope(g, half, j, first=False):
                rr = 10 * g + 5 * half + j
                pb = PB[j % 2]
                dve.wait_ge(sem["projected"], 12 * g + 6 * half + j + 1)
                if not first and j == 0:
                    dve.wait_ge(sem["v_transposed"], 2 * g + half)
                if not first or j >= 2:
                    dve.wait_ge(sem["roped"], rr - 1)
                nc.vector.tensor_tensor(rot[:, (half + j) % 2, :], pb[:], half_of(m["cosT"][:], half), ALU.mult)
                nc.vector.tensor_tensor(cross[0:64, (half + j) % 2, :], pb[64:128, :], half_of(m["sinT"][0:64, :], half), ALU.mult)
                nc.vector.tensor_tensor(cross[64:128, (half + j) % 2, :], pb[0:64, :], half_of(m["sinT"][64:128, :], half), ALU.mult).then_inc(sem["rope_read"], 1)

            def v_low(g, half):
                dve.wait_ge(sem["v_high"], 2 * g + half + 1)
                nc.vector.tensor_tensor(v[:, 1, half * HALF:(half + 1) * HALF, :], PB[1][:].rearrange("p (b d) -> p b d", b=HALF),
                                        v[:, 0, half * HALF:(half + 1) * HALF, :].bitcast(F32), ALU.subtract).then_inc(sem["v_low"], 1)

            def add_output(g, y, first):
                dve.wait_ge(sem["out2"], SEQS * g + y + 1)
                if not (first and y == 0):
                    dve.wait_ge(sem["x2"], SEQS * g + y)
                nc.vector.tensor_tensor(x[:, y % SEQS, :], x[:, y % SEQS, :], YB[:], ALU.add).then_inc(sem["x2"], 1)

            for k in range(EARLY):
                norm_stats(nc, dve, m, sem, k)
            for k in range(EARLY):
                norm_rows(nc, dve, m, sem, k, rows_of(k))
            for j in range(PIECES - 1):
                rope(0, 0, j, first=True)
                if j < EARLY:
                    norm_low(nc, dve, m, sem, j, norm_bank(j))
            v_low(0, 0)

            def body(g, first, last, tail=False):
                for b in range(3 if tail else SEQS):
                    n = SEQS * g + b
                    blocks = [x for x in blocks_in(b) if not (x[2] and last)] if not tail else []
                    if not tail:
                        dve.wait_ge(sem["scores2"], n + 1)
                        if not first or b >= 2:
                            dve.wait_ge(sem["probs_transposed2"], n - 1)
                        nc.vector.scalar_tensor_tensor(out=S[:, b % 2], in0=SC[b % 2][:].rearrange("p (h k) -> p h k", h=QUAD), scalar=SCALE2,
                                                       in1=cap[:, b, :].unsqueeze(1).to_broadcast([P, QUAD, P]), op0=ALU.mult, op1=ALU.min).then_inc(sem["masked2"], 1)
                        dve.wait_ge(sem["masked2"], n + 1)
                        nc.vector.tensor_reduce(negmax[:, b % 2, :], S[:, b % 2], AX.X, ALU.max, negate=True).then_inc(sem["max2"], 1)
                    for j, half, ahead in blocks[:1]:
                        rope(g + ahead, half, j)
                    before, after, late = outputs_in(b, first, last, tail)
                    for y in before:
                        add_output(g, y, first)
                    for j, half, ahead in blocks[1:]:
                        if j < PIECES - 1:
                            rope(g + ahead, half, j)
                    for y in after:
                        add_output(g, y, first)
                    for k in norms_in(NORM_LOWS, b, last, tail):
                        norm_low(nc, dve, m, sem, k, norm_bank(k))
                    for k in norms_in(NORM_STATS, b, last, tail):
                        norm_stats(nc, dve, m, sem, k)
                    for k in norms_in(NORM_ROWS, b, last, tail):
                        norm_rows(nc, dve, m, sem, k, rows_of(k))
                    if not tail:
                        dve.wait_ge(sem["exp2"], n + 1)
                        nc.vector.reciprocal(rinv[:, b % 2, :], rowsum[:, b % 2, :]).then_inc(sem["rinv2"], 1)
                    if (not first or b >= 2) and (not tail or b < 2):
                        dve.wait_ge(sem["outT_high"], n - 1)
                        nc.vector.tensor_tensor(oT[:, b % 2, 1], OB[:], oT[:, b % 2, 0].bitcast(F32), ALU.subtract).then_inc(sem["outT_low"], 1)
                    if (not first or b >= 1) and (not tail or b < 1):
                        dve.wait_ge(sem["probsT_high"], n)
                        nc.vector.tensor_tensor(PT[:, 1], TB[(b - 1) % 2][:], PT[:, 0].bitcast(F32), ALU.subtract).then_inc(sem["probsT_low"], 1)
                    for j, half, ahead in blocks[1:]:
                        if j == PIECES - 1:
                            v_low(g + ahead, half)
                    for y in late:
                        add_output(g, y, first)

            body(0, True, False)
            with dve.Fori(1, GROUPS - 1) as g:
                body(g, False, False)
            body(GROUPS - 1, False, True)
            body(GROUPS, False, True, tail=True)

        @block.scalar
        def _(act):
            def v_copy(g, half):
                act.wait_ge(sem["projected"], 12 * g + 6 * half + 6)
                act.wait_ge(sem["roped"], 10 * g + 5 * half + 4)
                nc.scalar.copy(rot[:, (half + 1) % 2, :], PB[1][:]).then_inc(sem["vT"], 1)

            def v_high(g, half, first=False):
                act.wait_ge(sem["v_transposed"], 2 * g + half + 1)
                if not first:
                    act.wait_ge(sem["pv2"], SEQS * g if half else SEQS * g - HALF)
                nc.scalar.copy(v[:, 0, half * HALF:(half + 1) * HALF, :], PB[1][:].rearrange("p (b d) -> p b d", b=HALF)).then_inc(sem["v_high"], 1)

            for k in range(EARLY):
                norm_high(nc, act, m, sem, k, norm_bank(k))
            v_copy(0, 0)
            v_high(0, 0, first=True)

            def body(g, first, last, tail=False):
                for b in range(3 if tail else SEQS):
                    n = SEQS * g + b
                    if not tail:
                        act.wait_ge(sem["max2"], n + 1)
                        for h in range(QUAD):
                            e = nc.scalar.activation(S[:, b % 2, h, :], S[:, b % 2, h, :], ACT.Exp, bias=negmax[:, b % 2, h:h + 1],
                                                     accum_out=rowsum[:, b % 2, h:h + 1])
                        e.then_inc(sem["exp2"], 1)
                        for j, half, ahead in blocks_in(b):
                            if j == PIECES - 1 and not (ahead and last):
                                v_copy(g + ahead, half)
                    if (not first or b >= 2) and (not tail or b < 2):
                        act.wait_ge(sem["pv2"], n - 1)
                        if not first or b >= 4:
                            act.wait_ge(sem["out2"], n - 3)
                        nc.scalar.copy(oT[:, b % 2, 0], OB[:]).then_inc(sem["outT_high"], 1)
                    if (not first or b >= 1) and (not tail or b < 1):
                        act.wait_ge(sem["probs_transposed2"], n)
                        if not first or b >= 2:
                            act.wait_ge(sem["pv2"], n - 1)
                        nc.scalar.copy(PT[:, 0], TB[(b - 1) % 2][:]).then_inc(sem["probsT_high"], 1)
                    if not tail:
                        for j, half, ahead in blocks_in(b):
                            if j == PIECES - 1 and not (ahead and last):
                                v_high(g + ahead, half, first=first and not ahead)
                    for which, ahead, t in turns_in(b, last) if not tail else ():
                        if which < PIECES:
                            act.wait_ge(sem["projected"], 12 * g + 6 + which + 1)
                            dst = w[:, which]
                        else:
                            if not first:
                                act.wait_ge(sem["out2"], SEQS * g)
                            dst = wo[:, :, which - PIECES]
                        piece_high(nc, act, m, sem, (PIECES + t) % SLOTS, TURNS // SLOTS * g + (PIECES + t) // SLOTS + 1, dst)
                    for k in norms_in(NORM_ROWS, b, last, tail):
                        norm_high(nc, act, m, sem, k, norm_bank(k))

            body(0, True, False)
            with act.Fori(1, GROUPS - 1) as g:
                body(g, False, False)
            body(GROUPS - 1, False, True)
            body(GROUPS, False, True, tail=True)

        @block.tensor
        def _(pe):
            def project(g, half, j, first=False):
                rr = 10 * g + 5 * half + j
                if j == 0 and not first:
                    pe.wait_ge(sem["rope_read"], rr)
                elif j == 1 and not first:
                    pe.wait_ge(sem["v_low"], 2 * g + half)
                elif j >= 2:
                    pe.wait_ge(sem["rope_read"], rr - 1)
                if half == 0:
                    turn = j if isinstance(g, int) and g == 0 else PIECES + TURNS * (g - 1) + PIECE_TURN[j]
                    pe.wait_ge(sem["piece_split"], turn + 1)
                src = hsT if 0 < j < PIECES - 1 else ctxT
                for t in range(KT):
                    i = products(nc, PB[j % 2][:], w[:, j, :, t], half_of(src[:, :, t], half), t == 0, t == KT - 1)
                i.then_inc(sem["projected"], 1)

            def transpose_v(g, half):
                pe.wait_ge(sem["vT"], 2 * g + half + 1)
                for b in range(HALF):
                    i = nc.tensor.transpose(PB[1][:, b * P:(b + 1) * P], rot[:, (half + 1) % 2, b * P:(b + 1) * P], ident[:])
                i.then_inc(sem["v_transposed"], 1)

            def output(g, y, first, last):
                pe.wait_ge(sem["outT_low"], SEQS * g + y + 1)
                if first and y == 0:
                    pe.wait_ge(sem["norm_low"], EARLY)
                else:
                    pe.wait_ge(sem["x2"], SEQS * g + y)
                for h in range(QUAD):
                    if y == 0:
                        pe.wait_ge(sem["piece_split"], PIECES + TURNS * g + (0 if last else WO_TURN) + h + 1)
                    i = products(nc, YB[:], oT[:, y % 2, :, h * P:(h + 1) * P], wo[:, :, h], h == 0, h == QUAD - 1)
                i.then_inc(sem["out2"], 1)

            for j in range(PIECES):
                project(0, 0, j, first=True)
                if j < EARLY:
                    norm_transposes(nc, pe, m, sem, j, rows_of(j), norm_bank(j))
            transpose_v(0, 0)

            def body(g, first, last, tail=False):
                for b in range(3 if tail else SEQS):
                    n = SEQS * g + b
                    blocks = [x for x in blocks_in(b) if not (x[2] and last)] if not tail else []
                    if not tail:
                        if b % HALF == 0:
                            pe.wait_ge(sem["roped"], 10 * g + (10 if b else 5))
                        if not first or b >= 2:
                            pe.wait_ge(sem["masked2"], n - 1)
                        for h in range(QUAD):
                            i = nc.tensor.matmul(SC[b % 2][:, h * P:(h + 1) * P], qT[:, h, b * P:(b + 1) * P], kT[:, b * P:(b + 1) * P],
                                                 start=True, stop=True)
                        i.then_inc(sem["scores2"], 1)
                    for j, half, ahead in blocks[:1]:
                        project(g + ahead, half, j)
                    before, after, late = outputs_in(b, first, last, tail)
                    for y in before:
                        output(g, y, first, last)
                    if first and b == 0:
                        pe.wait_ge(sem["norm_low"], EARLY)
                    for j, half, ahead in blocks[1:]:
                        project(g + ahead, half, j)
                    for y in after:
                        output(g, y, first, last)
                    if (not first or b >= 2) and (not tail or b < 2):
                        if b == 2:
                            pe.wait_ge(sem["v_low"], 2 * g + 1)
                        if b == 6:
                            pe.wait_ge(sem["v_low"], 2 * g + 2)
                        pe.wait_ge(sem["probsT_low"], n - 1)
                        if not first or b >= 3:
                            pe.wait_ge(sem["outT_low"], n - 2)
                        products(nc, OB[:], v[:, :, (b - 2) % SEQS, :], PT[:], True, True).then_inc(sem["pv2"], 1)
                    if (not first or b >= 1) and (not tail or b < 1):
                        pe.wait_ge(sem["probs2"], n)
                        if not first or b >= 3:
                            pe.wait_ge(sem["probsT_low"], n - 2)
                        for h in range(QUAD):
                            i = nc.tensor.transpose(TB[(b - 1) % 2][:, h * P:(h + 1) * P], S[:, (b - 1) % 2, h, :], ident[:])
                        i.then_inc(sem["probs_transposed2"], 1)
                    for j, half, ahead in blocks[1:]:
                        if j == PIECES - 1:
                            transpose_v(g + ahead, half)
                    for y in late:
                        output(g, y, first, last)
                    for k in norms_in(NORM_ROWS, b, last, tail):
                        if k >= EARLY + 2:
                            pe.wait_ge(sem["norm_low"], k - 1)
                        else:
                            pe.wait_ge(sem["rope_read"], 10 * GROUPS)
                            pe.wait_ge(sem["v_low"], 2 * GROUPS)
                        norm_transposes(nc, pe, m, sem, k, rows_of(k), norm_bank(k))

            body(0, True, False)
            with pe.Fori(1, GROUPS - 1) as g:
                body(g, False, False)
            body(GROUPS - 1, False, True)
            body(GROUPS, False, True, tail=True)


def feed_forward(nc, m, sem, ps, io):
    GATE, UP, TW, TD, YB = ps[0:2], ps[2:4], ps[4:6], ps[6], [ps[7], ps[6]]
    x, hsT, ident, raw, rawd = m["x"], m["hsT_hl"], m["ident"], m["gate_up_rows"], m["down_rows"]
    LATE = {7: GATE[1], 8: UP[1], 9: YB[0]}
    with ExitStack() as stack:
        def sb(name, shape, dt=F32):
            return stack.enter_context(nc.sbuf_tensor(name, shape, dt))

        hT = sb("ff_hT_hl", [P, 2, FT, TOK], F32R)
        wdT = sb("ff_downT_hl", [P, 2, FT, DM], F32R)
        wT = sb("ff_gate_upT_hl", [P, 2, 2, KT, P], F32R)
        tmp = sb("ff_work", [P, 4, DM])
        block = stack.enter_context(nc.Block())

        def products_by(i, k, half):
            if isinstance(i, int) and i == 0:
                return 2 * half + k + 1
            return 4 * i + 2 * k + half + 1

        def rows_of(k):
            return m["norm_rows"][:, k % 2, :]

        @block.sync
        def _(sp):
            with sp.Fori(1, FT - 1) as i:
                load_ff_rows(sp, m, sem, io, i)
            load_ff_rows(sp, m, sem, io, FT - 1)
            for b in range(SEQS):
                sp.wait_ge(sem["x3"], b + 1)
                sp.dma_start(io["out"][b], x[:, b, :]).then_inc(sem["out_stored"], 16)
            sp.wait_ge(sem["out_stored"], 16 * SEQS)

        @block.gpsimd
        def _(pool):
            for k in LATE:
                norm_rstd(nc, pool, m, sem, k)

            def h_low(i):
                n = width_of(i)
                for half in range(2):
                    pool.wait_ge(sem["h_high"], 2 * i + half + 1)
                    nc.gpsimd.tensor_tensor(half_of(hT[0:n, 1, bass.ds(i, 1), :], half), tmp[0:n, 2 + half:3 + half, :],
                                            half_of(hT[0:n, 0, bass.ds(i, 1), :], half).bitcast(F32), ALU.subtract).then_inc(sem["h_low"], 1)

            h_low(0)
            with pool.Fori(1, FT - 1) as i:
                h_low(i)
            h_low(FT - 1)

        @block.vector
        def _(dve):
            def w_low(i, k):
                n = width_of(i)
                dve.wait_ge(sem["w_high"], 2 * i + k + 1)
                nc.vector.tensor_tensor(wT[:, k, 1, :, 0:n], TW[k][:].rearrange("p (t f) -> p t f", t=KT)[:, :, 0:n],
                                        wT[:, k, 0, :, 0:n].bitcast(F32), ALU.subtract).then_inc(sem["w_low"], 1)

            def body(i, first=False):
                n = width_of(i)
                w_low(i, 1)
                dve.wait_ge(sem["wd_high"], i + 1)
                nc.vector.tensor_tensor(wdT[0:n, 1, bass.ds(i, 1), :], TD[0:n, :].unsqueeze(1), wdT[0:n, 0, bass.ds(i, 1), :].bitcast(F32),
                                        ALU.subtract).then_inc(sem["wd_low"], 1)
                if first:
                    norm_rows(nc, dve, m, sem, 9, rows_of(9))
                    for k in LATE:
                        norm_low(nc, dve, m, sem, k, LATE[k])
                if not (isinstance(i, int) and i == FT - 1):
                    w_low(i + 1, 0)
                for half in range(2):
                    dve.wait_ge(sem["silu"], 2 * i + half + 1)
                    dve.wait_ge(sem["ff_product"], products_by(i, 1, half))
                    if not first:
                        dve.wait_ge(sem["h_low"], 2 * i + half - 1)
                    nc.vector.tensor_tensor(tmp[0:n, 2 + half, :], tmp[0:n, half, :], UP[half][0:n, :], ALU.mult).then_inc(sem["h_product"], 1)

            norm_stats(nc, dve, m, sem, 7)
            w_low(0, 0)
            norm_stats(nc, dve, m, sem, 8)
            norm_rows(nc, dve, m, sem, 7, rows_of(7))
            norm_stats(nc, dve, m, sem, 9)
            norm_rows(nc, dve, m, sem, 8, rows_of(8))
            body(0, first=True)
            with dve.Fori(1, FT - 2) as i:
                body(i)
            body(FT - 2)
            body(FT - 1)
            for b in range(SEQS):
                dve.wait_ge(sem["y3"], b + 1)
                nc.vector.tensor_tensor(x[:, b, :], x[:, b, :], YB[b % 2][:], ALU.add).then_inc(sem["x3"], 1)

        @block.scalar
        def _(act):
            def w_high(i, k, first=False):
                n = width_of(i)
                act.wait_ge(sem["w_transposed"], 2 * i + k + 1)
                if not first:
                    act.wait_ge(sem["ff_product"], products_by(i - 1, k, 1))
                nc.scalar.copy(wT[:, k, 0, :, 0:n], TW[k][:].rearrange("p (t f) -> p t f", t=KT)[:, :, 0:n]).then_inc(sem["w_high"], 1)

            def body(i, first=False):
                n = width_of(i)
                w_high(i, 1, first)
                act.wait_ge(sem["wd_transposed"], i + 1)
                nc.scalar.copy(wdT[0:n, 0, bass.ds(i, 1), :], TD[0:n, :].unsqueeze(1)).then_inc(sem["wd_high"], 1)
                for k in LATE if first else ():
                    norm_high(nc, act, m, sem, k, LATE[k])
                for half in range(2):
                    act.wait_ge(sem["ff_product"], products_by(i, 0, half))
                    if not first:
                        act.wait_ge(sem["h_product"], 2 * i + half - 1)
                    nc.scalar.activation(tmp[0:n, half, :], GATE[half][0:n, :], ACT.Silu).then_inc(sem["silu"], 1)
                if not (isinstance(i, int) and i == FT - 1):
                    w_high(i + 1, 0)
                for half in range(2):
                    act.wait_ge(sem["h_product"], 2 * i + half + 1)
                    nc.scalar.copy(half_of(hT[0:n, 0, bass.ds(i, 1), :], half), tmp[0:n, 2 + half:3 + half, :]).then_inc(sem["h_high"], 1)

            w_high(0, 0, first=True)
            body(0, first=True)
            with act.Fori(1, FT - 2) as i:
                body(i)
            body(FT - 2)
            body(FT - 1)

        @block.tensor
        def _(pe):
            def w_transposes(i, k, first=False):
                n = width_of(i)
                pe.wait_ge(sem["wg_loaded" if k == 0 else "wu_loaded"], 16 * i + 16)
                if not first:
                    pe.wait_ge(sem["w_low"], 2 * i + k - 1)
                for t in range(KT):
                    e = nc.tensor.transpose(TW[k][:, t * P:t * P + n], raw[0:n, k, t * P:(t + 1) * P], ident[0:n, 0:n])
                e.then_inc(sem["w_transposed"], 1)

            def product(i, k, first=False, halves=(0, 1)):
                n = width_of(i)
                pe.wait_ge(sem["w_low"], 2 * i + k + 1)
                for half in halves:
                    if not first:
                        pe.wait_ge(sem["h_product" if k else "silu"], 2 * i + half - 1)
                    out = (UP if k else GATE)[half][0:n, :]
                    for t in range(KT):
                        e = products(nc, out, wT[:, k, :, t, 0:n], half_of(hsT[:, :, t], half), t == 0, t == KT - 1)
                    e.then_inc(sem["ff_product"], 1)

            def body(i, first=False):
                n = width_of(i)
                w_transposes(i, 1, first)
                pe.wait_ge(sem["wd_loaded"], 16 * i + 16)
                if not first:
                    pe.wait_ge(sem["wd_low"], i)
                for t in range(KT):
                    e = nc.tensor.transpose(TD[0:n, t * P:(t + 1) * P], rawd[:, t, 0:n], ident[:])
                e.then_inc(sem["wd_transposed"], 1)
                if first:
                    product(i, 0, first, halves=(0,))
                    for norm in LATE:
                        norm_transposes(nc, pe, m, sem, norm, rows_of(norm), LATE[norm])
                    product(i, 1, first, halves=(0,))
                    pe.wait_ge(sem["norm_low"], EARLY + SEQS)
                    product(i, 0, first, halves=(1,))
                    w_transposes(i + 1, 0)
                    product(i, 1, first, halves=(1,))
                    return
                product(i, 0)
                if not (isinstance(i, int) and i == FT - 1):
                    w_transposes(i + 1, 0)
                product(i, 1)

            w_transposes(0, 0, first=True)
            body(0, first=True)
            with pe.Fori(1, FT - 2) as i:
                body(i)
            body(FT - 2)
            body(FT - 1)
            pe.wait_ge(sem["wd_low"], FT - 1)
            pe.wait_ge(sem["h_low"], 2 * (FT - 1))
            for b in range(SEQS):
                if b >= 2:
                    pe.wait_ge(sem["x3"], b - 1)
                for i in range(FT):
                    if b == 0 and i == FT - 1:
                        pe.wait_ge(sem["wd_low"], FT)
                        pe.wait_ge(sem["h_low"], 2 * FT)
                    n = width_of(i)
                    e = products(nc, YB[b % 2][:], block_of(hT[0:n, :, i], b), wdT[0:n, :, i], i == 0, i == FT - 1)
                e.then_inc(sem["y3"], 1)


SEMAPHORES = """x_first rel_loaded head_of_row_loaded wkv1_loaded wq1_loaded x_rest pos_loaded wo1_loaded mask_loaded
ctx_loaded ctx_transposed ident_zero ident_ready exponent_ready ones_ready mv0 mv1 var_eps0 var_eps1 rstd0 rstd1
kv_high kv_copied scores1 kexp bias tables_loaded stats0 stats1 xn_transposed xn_centred hs_centred xn wk8 mask_is_set exp1 biased1 max1 ctx_high
ctx_low pv1 rsum1 attn_transposed attn out1 x1 hs_transposed hs hs_high hs_low kv1 xnT q1 q_transposed q_high q_copied qT
probs_transposed1 probsT1 attnT tables_transposed out_stored
piece_split piece_high rope_read roped rinv2 probs2 projected out2
scores2 masked2 max2 exp2 v_high v_low vT v_transposed x2 outT_high outT_low probsT_high probsT_low probs_transposed2 pv2
norm_stats norm_mv norm_var_eps norm_rstd norm_rows norm_transposed norm_high norm_low wg_loaded wu_loaded wd_loaded
w_transposed w_high w_low wd_transposed wd_high wd_low ff_product silu h_product h_high h_low y3 x3""".split() + [f"piece_loaded{slot}" for slot in range(SLOTS)]


def program(nc, io):
    with ExitStack() as stack:
        def sb(name, shape, dt=F32):
            return stack.enter_context(nc.sbuf_tensor(name, shape, dt))

        sem = {name: stack.enter_context(nc.semaphore(name)) for name in SEMAPHORES}
        ps = [stack.enter_context(nc.psum_tensor(f"bank{i}", [P, 512], F32)) for i in range(8)]
        stage = sb("staged_rows", [P, SLOTS, DM])
        m = {
            "stage": stage,
            "gate_up_rows": stage[:, 0:2, :],
            "down_rows": stage[:, 2, :].rearrange("p (t f) -> p t f", t=KT),
            "norm_rows": stage[:, 3:5, :],
            "exponent": sb("minus_half_and_eps", [P, 2]),
            "norm_stats": sb("norm_stats", [P, 6]),
            "norm_mv": sb("norm_mean_var", [P, EARLY + SEQS, 2]),
            "norm_rstd": sb("norm_rstd", [P, EARLY + SEQS, 2]),
            "x": sb("x", [P, SEQS, DM]),
            "ident": sb("ident", [P, P]),
            "hsT_hl": sb("hsT_hl", [P, 2, KT, TOK], F32R),
        }
        with ExitStack() as attention:
            def asb(name, shape, dt=F32):
                return attention.enter_context(nc.sbuf_tensor(name, shape, dt))

            m["ctxT_hl"] = asb("ctxT_hl", [P, 2, KT, TOK], F32R)
            m["cosT"] = asb("cosT", [P, TOK])
            m["sinT"] = asb("sinT", [P, TOK])
            m["cap"] = asb("cap", [P, SEQS, P])
            m["wqkv_hl"] = asb("cross_wqkv_hl", [P, PIECES, 2, KT, P], F32R)
            self_attention(nc, m, sem, ps, io)
            cross_attention(nc, m, sem, ps, io)
        feed_forward(nc, m, sem, ps, io)


def constant_tables():
    import numpy as np

    i = np.arange(P)
    rel = (i[None, :] - i[:, None]).astype(np.float32)
    rel[i[None, :] > i[:, None]] = -1.0e30
    own = (i[:, None] % (QUAD * HD1) // HD1 == np.arange(QUAD)[None, :]).astype(np.float32) * np.float32(SCALE1)
    inv = (1.0 / np.float32(10000.0) ** (np.arange(0, D2, 2, dtype=np.float32) / np.float32(D2))).astype(np.float32)
    angle = np.arange(MAX_POS, dtype=np.float32)[:, None] * inv[None, :]
    cos, sin = np.cos(angle), np.sin(angle)
    rope = np.concatenate([cos, cos, -sin, sin], axis=1).astype(np.float32)
    return np.ascontiguousarray(np.concatenate([rel, own], axis=1)), rope


_INPUTS = {
    "x": "x", "ctx": "ctx_4096", "pos": "pos_BxS2", "mask": "mask_BxSxS2_ik0",
    "wq1": "L0_attn_Wq", "wkv1": "L0_attn_Wkv", "wo1": "L0_attn_Wo",
    "wq2": "L0_xattn_Wq", "wk2": "L0_xattn_Wk", "wv2": "L0_xattn_Wv", "wo2": "L0_xattn_Wo",
    "wg": "L0_ffn_W_gate", "wu": "L0_ffn_W_up", "wd": "L0_ffn_W_down",
}


def kernel(**inputs):
    import numpy as _np
    import concourse.bacc as _bacc
    from concourse import mybir as _mybir
    from concourse.bass_utils import run_bass_kernel_spmd as _run

    nc = _bacc.Bacc("TRN2", target_bir_lowering=False, num_devices=1)
    arrays, io = {}, {}
    constants, rope = constant_tables()
    given = {name: _np.ascontiguousarray(inputs[source]) for name, source in _INPUTS.items()}
    given["pos"] = _np.ascontiguousarray(given["pos"].T)
    for name, a in {**given, "constants": constants, "rope": rope}.items():
        arrays[f"in_{name}"] = a
        io[name] = nc.dram_tensor(f"in_{name}", a.shape, _mybir.dt.from_np(a.dtype), kind="ExternalInput").ap()
    io["out"] = nc.dram_tensor("out", (SEQS, P, DM), _mybir.dt.float32, kind="ExternalOutput").ap()
    program(nc, io)
    r = _run(nc, [arrays], core_ids=[0])
    return r.results[0]["out"]
```
